# Optimizing a Trainium2 kernel written in Bass

```python
import numpy as np
import jax
import jax.numpy as jnp

def _softmax(x, axis=-1):
    return jax.nn.softmax(x, axis=axis)

def _gelu(x):
    return jax.nn.gelu(x, approximate=True)

def _silu(x):
    return jax.nn.silu(x)

def _sigmoid(x):
    return jax.nn.sigmoid(x)

def _layernorm(x, axis=-1, eps=1e-05):
    m = jnp.mean(x, axis=axis, keepdims=True)
    v = jnp.var(x, axis=axis, keepdims=True)
    return (x - m) / jnp.sqrt(v + eps)

def _scatter_add(tgt, idx, src, axis=0):
    return tgt.at[idx].add(src)

def _segment_sum(src, seg, n):
    return jax.ops.segment_sum(src, seg, n)
kernel_name = 'mk_prb_d2_jaxref_r8_63a516'

def setup_inputs(seed: int=0):
    np.random.seed(seed)
    _w = jnp.asarray

    def _L0_attn_setup():
        import jax, jax.numpy as jnp
        import numpy as np
        D_MODEL = 128
        NUM_HEADS = 16
        D_HEAD = D_MODEL // NUM_HEADS
        PATCH = 128

        def _patched_attn(x, Wq, bq, Wk, bk, Wv, bv, Wo, bo):
            B, T, D = x.shape
            P = PATCH
            pad_len = (P - T % P) % P
            if pad_len > 0:
                x = jnp.pad(x, ((0, 0), (0, pad_len), (0, 0)))
            Tp = T + pad_len
            n = Tp // P
            xp = x.reshape(B * n, P, D)

            def heads(y):
                return y.reshape(B * n, P, NUM_HEADS, D_HEAD).transpose(0, 2, 1, 3)
            q = heads(xp @ Wq + bq)
            k = heads(xp @ Wk + bk)
            v = heads(xp @ Wv + bv)
            scores = jnp.einsum('bhtd,bhTd->bhtT', q, k) / jnp.sqrt(jnp.asarray(D_HEAD, x.dtype))
            w = jax.nn.softmax(scores, axis=-1)
            out = jnp.einsum('bhtT,bhTd->bhtd', w, v)
            out = out.transpose(0, 2, 1, 3).reshape(B * n, P, D)
            out = out @ Wo + bo
            out = out.reshape(B, Tp, D)
            if pad_len > 0:
                out = out[:, :T, :]
            return out
        key = jax.random.key(seed)
        ks = jax.random.split(key, 10)
        B, T = (4, 1024)
        x = jax.random.normal(ks[0], (B, T, D_MODEL), dtype=jnp.float32)
        coords = jax.random.uniform(ks[1], (B, T, 2), dtype=jnp.float32)
        s = 1.0 / np.sqrt(D_MODEL)
        Wq = jax.random.normal(ks[2], (D_MODEL, D_MODEL), dtype=jnp.float32) * s
        Wk = jax.random.normal(ks[3], (D_MODEL, D_MODEL), dtype=jnp.float32) * s
        Wv = jax.random.normal(ks[4], (D_MODEL, D_MODEL), dtype=jnp.float32) * s
        Wo = jax.random.normal(ks[5], (D_MODEL, D_MODEL), dtype=jnp.float32) * s
        bq = jnp.zeros((D_MODEL,), jnp.float32)
        bk = jnp.zeros((D_MODEL,), jnp.float32)
        bv = jnp.zeros((D_MODEL,), jnp.float32)
        bo = jnp.zeros((D_MODEL,), jnp.float32)
        return {'x': x, 'coords': coords, 'Wq': Wq, 'bq': bq, 'Wk': Wk, 'bk': bk, 'Wv': Wv, 'bv': bv, 'Wo': Wo, 'bo': bo}
    _L0_attn_in = _L0_attn_setup()

    def _L0_ffn_setup():
        import jax, jax.numpy as jnp
        import numpy as np
        from jax import lax
        H = 128
        E = 8
        E_MLP = E - 4
        TOP_K = 2
        I = 64
        KC = 4
        SHARED_SCALE = 1.0
        key = jax.random.key(seed)
        ks = jax.random.split(key, 8)
        B, S = (4, 512)
        s_h = 1.0 / np.sqrt(H)
        s_i = 1.0 / np.sqrt(I)
        return {'hidden_states': jax.random.normal(ks[0], (B, S, H), dtype=jnp.float32), 'Wr': jax.random.normal(ks[1], (H, E), dtype=jnp.float32) * s_h, 'router_bias': jnp.zeros((E,), dtype=jnp.float32), 'Wg': jax.random.normal(ks[2], (E_MLP, H, I), dtype=jnp.float32) * s_h, 'Wu': jax.random.normal(ks[3], (E_MLP, H, I), dtype=jnp.float32) * s_h, 'Wd': jax.random.normal(ks[4], (E_MLP, I, H), dtype=jnp.float32) * s_i, 'conv_w': jax.random.normal(ks[5], (KC, 1, H), dtype=jnp.float32) * (1.0 / np.sqrt(KC)), 'conv_b': jnp.zeros((H,), dtype=jnp.float32)}
    _L0_ffn_in = _L0_ffn_setup()

    def _L1_attn_setup():
        import jax, jax.numpy as jnp
        from jax import lax
        import numpy as np
        D_MODEL = 128
        D_STATE = 16
        D_INNER = 2 * D_MODEL
        B, L = (4, 256)

        def _layernorm(y, w, b, eps=1e-05):
            mu = y.mean(-1, keepdims=True)
            var = ((y - mu) ** 2).mean(-1, keepdims=True)
            return (y - mu) / jnp.sqrt(var + eps) * w + b
        key = jax.random.key(seed)
        ks = jax.random.split(key, 8)
        s = 0.02
        x = jax.random.normal(ks[0], (B, L, D_MODEL), dtype=jnp.float32)
        W_in = jax.random.normal(ks[1], (2 * D_INNER, D_MODEL), dtype=jnp.float32) * s
        conv_w = jax.random.normal(ks[2], (D_INNER, 1, 4), dtype=jnp.float32) * 0.25
        conv_b = jax.random.normal(ks[3], (D_INNER,), dtype=jnp.float32) * 0.01
        W_x = jax.random.normal(ks[4], (2 * D_STATE + 1, D_INNER), dtype=jnp.float32) * s
        W_dt = jax.random.normal(ks[5], (D_INNER, 1), dtype=jnp.float32) * s
        b_dt = jax.random.normal(ks[6], (D_INNER,), dtype=jnp.float32) * 0.01
        A_log = jnp.log(jnp.arange(1, D_STATE + 1, dtype=jnp.float32) * 0.1)
        D_param = jnp.ones((D_INNER,), dtype=jnp.float32)
        W_out = jax.random.normal(ks[7], (D_MODEL, D_INNER), dtype=jnp.float32) * s
        ln_w = jnp.ones((D_INNER,), dtype=jnp.float32)
        ln_b = jnp.zeros((D_INNER,), dtype=jnp.float32)
        return {'x': x, 'W_in': W_in, 'conv_w': conv_w, 'conv_b': conv_b, 'W_x': W_x, 'W_dt': W_dt, 'b_dt': b_dt, 'A_log': A_log, 'D_param': D_param, 'W_out': W_out, 'ln_w': ln_w, 'ln_b': ln_b}
    _L1_attn_in = _L1_attn_setup()

    def _L1_ffn_setup():
        import jax, jax.numpy as jnp
        import numpy as np
        DIM = 128
        DEPTH = 6
        HEADS = 16
        DIM_HEAD = 64
        WINDOW = 32
        INNER = HEADS * DIM_HEAD
        DIM_INNER = int(DIM * 4 * 2 / 3)
        QK_SCALE = 8.0

        def shift_tokens(t):
            a, s = jnp.split(t, 2, -1)
            s = jnp.pad(s, ((0, 0), (1, 0), (0, 0)))[:, :-1]
            return jnp.concatenate([a, s], -1)

        def l2norm(t):
            return t / jnp.maximum(jnp.linalg.norm(t, axis=-1, keepdims=True), 1e-12)

        def rotate_half(x):
            x1, x2 = jnp.split(x, 2, -1)
            return jnp.concatenate([-x2, x1], -1)

        def rotary_tables(n):
            half = jnp.arange(0, DIM_HEAD, 2, dtype=jnp.float32)
            inv_freq = 1.0 / 10000.0 ** (half / DIM_HEAD)
            t = jnp.arange(n, dtype=jnp.float32)
            freqs = t[:, None] * inv_freq[None, :]
            freqs = jnp.concatenate([freqs, freqs], -1)
            base_scale = (half + 0.4 * DIM_HEAD) / (1.4 * DIM_HEAD)
            power = (t - n // 2) / (WINDOW // 2)
            scale = base_scale[None, :] ** power[:, None]
            scale = jnp.concatenate([scale, scale], -1)
            return (freqs, scale)

        def local_attention(q, k, v):
            b, h, n, d = q.shape
            w = WINDOW
            nw = n // w
            bq = q.reshape(b, h, nw, w, d)
            bk = k.reshape(b, h, nw, w, d)
            bv = v.reshape(b, h, nw, w, d)

            def look(t):
                p = jnp.pad(t, ((0, 0), (0, 0), (1, 0), (0, 0), (0, 0)))
                return jnp.concatenate([p[:, :, :nw], p[:, :, 1:]], axis=3)
            bk2, bv2 = (look(bk), look(bv))
            seq = jnp.arange(n).reshape(nw, w)
            seq_p = jnp.pad(seq, ((1, 0), (0, 0)), constant_values=-1)
            jt = jnp.concatenate([seq_p[:nw], seq_p[1:]], axis=1)
            it = seq[:, :, None]
            jb = jt[:, None, :]
            mask = (it < jb) | (it > jb + w) | (jb == -1)
            sim = jnp.einsum('bhwie,bhwje->bhwij', bq, bk2) * QK_SCALE
            sim = jnp.where(mask, -jnp.finfo(sim.dtype).max, sim)
            attn = jax.nn.softmax(sim, -1)
            out = jnp.einsum('bhwij,bhwje->bhwie', attn, bv2)
            return out.reshape(b, h, n, d)

        def attn_layer(x, Wqkv, qs, ksc, Wo):
            b, n, _ = x.shape
            qkv = x @ Wqkv
            q, k, v = jnp.split(qkv, 3, -1)
            sh = lambda t: t.reshape(b, n, HEADS, DIM_HEAD).transpose(0, 2, 1, 3)
            q, k, v = (sh(q), sh(k), sh(v))
            q = l2norm(q) * qs
            k = l2norm(k) * ksc
            freqs, scale = rotary_tables(n)
            cos, sin = (jnp.cos(freqs), jnp.sin(freqs))
            q = q * cos * scale + rotate_half(q) * sin * scale
            inv = 1.0 / scale
            k = k * cos * inv + rotate_half(k) * sin * inv
            out = local_attention(q, k, v)
            out = out.transpose(0, 2, 1, 3).reshape(b, n, INNER)
            return out @ Wo

        def ffn_layer(x, g, bln, W1, b1, W2, b2):
            mu = x.mean(-1, keepdims=True)
            var = ((x - mu) ** 2).mean(-1, keepdims=True)
            xn = (x - mu) / jnp.sqrt(var + 1e-05) * g + bln
            hg = xn @ W1 + b1
            a, gate = jnp.split(hg, 2, -1)
            return a * jax.nn.gelu(gate, approximate=False) @ W2 + b2
        key = jax.random.key(seed)
        ks = jax.random.split(key, 8)
        B, N = (2, 256)
        init = lambda k, shape: jax.random.normal(k, shape, jnp.float32) * 0.02
        return {'x': jax.random.normal(ks[0], (B, N, DIM), jnp.float32), 'Wqkv': init(ks[1], (DEPTH, DIM, 3 * INNER)), 'q_scale': jnp.ones((DEPTH, DIM_HEAD), jnp.float32), 'k_scale': jnp.ones((DEPTH, DIM_HEAD), jnp.float32), 'Wo': init(ks[2], (DEPTH, INNER, DIM)), 'ln_g': jnp.ones((DEPTH, DIM), jnp.float32), 'ln_b': jnp.zeros((DEPTH, DIM), jnp.float32), 'W1': init(ks[3], (DEPTH, DIM, 2 * DIM_INNER)), 'b1': jnp.zeros((DEPTH, 2 * DIM_INNER), jnp.float32), 'W2': init(ks[4], (DEPTH, DIM_INNER, DIM)), 'b2': jnp.zeros((DEPTH, DIM), jnp.float32)}
    _L1_ffn_in = _L1_ffn_setup()
    _d = {'L0_attn_x': _L0_attn_in['x'], 'L0_attn_coords': _L0_attn_in['coords'], 'L0_attn_Wq': _L0_attn_in['Wq'], 'L0_attn_bq': _L0_attn_in['bq'], 'L0_attn_Wk': _L0_attn_in['Wk'], 'L0_attn_bk': _L0_attn_in['bk'], 'L0_attn_Wv': _L0_attn_in['Wv'], 'L0_attn_bv': _L0_attn_in['bv'], 'L0_attn_Wo': _L0_attn_in['Wo'], 'L0_attn_bo': _L0_attn_in['bo'], 'L0_ffn_Wr': _L0_ffn_in['Wr'], 'L0_ffn_router_bias': _L0_ffn_in['router_bias'], 'L0_ffn_Wg': _L0_ffn_in['Wg'], 'L0_ffn_Wu': _L0_ffn_in['Wu'], 'L0_ffn_Wd': _L0_ffn_in['Wd'], 'L0_ffn_conv_w': _L0_ffn_in['conv_w'], 'L0_ffn_conv_b': _L0_ffn_in['conv_b'], 'L1_attn_W_in': _L1_attn_in['W_in'], 'L1_attn_conv_w': _L1_attn_in['conv_w'], 'L1_attn_conv_b': _L1_attn_in['conv_b'], 'L1_attn_W_x': _L1_attn_in['W_x'], 'L1_attn_W_dt': _L1_attn_in['W_dt'], 'L1_attn_b_dt': _L1_attn_in['b_dt'], 'L1_attn_A_log': _L1_attn_in['A_log'], 'L1_attn_D_param': _L1_attn_in['D_param'], 'L1_attn_W_out': _L1_attn_in['W_out'], 'L1_attn_ln_w': _L1_attn_in['ln_w'], 'L1_attn_ln_b': _L1_attn_in['ln_b'], 'L1_ffn_Wqkv': _L1_ffn_in['Wqkv'], 'L1_ffn_q_scale': _L1_ffn_in['q_scale'], 'L1_ffn_k_scale': _L1_ffn_in['k_scale'], 'L1_ffn_Wo': _L1_ffn_in['Wo'], 'L1_ffn_ln_g': _L1_ffn_in['ln_g'], 'L1_ffn_ln_b': _L1_ffn_in['ln_b'], 'L1_ffn_W1': _L1_ffn_in['W1'], 'L1_ffn_b1': _L1_ffn_in['b1'], 'L1_ffn_W2': _L1_ffn_in['W2'], 'L1_ffn_b2': _L1_ffn_in['b2']}
    _x0 = _d['L0_attn_x']
    _d['L0_attn_x'] = jax.random.normal(jax.random.fold_in(jax.random.key(seed), 1), (8, 512, 128), dtype=_x0.dtype)
    del _x0
    return _d

def reference(L0_attn_x, L0_attn_coords, L0_attn_Wq, L0_attn_bq, L0_attn_Wk, L0_attn_bk, L0_attn_Wv, L0_attn_bv, L0_attn_Wo, L0_attn_bo, L0_ffn_Wr, L0_ffn_router_bias, L0_ffn_Wg, L0_ffn_Wu, L0_ffn_Wd, L0_ffn_conv_w, L0_ffn_conv_b, L1_attn_W_in, L1_attn_conv_w, L1_attn_conv_b, L1_attn_W_x, L1_attn_W_dt, L1_attn_b_dt, L1_attn_A_log, L1_attn_D_param, L1_attn_W_out, L1_attn_ln_w, L1_attn_ln_b, L1_ffn_Wqkv, L1_ffn_q_scale, L1_ffn_k_scale, L1_ffn_Wo, L1_ffn_ln_g, L1_ffn_ln_b, L1_ffn_W1, L1_ffn_b1, L1_ffn_W2, L1_ffn_b2):

    def _L0_attn_ref(x, coords, Wq, bq, Wk, bk, Wv, bv, Wo, bo):
        import jax, jax.numpy as jnp
        import numpy as np
        D_MODEL = 128
        NUM_HEADS = 16
        D_HEAD = D_MODEL // NUM_HEADS
        PATCH = 128

        def _patched_attn(x, Wq, bq, Wk, bk, Wv, bv, Wo, bo):
            B, T, D = x.shape
            P = PATCH
            pad_len = (P - T % P) % P
            if pad_len > 0:
                x = jnp.pad(x, ((0, 0), (0, pad_len), (0, 0)))
            Tp = T + pad_len
            n = Tp // P
            xp = x.reshape(B * n, P, D)

            def heads(y):
                return y.reshape(B * n, P, NUM_HEADS, D_HEAD).transpose(0, 2, 1, 3)
            q = heads(xp @ Wq + bq)
            k = heads(xp @ Wk + bk)
            v = heads(xp @ Wv + bv)
            scores = jnp.einsum('bhtd,bhTd->bhtT', q, k) / jnp.sqrt(jnp.asarray(D_HEAD, x.dtype))
            w = jax.nn.softmax(scores, axis=-1)
            out = jnp.einsum('bhtT,bhTd->bhtd', w, v)
            out = out.transpose(0, 2, 1, 3).reshape(B * n, P, D)
            out = out @ Wo + bo
            out = out.reshape(B, Tp, D)
            if pad_len > 0:
                out = out[:, :T, :]
            return out
        return _patched_attn(x, Wq, bq, Wk, bk, Wv, bv, Wo, bo)

    def _L0_ffn_ref(hidden_states, Wr, router_bias, Wg, Wu, Wd, conv_w, conv_b):
        import jax, jax.numpy as jnp
        import numpy as np
        from jax import lax
        H = 128
        E = 8
        E_MLP = E - 4
        TOP_K = 2
        I = 64
        KC = 4
        SHARED_SCALE = 1.0
        B, S, Hd = hidden_states.shape
        T = B * S
        x = hidden_states.reshape(T, Hd)
        scores = jax.nn.sigmoid(x @ Wr)
        _, idx = lax.top_k(scores + router_bias, TOP_K)
        w = jnp.take_along_axis(scores, idx, axis=-1)
        w = w / (jnp.sum(w, axis=-1, keepdims=True) + 1e-09)
        cw = jnp.zeros((T, E), dtype=x.dtype).at[jnp.arange(T)[:, None], idx].add(w)
        g = jnp.einsum('th,ehi->tei', x, Wg)
        u = jnp.einsum('th,ehi->tei', x, Wu)
        hid = jax.nn.silu(g) * u
        mlp_out = jnp.einsum('tei,eih->teh', hid, Wd)
        routed = jnp.einsum('te,teh->th', cw[:, :E_MLP], mlp_out)
        routed = routed + cw[:, E_MLP:E_MLP + 1] * x
        routed = routed + cw[:, E_MLP + 2:E_MLP + 3] * x
        routed = routed + cw[:, E_MLP + 3:E_MLP + 4] * jax.nn.relu(x)
        routed = routed.reshape(B, S, Hd)
        shared = lax.conv_general_dilated(hidden_states, conv_w, window_strides=(1,), padding=[(KC - 1, 0)], dimension_numbers=('NHC', 'HIO', 'NHC'), feature_group_count=Hd) + conv_b
        return routed + SHARED_SCALE * shared

    def _L1_attn_ref(x, W_in, conv_w, conv_b, W_x, W_dt, b_dt, A_log, D_param, W_out, ln_w, ln_b):
        import jax, jax.numpy as jnp
        from jax import lax
        import numpy as np
        D_MODEL = 128
        D_STATE = 16
        D_INNER = 2 * D_MODEL
        B, L = (4, 256)

        def _layernorm(y, w, b, eps=1e-05):
            mu = y.mean(-1, keepdims=True)
            var = ((y - mu) ** 2).mean(-1, keepdims=True)
            return (y - mu) / jnp.sqrt(var + eps) * w + b
        Bb, Ll, _ = x.shape
        d_inner = D_param.shape[0]
        d_state = A_log.shape[0]
        xz = x @ W_in.T
        xi, z = jnp.split(xz, 2, axis=-1)
        xc = jnp.transpose(xi, (0, 2, 1))
        xc = lax.conv_general_dilated(xc, conv_w, (1,), [(3, 0)], dimension_numbers=('NCH', 'OIH', 'NCH'), feature_group_count=d_inner)
        xc = xc + conv_b[None, :, None]
        xi = jax.nn.silu(jnp.transpose(xc, (0, 2, 1)))
        xd = xi @ W_x.T
        dt_in = xd[..., :1]
        Bp = xd[..., 1:1 + d_state]
        Cp = xd[..., 1 + d_state:]
        dt = jnp.clip(jax.nn.softplus(dt_in @ W_dt.T + b_dt), 0.0001, 10.0)
        A = -jnp.exp(jnp.minimum(A_log, 5.0))

        def step(h, ins):
            dt_t, B_t, C_t, x_t = ins
            dA = jnp.exp(jnp.clip(dt_t[:, :, None] * A, -20.0, 0.0))
            dBu = jnp.clip(dt_t[:, :, None] * B_t[:, None, :] * x_t[:, :, None], -10.0, 10.0)
            h = jnp.clip(h * dA + dBu, -100.0, 100.0)
            y_t = jnp.einsum('bds,bs->bd', h, C_t)
            return (h, y_t)
        h0 = jnp.zeros((Bb, d_inner, d_state), x.dtype)
        ins = (jnp.transpose(dt, (1, 0, 2)), jnp.transpose(Bp, (1, 0, 2)), jnp.transpose(Cp, (1, 0, 2)), jnp.transpose(xi, (1, 0, 2)))
        _, ys = lax.scan(step, h0, ins)
        y = jnp.transpose(ys, (1, 0, 2))
        out = (_layernorm(y, ln_w, ln_b) + D_param * xi) * jax.nn.silu(z)
        return out @ W_out.T

    def _L1_ffn_ref(x, Wqkv, q_scale, k_scale, Wo, ln_g, ln_b, W1, b1, W2, b2):
        import jax, jax.numpy as jnp
        import numpy as np
        DIM = 128
        DEPTH = 6
        HEADS = 16
        DIM_HEAD = 64
        WINDOW = 32
        INNER = HEADS * DIM_HEAD
        DIM_INNER = int(DIM * 4 * 2 / 3)
        QK_SCALE = 8.0

        def shift_tokens(t):
            a, s = jnp.split(t, 2, -1)
            s = jnp.pad(s, ((0, 0), (1, 0), (0, 0)))[:, :-1]
            return jnp.concatenate([a, s], -1)

        def l2norm(t):
            return t / jnp.maximum(jnp.linalg.norm(t, axis=-1, keepdims=True), 1e-12)

        def rotate_half(x):
            x1, x2 = jnp.split(x, 2, -1)
            return jnp.concatenate([-x2, x1], -1)

        def rotary_tables(n):
            half = jnp.arange(0, DIM_HEAD, 2, dtype=jnp.float32)
            inv_freq = 1.0 / 10000.0 ** (half / DIM_HEAD)
            t = jnp.arange(n, dtype=jnp.float32)
            freqs = t[:, None] * inv_freq[None, :]
            freqs = jnp.concatenate([freqs, freqs], -1)
            base_scale = (half + 0.4 * DIM_HEAD) / (1.4 * DIM_HEAD)
            power = (t - n // 2) / (WINDOW // 2)
            scale = base_scale[None, :] ** power[:, None]
            scale = jnp.concatenate([scale, scale], -1)
            return (freqs, scale)

        def local_attention(q, k, v):
            b, h, n, d = q.shape
            w = WINDOW
            nw = n // w
            bq = q.reshape(b, h, nw, w, d)
            bk = k.reshape(b, h, nw, w, d)
            bv = v.reshape(b, h, nw, w, d)

            def look(t):
                p = jnp.pad(t, ((0, 0), (0, 0), (1, 0), (0, 0), (0, 0)))
                return jnp.concatenate([p[:, :, :nw], p[:, :, 1:]], axis=3)
            bk2, bv2 = (look(bk), look(bv))
            seq = jnp.arange(n).reshape(nw, w)
            seq_p = jnp.pad(seq, ((1, 0), (0, 0)), constant_values=-1)
            jt = jnp.concatenate([seq_p[:nw], seq_p[1:]], axis=1)
            it = seq[:, :, None]
            jb = jt[:, None, :]
            mask = (it < jb) | (it > jb + w) | (jb == -1)
            sim = jnp.einsum('bhwie,bhwje->bhwij', bq, bk2) * QK_SCALE
            sim = jnp.where(mask, -jnp.finfo(sim.dtype).max, sim)
            attn = jax.nn.softmax(sim, -1)
            out = jnp.einsum('bhwij,bhwje->bhwie', attn, bv2)
            return out.reshape(b, h, n, d)

        def attn_layer(x, Wqkv, qs, ksc, Wo):
            b, n, _ = x.shape
            qkv = x @ Wqkv
            q, k, v = jnp.split(qkv, 3, -1)
            sh = lambda t: t.reshape(b, n, HEADS, DIM_HEAD).transpose(0, 2, 1, 3)
            q, k, v = (sh(q), sh(k), sh(v))
            q = l2norm(q) * qs
            k = l2norm(k) * ksc
            freqs, scale = rotary_tables(n)
            cos, sin = (jnp.cos(freqs), jnp.sin(freqs))
            q = q * cos * scale + rotate_half(q) * sin * scale
            inv = 1.0 / scale
            k = k * cos * inv + rotate_half(k) * sin * inv
            out = local_attention(q, k, v)
            out = out.transpose(0, 2, 1, 3).reshape(b, n, INNER)
            return out @ Wo

        def ffn_layer(x, g, bln, W1, b1, W2, b2):
            mu = x.mean(-1, keepdims=True)
            var = ((x - mu) ** 2).mean(-1, keepdims=True)
            xn = (x - mu) / jnp.sqrt(var + 1e-05) * g + bln
            hg = xn @ W1 + b1
            a, gate = jnp.split(hg, 2, -1)
            return a * jax.nn.gelu(gate, approximate=False) @ W2 + b2
        for i in range(DEPTH):
            x = attn_layer(shift_tokens(x), Wqkv[i], q_scale[i], k_scale[i], Wo[i]) + x
            x = ffn_layer(shift_tokens(x), ln_g[i], ln_b[i], W1[i], b1[i], W2[i], b2[i]) + x
        return x
    x = L0_attn_x
    xn = _layernorm(x, axis=-1)
    x = x + _L0_attn_ref(xn, L0_attn_coords, L0_attn_Wq, L0_attn_bq, L0_attn_Wk, L0_attn_bk, L0_attn_Wv, L0_attn_bv, L0_attn_Wo, L0_attn_bo) + _L0_ffn_ref(xn, L0_ffn_Wr, L0_ffn_router_bias, L0_ffn_Wg, L0_ffn_Wu, L0_ffn_Wd, L0_ffn_conv_w, L0_ffn_conv_b)
    xn = _layernorm(x, axis=-1)
    x = x + _L1_attn_ref(xn, L1_attn_W_in, L1_attn_conv_w, L1_attn_conv_b, L1_attn_W_x, L1_attn_W_dt, L1_attn_b_dt, L1_attn_A_log, L1_attn_D_param, L1_attn_W_out, L1_attn_ln_w, L1_attn_ln_b) + _L1_ffn_ref(xn, L1_ffn_Wqkv, L1_ffn_q_scale, L1_ffn_k_scale, L1_ffn_Wo, L1_ffn_ln_g, L1_ffn_ln_b, L1_ffn_W1, L1_ffn_b1, L1_ffn_W2, L1_ffn_b2)
    return x

_drawn_inputs = setup_inputs


def setup_inputs(seed=0):
    import zlib

    import numpy as np

    out = dict(_drawn_inputs(seed))
    spreads = {'L0_attn_bq': (0.0, 0.8),
     'L0_attn_bk': (0.0, 2.0),
     'L0_attn_bv': (0.0, 0.1),
     'L0_attn_bo': (0.0, 0.1),
     'L0_ffn_router_bias': (0.0, 0.1),
     'L0_ffn_conv_b': (0.0, 0.1),
     'L1_attn_D_param': (1.0, 0.6),
     'L1_attn_ln_w': (1.0, 0.6),
     'L1_attn_ln_b': (0.0, 0.8),
     'L1_ffn_q_scale': (1.0, 0.6),
     'L1_ffn_k_scale': (1.0, 0.6),
     'L1_ffn_ln_g': (1.0, 0.6),
     'L1_ffn_ln_b': (0.0, 0.8),
     'L1_ffn_b1': (0.0, 0.8),
     'L1_ffn_b2': (0.0, 0.375)}
    factors = {'L1_attn_W_in': 8.0,
     'L1_attn_conv_w': 8.0,
     'L1_attn_conv_b': 34.018,
     'L1_attn_W_x': 8.0,
     'L1_attn_W_dt': 8.0,
     'L1_attn_b_dt': 48.091,
     'L1_attn_A_log': 8.0,
     'L1_attn_W_out': 8.0,
     'L1_ffn_W1': 4.963,
     'L1_ffn_W2': 4.861}
    for name, (base, spread) in spreads.items():
        noise = np.random.default_rng([zlib.crc32(name.encode()), seed]).standard_normal(out[name].shape)
        drawn = base * np.exp(spread * noise) if base else spread * noise
        out[name] = jnp.asarray(drawn.astype(out[name].dtype))
    for name, factor in factors.items():
        out[name] = (out[name] * factor).astype(out[name].dtype)
    return out
```

```python
import numpy as np
from contextlib import ExitStack

import concourse.bass as bass
from concourse import mybir

F32 = mybir.dt.float32
ALU = mybir.AluOpType
ACT = mybir.ActivationFunctionType
AX = mybir.AxisListType.X

P = 128
C = 128
B, L = 8, 512
T4 = L // P


def start_at_one(eng, sems):
    for s in sems:
        eng.sem_inc(s, 1)


DEPTH = 6
HEADS, DH = 16, 64
INNER = HEADS * DH
HALF = DH // 2
HG = P // HALF
GROUPS = HEADS // HG
WINDOW = 32
DI = int(C * 4 * 2 / 3)
HM = [P, P, DI - 2 * P]
QK_SCALE = 8.0
BIG = 1e30
QS1, QS2, KS1, KS2, LNG, LNB, B2C, B1A, B1G = 0, 1, 2, 3, 4, 5, 6, 7, 10
NSMALL = 13
NW = 7


def rotary_constants():
    half = np.arange(0, DH, 2, dtype=np.float32)
    inv = (np.float32(1.0) / np.float32(10000.0) ** (half / np.float32(DH))).astype(np.float32)
    t = np.arange(L, dtype=np.float32)
    fr = t[:, None] * inv[None, :]
    base = (half + np.float32(0.4 * DH)) / np.float32(1.4 * DH)
    power = (t - L // 2) / np.float32(WINDOW // 2)
    sc = base[None, :].astype(np.float32) ** power[:, None].astype(np.float32)
    c, s = np.cos(fr), np.sin(fr)
    tabs = np.stack([c * sc, s * sc, c / sc, s / sc]).transpose(2, 0, 1).astype(np.float32)
    return np.ascontiguousarray(np.tile(tabs, (HG, 1, 1)))


def band_masks():
    i, j = np.arange(P)[:, None], np.arange(P)[None, :]
    own = (j <= i) & (j >= i - WINDOW)
    before = (i < WINDOW) & (j >= P - WINDOW) & (j - (P - WINDOW) >= i)
    m = np.stack([own, own | before], 1)
    return np.where(m, 0.0, -BIG).astype(np.float32)


def head_blocks():
    return np.repeat(np.eye(HG, dtype=np.float32), HALF, 0)


def spreads():
    m = np.zeros((2 * HEADS, 2 * GROUPS, P), np.float32)
    for g in range(2 * GROUPS):
        for h in range(HG):
            m[g * HG + h, g, h * HALF:(h + 1) * HALF] = 1.0
    return m


RSQRT_STEPS = 11


def rsqrt(nc, eng, sem, base, x, y, t):
    ts, stt = nc.vector.tensor_scalar, nc.vector.scalar_tensor_tensor
    xi, yi, ti = x.bitcast(mybir.dt.int32), y.bitcast(mybir.dt.int32), t.bitcast(mybir.dt.int32)
    ts(ti, xi, 1, None, ALU.logical_shift_right).then_inc(sem, 1)
    eng.wait_ge(sem, 1 + base + 1)
    ts(yi, ti, -1.0, float(0x5F3759DF), ALU.mult, ALU.add).then_inc(sem, 1)
    for k in range(3):
        eng.wait_ge(sem, 1 + base + 2 + 3 * k)
        nc.vector.tensor_tensor(t, y, y, ALU.mult).then_inc(sem, 1)
        eng.wait_ge(sem, 1 + base + 3 + 3 * k)
        stt(t, x, -0.5, t, ALU.mult, ALU.mult).then_inc(sem, 1)
        eng.wait_ge(sem, 1 + base + 4 + 3 * k)
        stt(y, t, 1.5, y, ALU.add, ALU.mult).then_inc(sem, 1)
    eng.wait_ge(sem, 1 + base + RSQRT_STEPS)


def build_local(nc, xin, xout, tabs, masks, blocks, spread, wqk, wv, wo, w1, w2, small, ident_d,
                depth=DEPTH, nb=B):
    with ExitStack() as ctx:
        def sb(name, shape):
            return ctx.enter_context(nc.sbuf_tensor(name, shape, F32))

        def ps(name, shape=(P, 512)):
            return ctx.enter_context(nc.psum_tensor(name, list(shape), F32))

        sems = []

        def sem(name):
            sems.append(ctx.enter_context(nc.semaphore(name)))
            return sems[-1]

        xT = sb("xT", [P, nb * L])
        xs = sb("xs", [P, L])
        xf = sb("xf", [P, L])
        Wqk = sb("Wqk", [P, 2 * INNER])
        Wv = sb("Wv", [P, INNER])
        Wo = sb("Wo", [P, INNER // P, C])
        W1 = sb("W1", [P, 2 * DI])
        W2 = sb("W2", [P, 3, C])
        sm = sb("smalls", [P, NSMALL])
        tb = sb("tb", [P, 4, L])
        tl = sb("tl", [P, 8, L])
        mk = sb("mk", [P, 2, P])
        blk = sb("blk", [P, HG])
        pad, padA = sb("pad", [P, 1]), sb("padA", [P, 1])
        spr = sb("spr", [2 * HEADS, 2 * GROUPS, P])
        idn = sb("idn", [P, P])
        onesC = sb("onesC", [P, P])
        sq = sb("sq", [P, 2, 2, L])
        sqs = sb("sqs", [P, 2, L])
        mm = sb("mm", [P, 2, 4, L])
        qk = sb("qk", [P, 2 * GROUPS, 2, L])
        ssm = sb("ssm", [P, T4, 2 * HEADS])
        rs = sb("rs", [P, T4, 2 * HEADS])
        rt = sb("rt", [P, T4, 2 * HEADS])
        rT = sb("rT", [2 * HEADS, L])
        V = sb("V", [P, T4, INNER])
        Vd = sb("Vd", [P, T4 - 1, INNER])
        sp = sb("sp", [P, 8, HG, P])
        mx = sb("mx", [P, 8, HG])
        nm = sb("nm", [P, 8, HG])
        su = sb("su", [P, 8, HG])
        rc = sb("rc", [P, 8, HG])
        PT = sb("PT", [P, 2, HG, P])
        OT = sb("OT", [P, INNER // P, L])
        xc = sb("xc", [P, L])
        xq = sb("xq", [P, L])
        xn = sb("xn", [P, L])
        va = sb("va", [P, T4])
        rstd = sb("rstd", [P, T4])
        vt = sb("vt", [P, T4])
        ge, hd = mm[:, 0], mm[:, 1]

        bS = [ps("bS0"), ps("bS1")]
        bT = [ps("bT0"), ps("bT1")]
        bO = [ps("bO0"), ps("bO1")]
        bW, bX = ps("bW"), ps("bX")
        proj = [bS, bT]
        bank4 = bS + [bW, bX]

        s_const, s_wts, s_out = sem("s_const"), sem("s_wts"), sem("s_out")
        s_ini = sem("s_ini")
        s_tab = sem("s_tab")
        s_xs = sem("s_xs")
        s_qk = sem("s_qk")
        s_sq = sem("s_sq")
        s_sqa = sem("s_sqa")
        s_rot = sem("s_rot")
        s_rope = sem("s_rope")
        s_ss = sem("s_ss")
        s_ssm = sem("s_ssm")
        s_rs = sem("s_rs")
        s_rtp = sem("s_rtp")
        s_rT = sem("s_rT")
        s_rb = sem("s_rb")
        s_nrm = sem("s_nrm")
        s_vp = sem("s_vp")
        s_v = sem("s_v")
        s_vd = sem("s_vd")
        s_s = sem("s_s")
        s_mx = sem("s_mx")
        s_nm = sem("s_nm")
        s_exp = sem("s_exp")
        s_rc = sem("s_rc")
        s_pn = sem("s_pn")
        s_pt = sem("s_pt")
        s_pte = sem("s_pte")
        s_pv = sem("s_pv")
        s_ot = sem("s_ot")
        s_wo = sem("s_wo")
        s_x1 = sem("s_x1")
        s_xf = sem("s_xf")
        s_mean, s_xc, s_xq, s_var, s_va = sem("s_mean"), sem("s_xc"), sem("s_xq"), sem("s_var"), sem("s_va")
        s_rstd, s_rbb, s_xh, s_xn = sem("s_rstd"), sem("s_rbb"), sem("s_xh"), sem("s_xn")
        s_w1 = sem("s_w1")
        s_ge = sem("s_ge")
        s_hd = sem("s_hd")
        s_w2 = sem("s_w2")
        s_res = sem("s_res")

        CONSTS = 16 * 6
        NQ, NT = 2 * GROUPS, T4 * GROUPS
        block = ctx.enter_context(nc.Block())

        @block.sync
        def _(sp_):
            start_at_one(sp_, sems)
            sp_.dma_start(xT[:], xin).then_inc(s_const, 16)
            sp_.dma_start(tb[:], tabs).then_inc(s_const, 16)
            sp_.dma_start(mk[:], masks).then_inc(s_const, 16)
            sp_.dma_start(blk[:], blocks).then_inc(s_const, 16)
            sp_.dma_start(spr[:], spread).then_inc(s_const, 16)
            sp_.dma_start(idn[:], ident_d).then_inc(s_const, 16)
            with sp_.Fori(0, depth) as l:
                sp_.wait_ge(s_w2, 1 + l * nb)
                sp_.wait_ge(s_res, 1 + l * nb)
                sp_.dma_start(Wqk[:], wqk[bass.ds(l, 1)].rearrange("a p n -> p (a n)")).then_inc(s_wts, 16)
                sp_.dma_start(Wv[:], wv[bass.ds(l, 1)].rearrange("a p n -> p (a n)")).then_inc(s_wts, 16)
                sp_.dma_start(sm[:], small[bass.ds(l, 1)].rearrange("a p n -> p (a n)")).then_inc(s_wts, 16)
                sp_.dma_start(Wo[:], wo[bass.ds(l, 1)].rearrange("a (k p) n -> p (a k) n", p=P)).then_inc(s_wts, 16)
                sp_.dma_start(W1[:], w1[bass.ds(l, 1)].rearrange("a p n -> p (a n)")).then_inc(s_wts, 16)
                sp_.dma_start(W2[:, 0:2, :], w2[bass.ds(l, 1), 0:2 * P].rearrange("a (k p) n -> p (a k) n", p=P)).then_inc(s_wts, 16)
                sp_.dma_start(W2[0:HM[2], 2, :], w2[bass.ds(l, 1), 2 * P:DI].rearrange("a p n -> p (a n)")).then_inc(s_wts, 16)
            sp_.wait_ge(s_res, 1 + depth * nb)
            sp_.dma_start(xout, xT[:]).then_inc(s_out, 16)
            sp_.wait_ge(s_out, 1 + 16)

        @block.gpsimd
        def _(pool):
            nc.gpsimd.memset(xs[:], 0.0).then_inc(s_ini, 1)
            nc.gpsimd.memset(xf[:], 0.0).then_inc(s_ini, 1)
            nc.gpsimd.memset(onesC[:], 1.0 / C).then_inc(s_ini, 1)
            pool.wait_ge(s_ini, 1 + 3)
            pool.wait_ge(s_const, 1 + CONSTS)
            with pool.Fori(0, depth) as l:
                with pool.Fori(0, nb) as b:
                    it = l * nb + b
                    for g in range(NQ):
                        sl = g % 2
                        pool.wait_ge(s_sq, 1 + it * NQ + g + 1)
                        pool.wait_ge(s_ss, 1 + (it * NQ + g - 1 if g >= 2 else it * NQ))
                        nc.gpsimd.tensor_tensor(sqs[:, sl], sq[:, sl, 0], sq[:, sl, 1], ALU.add).then_inc(s_sqa, 1)
                        pool.wait_ge(s_rot, 1 + it * NQ + g + 1)
                        if g == 0:
                            pool.wait_ge(s_s, 1 + it * T4)
                        nc.gpsimd.tensor_tensor(qk[:, g, 0], mm[:, sl, 0], mm[:, sl, 1], ALU.subtract)
                        nc.gpsimd.tensor_tensor(qk[:, g, 1], mm[:, sl, 2], mm[:, sl, 3], ALU.add).then_inc(s_rope, 1)

        @block.tensor
        def _(pe):
            mul = nc.tensor.matmul
            pe.wait_ge(s_const, 1 + CONSTS)
            pe.wait_ge(s_ini, 1 + 3)
            with pe.Fori(0, depth) as l:
                with pe.Fori(0, nb) as b:
                    pe.wait_ge(s_wts, 1 + (l + 1) * 16 * NW)
                    it = l * nb + b

                    def project(g):
                        if g >= 2:
                            pe.wait_ge(s_rot, 1 + it * NQ + g - 1)
                        for half in range(2):
                            w = mul(proj[g % 2][half][:], Wqk[:, (2 * g + half) * P:(2 * g + half + 1) * P], xs[:],
                                    start=True, stop=True)
                        w.then_inc(s_qk, 1)

                    def sums(g):
                        pe.wait_ge(s_sqa, 1 + it * NQ + g + 1)
                        for t in range(T4):
                            c = t * 2 * HEADS + g * HG
                            w = mul(bO[0][:, c:c + HG], sqs[:, g % 2, t * P:(t + 1) * P], blk[:], start=True, stop=True)
                        w.then_inc(s_ss, 1)

                    def values(t, n):
                        bank = bO[n]
                        if t > 0:
                            pe.wait_ge(s_v, 1 + it * 2 * T4 + 2 * t + n - 1)
                        mul(bank[:], xs[:, t * P:(t + 1) * P], Wv[:, n * 512:(n + 1) * 512], start=True, stop=True)\
                            .then_inc(s_vp, 1)

                    def scores(n):
                        t, g = divmod(n, GROUPS)
                        if t and g == 0:
                            pe.wait_ge(s_mx, 1 + it * NT * HG + n * HG)
                        c = g * P
                        for half in range(2):
                            for h in range(HG):
                                r = slice(h * HALF, (h + 1) * HALF)
                                w = mul(bank4[h][:, c:c + P], qk[r, g, half, t * P:(t + 1) * P],
                                        qk[r, GROUPS + g, half, t * P:(t + 1) * P],
                                        start=half == 0, stop=half == 1, tile_position=(h * HALF, 0))
                        if t:
                            for half in range(2):
                                for h in range(HG):
                                    r = slice(h * HALF, (h + 1) * HALF)
                                    w = mul(bank4[h][0:WINDOW, c + P - WINDOW:c + P], qk[r, g, half, t * P:t * P + WINDOW],
                                            qk[r, GROUPS + g, half, t * P - WINDOW:t * P],
                                            start=half == 0, stop=half == 1, tile_position=(h * HALF, 0))
                        if g == GROUPS - 1:
                            w.then_inc(s_s, 1)

                    def turn(n):
                        pe.wait_ge(s_pn, 1 + it * NT + n + 1)
                        if n >= 2:
                            pe.wait_ge(s_pte, 1 + it * NT + n - 1)
                        for h in range(HG):
                            w = nc.tensor.transpose(bT[n % 2][:, h * P:(h + 1) * P], sp[:, n % 8, h], idn[:])
                        w.then_inc(s_pt, 1)

                    def mix(n):
                        t, g = divmod(n, GROUPS)
                        pe.wait_ge(s_pte, 1 + it * NT + n + 1)
                        if t:
                            pe.wait_ge(s_vd, 1 + it * (T4 - 1) + t)
                        if n >= 2:
                            pe.wait_ge(s_ot, 1 + it * NT + n - 1)
                        for h in range(HG):
                            q = slice(64 * (h % 2), 64 * (h % 2) + 64)
                            v = slice((g * HG + h) * DH, (g * HG + h + 1) * DH)
                            c = (h // 2) * P
                            w = mul(bO[n % 2][q, c:c + P], V[:, t, v], PT[:, n % 2, h], start=True, stop=True)
                            if t:
                                w = mul(bO[n % 2][q, c:c + WINDOW], Vd[96:P, t - 1, v], PT[96:P, n % 2, h, 0:WINDOW],
                                        start=False, stop=True, tile_position=(96, 64 * (h % 2)), skip_group_check=True)
                        w.then_inc(s_pv, 1)

                    pe.wait_ge(s_xs, 1 + it + 1)
                    pe.wait_ge(s_hd, 1 + it * 3)
                    for i in range(NQ + 2):
                        if i < NQ:
                            project(i)
                        if i == 2:
                            pe.wait_ge(s_res, 1 + it)
                        if i >= 2:
                            sums(i - 2)
                    pe.wait_ge(s_ssm, 1 + it + 1)
                    for t in range(T4):
                        for n in range(2):
                            values(t, n)
                    pe.wait_ge(s_rs, 1 + (it + 1) * RSQRT_STEPS)
                    for t in range(T4):
                        w = nc.tensor.transpose(bT[0][0:2 * HEADS, t * P:(t + 1) * P], rs[:, t], idn[:])
                    w.then_inc(s_rtp, 1)
                    pe.wait_ge(s_rT, 1 + it + 1)
                    for g in range(NQ):
                        if g >= 2:
                            pe.wait_ge(s_nrm, 1 + it * NQ + g - 1)
                        mul((bW, bX)[g % 2][:], spr[:, g], rT[:], start=True, stop=True).then_inc(s_rb, 1)
                    pe.wait_ge(s_nrm, 1 + it * NQ + NQ)
                    pe.wait_ge(s_v, 1 + it * 2 * T4 + 2 * T4)
                    for t in range(T4 + 1):
                        if t < T4:
                            for g in range(GROUPS):
                                scores(t * GROUPS + g)
                        if t >= 1:
                            for n in range((t - 1) * GROUPS, t * GROUPS):
                                turn(n)
                                if n % GROUPS:
                                    mix(n - 1)
                            mix(t * GROUPS - 1)
                    pe.wait_ge(s_ot, 1 + it * NT + NT)
                    pe.wait_ge(s_mx, 1 + (it + 1) * NT * HG)
                    for k in range(INNER // P):
                        w = mul(bW[:], Wo[:, k], OT[:, k], start=k == 0, stop=k == INNER // P - 1)
                    w.then_inc(s_wo, 1)
                    pe.wait_ge(s_xf, 1 + it + 1)
                    mul(bX[:], onesC[:], xf[:], start=True, stop=True).then_inc(s_mean, 1)
                    pe.wait_ge(s_xq, 1 + it + 1)
                    for t in range(T4):
                        w = mul(bW[:, t:t + 1], xq[:, t * P:(t + 1) * P], onesC[:, 0:1], start=True, stop=True)
                    w.then_inc(s_var, 1)
                    pe.wait_ge(s_rstd, 1 + (it + 1) * RSQRT_STEPS)
                    for t in range(T4):
                        w = mul(bX[:, t * P:(t + 1) * P], rstd[:, t:t + 1].broadcast_to([P, P]), idn[:],
                                start=True, stop=True)
                    w.then_inc(s_rbb, 1)
                    pe.wait_ge(s_xn, 1 + it + 1)
                    for m in range(3):
                        if m == 2:
                            pe.wait_ge(s_hd, 1 + it * 3 + 1)
                        k = HM[m]
                        gate, val = proj[m % 2]
                        mul(gate[0:k, :], W1[:, DI + m * P:DI + m * P + k], xn[:], start=True, stop=True)
                        mul(val[0:k, :], W1[:, m * P:m * P + k], xn[:], start=True, stop=True).then_inc(s_w1, 1)
                    for m in range(3):
                        pe.wait_ge(s_hd, 1 + it * 3 + m + 1)
                        w = mul(bO[0][:], W2[0:HM[m], m], hd[0:HM[m], m], start=m == 0, stop=m == 2)
                    w.then_inc(s_w2, 1)

        @block.scalar
        def _(act):
            f = nc.scalar.activation
            act.wait_ge(s_const, 1 + CONSTS)
            act.wait_ge(s_ini, 1 + 3)
            with act.Fori(0, depth) as l:
                act.wait_ge(s_wts, 1 + (l + 1) * 16 * NW)
                with act.Fori(0, nb) as b:
                    it = l * nb + b
                    act.wait_ge(s_res, 1 + it)
                    act.wait_ge(s_vp, 1 + it * 2 * T4)
                    f(padA[:], blk[:, 0:1], ACT.Copy)
                    f(xs[0:64, :], xT[0:64, bass.ds(b * L, L)], ACT.Copy)
                    f(xs[64:P, 1:L], xT[64:P, bass.ds(b * L, L - 1)], ACT.Copy).then_inc(s_xs, 1)
                    for g in range(NQ):
                        act.wait_ge(s_qk, 1 + it * NQ + g + 1)
                        act.wait_ge(s_sqa, 1 + (it * NQ + g - 1 if g >= 2 else it * NQ))
                        f(sq[:, g % 2, 0], proj[g % 2][0][:], ACT.Square)
                        f(sq[:, g % 2, 1], proj[g % 2][1][:], ACT.Square).then_inc(s_sq, 1)
                    act.wait_ge(s_vd, 1 + it * (T4 - 1))
                    for n in range(2 * T4):
                        act.wait_ge(s_vp, 1 + it * 2 * T4 + n + 1)
                        f(V[:, n // 2, (n % 2) * 512:(n % 2 + 1) * 512], bO[n % 2][:], ACT.Copy).then_inc(s_v, 1)

                    def exps(n):
                        act.wait_ge(s_nm, 1 + it * NT + n + 1)
                        for h in range(HG):
                            f(sp[:, n % 8, h], sp[:, n % 8, h], ACT.Exp, bias=nm[:, n % 8, h:h + 1], scale=QK_SCALE,
                              accum_out=su[:, n % 8, h:h + 1]).then_inc(s_exp, 1)

                    def turned(n):
                        act.wait_ge(s_pt, 1 + it * NT + n + 1)
                        if n >= 2:
                            act.wait_ge(s_pv, 1 + it * NT + n - 1)
                        f(PT[:, n % 2], bT[n % 2][:].rearrange("p (h q) -> p h q", h=HG), ACT.Copy).then_inc(s_pte, 1)

                    def mixed(n):
                        t, g = divmod(n, GROUPS)
                        act.wait_ge(s_pv, 1 + it * NT + n + 1)
                        f(OT[:, 2 * g:2 * g + 2, t * P:(t + 1) * P],
                          bO[n % 2][:, 0:2 * P].rearrange("p (h q) -> p h q", h=2), ACT.Copy).then_inc(s_ot, 1)

                    act.wait_ge(s_wo, 1 + it)
                    for t in range(T4 + 1):
                        for g in range(GROUPS):
                            n = t * GROUPS + g
                            if t >= 1:
                                turned(n - GROUPS)
                                if g:
                                    mixed(n - GROUPS - 1)
                            if t < T4:
                                exps(n)
                        if t >= 1:
                            mixed(t * GROUPS - 1)
                    act.wait_ge(s_x1, 1 + it + 1)
                    f(padA[:], blk[:, 0:1], ACT.Copy)
                    f(xf[0:64, :], xT[0:64, bass.ds(b * L, L)], ACT.Copy)
                    f(xf[64:P, 1:L], xT[64:P, bass.ds(b * L, L - 1)], ACT.Copy).then_inc(s_xf, 1)
                    act.wait_ge(s_xc, 1 + it + 1)
                    f(xq[:], xc[:], ACT.Square).then_inc(s_xq, 1)
                    act.wait_ge(s_w2, 1 + it)
                    for m in range(3):
                        act.wait_ge(s_w1, 1 + it * 3 + m + 1)
                        k = HM[m]
                        f(ge[0:k, m], proj[m % 2][0][0:k, :], ACT.Gelu, bias=sm[0:k, B1G + m:B1G + m + 1]).then_inc(s_ge, 1)

        @block.vector
        def _(dve):
            tt, ts = nc.vector.tensor_tensor, nc.vector.tensor_scalar
            dve.wait_ge(s_const, 1 + CONSTS)
            dve.wait_ge(s_ini, 1 + 3)
            with dve.Fori(0, depth) as l:
                dve.wait_ge(s_wts, 1 + (l + 1) * 16 * NW)
                dve.wait_ge(s_rot, 1 + l * nb * NQ)
                for i, (src, col) in enumerate([(0, QS1), (1, QS2), (0, QS2), (1, QS1),
                                                (2, KS1), (3, KS2), (2, KS2), (3, KS1)]):
                    ts(tl[:, i], tb[:, src], sm[:, col:col + 1], None, ALU.mult).then_inc(s_tab, 1)
                with dve.Fori(0, nb) as b:
                    dve.wait_ge(s_tab, 1 + (l + 1) * 8)
                    it = l * nb + b
                    for g in range(NQ):
                        k = 4 * (g // GROUPS)
                        q1, q2 = proj[g % 2]
                        dve.wait_ge(s_sq, 1 + it * NQ + g + 1)
                        dve.wait_ge(s_rope, 1 + (it * NQ + g - 1 if g >= 2 else it * NQ))
                        tt(mm[:, g % 2, 0], q1[:], tl[:, k], ALU.mult)
                        tt(mm[:, g % 2, 1], q2[:], tl[:, k + 1], ALU.mult)
                        tt(mm[:, g % 2, 2], q2[:], tl[:, k + 2], ALU.mult)
                        tt(mm[:, g % 2, 3], q1[:], tl[:, k + 3], ALU.mult).then_inc(s_rot, 1)
                    dve.wait_ge(s_ss, 1 + it * NQ + NQ)
                    ts(ssm[:].rearrange("p t h -> p (t h)"), bO[0][:, 0:P], 1e-24, None, ALU.max).then_inc(s_ssm, 1)
                    dve.wait_ge(s_ssm, 1 + it + 1)
                    rsqrt(nc, dve, s_rs, it * RSQRT_STEPS, *(a[:].rearrange("p t h -> p (t h)") for a in (ssm, rs, rt)))
                    dve.wait_ge(s_rtp, 1 + it + 1)
                    nc.vector.tensor_copy(rT[:], bT[0][0:2 * HEADS, :]).then_inc(s_rT, 1)
                    dve.wait_ge(s_pv, 1 + it * NT)
                    for t in range(1, T4):
                        dve.wait_ge(s_v, 1 + it * 2 * T4 + 2 * t + 2)
                        tt(Vd[96:P, t - 1], V[96:P, t - 1], V[96:P, t], ALU.subtract).then_inc(s_vd, 1)
                    for g in range(NQ):
                        dve.wait_ge(s_rb, 1 + it * NQ + g + 1)
                        dve.wait_ge(s_rope, 1 + it * NQ + g + 1)
                        rb = (bW, bX)[g % 2]
                        tt(qk[:, g, 0], qk[:, g, 0], rb[:], ALU.mult)
                        tt(qk[:, g, 1], qk[:, g, 1], rb[:], ALU.mult).then_inc(s_nrm, 1)

                    def maxima(n):
                        t, g = divmod(n, GROUPS)
                        if g == 0:
                            dve.wait_ge(s_s, 1 + it * T4 + t + 1)
                            nc.vector.memset(pad[:], 0.0)
                        for h in range(HG):
                            nc.vector.tensor_tensor_reduce(
                                sp[:, n % 8, h], bank4[h][:, g * P:(g + 1) * P], mk[:, 1 if t else 0], 1.0, -3e38,
                                ALU.add, ALU.max, mx[:, n % 8, h:h + 1]).then_inc(s_mx, 1)

                    def negate(n):
                        dve.wait_ge(s_mx, 1 + it * NT * HG + (n + 1) * HG)
                        ts(nm[:, n % 8], mx[:, n % 8], -QK_SCALE, None, ALU.mult).then_inc(s_nm, 1)

                    def normalise(n):
                        dve.wait_ge(s_exp, 1 + it * NT * HG + (n + 1) * HG)
                        nc.vector.reciprocal(rc[:, n % 8], su[:, n % 8]).then_inc(s_rc, 1)
                        dve.wait_ge(s_rc, 1 + it * NT + n + 1)
                        tt(sp[:, n % 8], sp[:, n % 8], rc[:, n % 8].unsqueeze(2).broadcast_to([P, HG, P]), ALU.mult)\
                            .then_inc(s_pn, 1)

                    for t in range(T4):
                        for g in range(GROUPS):
                            maxima(t * GROUPS + g)
                            if g:
                                negate(t * GROUPS + g - 1)
                        negate(t * GROUPS + GROUPS - 1)
                        for g in range(GROUPS):
                            normalise(t * GROUPS + g)
                    xb = xT[:, bass.ds(b * L, L)]
                    dve.wait_ge(s_wo, 1 + it + 1)
                    tt(xb, bW[:], xb, ALU.add).then_inc(s_x1, 1)
                    dve.wait_ge(s_mean, 1 + it + 1)
                    tt(xc[:], xf[:], bX[:], ALU.subtract).then_inc(s_xc, 1)
                    dve.wait_ge(s_var, 1 + it + 1)
                    ts(va[:], bW[:, 0:T4], 1e-5, None, ALU.add).then_inc(s_va, 1)
                    dve.wait_ge(s_va, 1 + it + 1)
                    rsqrt(nc, dve, s_rstd, it * RSQRT_STEPS, va[:], rstd[:], vt[:])
                    dve.wait_ge(s_rbb, 1 + it + 1)
                    tt(xc[:], xc[:], bX[:], ALU.mult).then_inc(s_xh, 1)
                    dve.wait_ge(s_xh, 1 + it + 1)
                    ts(xn[:], xc[:], sm[:, LNG:LNG + 1], sm[:, LNB:LNB + 1], ALU.mult, ALU.add).then_inc(s_xn, 1)
                    for m in range(3):
                        k = HM[m]
                        dve.wait_ge(s_ge, 1 + it * 3 + m + 1)
                        nc.vector.scalar_tensor_tensor(hd[0:k, m], proj[m % 2][1][0:k, :], sm[0:k, B1A + m:B1A + m + 1],
                                                       ge[0:k, m], ALU.add, ALU.mult).then_inc(s_hd, 1)
                    dve.wait_ge(s_w2, 1 + it + 1)
                    nc.vector.scalar_tensor_tensor(xb, bO[0][:], sm[:, B2C:B2C + 1], xb, ALU.add, ALU.add)\
                        .then_inc(s_res, 1)


def pack_local(d):
    def split(w):
        return w.reshape(DEPTH, C, GROUPS, HG, 2, HALF).transpose(0, 1, 2, 4, 3, 5).reshape(DEPTH, C, INNER)
    w = d["L1_ffn_Wqkv"]
    wqk = np.concatenate([split(w[:, :, 0:INNER]), split(w[:, :, INNER:2 * INNER])], -1)
    sm = np.zeros((DEPTH, P, NSMALL), np.float32)
    for c, v in ((QS1, d["L1_ffn_q_scale"]), (KS1, d["L1_ffn_k_scale"])):
        for half in range(2):
            sm[:, :, c + half] = np.tile(v[:, half * HALF:(half + 1) * HALF], (1, HG))
    sm[:, :, LNG], sm[:, :, LNB], sm[:, :, B2C] = d["L1_ffn_ln_g"], d["L1_ffn_ln_b"], d["L1_ffn_b2"]
    for m in range(3):
        sm[:, 0:HM[m], B1A + m] = d["L1_ffn_b1"][:, m * P:m * P + HM[m]]
        sm[:, 0:HM[m], B1G + m] = d["L1_ffn_b1"][:, DI + m * P:DI + m * P + HM[m]]
    return wqk, np.ascontiguousarray(w[:, :, 2 * INNER:]), sm


DIN = 2 * C
NH = DIN // P
NS = 16
TC = 16
HB = NH * B
W_ = HB * NS
NCH = L // TC
SU = 4
CW, CB, BDT, DPAR, LNW2, LNB2 = 0, 4, 5, 6, 7, 8
NV = 9


def build_ssm_inputs(nc, xn_d, w_in, w_x, w_dt, vec, dt, u, bc, xi_d, sz_d):
    with ExitStack() as ctx:
        def sb(name, shape):
            return ctx.enter_context(nc.sbuf_tensor(name, shape, F32))

        sems = []

        def sem(name):
            sems.append(ctx.enter_context(nc.semaphore(name)))
            return sems[-1]

        xn = sb("m_xn", [P, 2, L])
        win = sb("m_win", [P, 2 * DIN])
        wx = sb("m_wx", [P, NH, 33])
        wdt = sb("m_wdt", [1, DIN])
        vc = sb("m_vec", [P, NH, NV])
        xcv = sb("m_xcv", [P, NH, L])
        xis = sb("m_xis", [P, NH, L])
        szs = sb("m_szs", [P, NH, L])
        dtr = sb("m_dtr", [1, L])
        ab = sb("m_ab", [P, NH, L])
        re = sb("m_re", [P, NH, L])
        bank = [ctx.enter_context(nc.psum_tensor(f"m_b{i}", [P, 512], F32)) for i in range(8)]
        s_c, s_x, s_in, s_cv, s_sl, s_st = (sem(n) for n in ("m_c", "m_x", "m_in", "m_cv", "m_sl", "m_st"))
        s_xd, s_row, s_dtp, s_abs, s_ex, s_ln = (sem(n) for n in ("m_xd", "m_row", "m_dtp", "m_abs", "m_ex", "m_ln"))
        s_bc = sem("m_zero")
        s_re, s_sum, s_dt, s_u = (sem(n) for n in ("m_re", "m_sum", "m_dt", "m_u"))
        block = ctx.enter_context(nc.Block())

        @block.sync
        def _(sp):
            start_at_one(sp, sems)
            sp.dma_start(win[:], w_in).then_inc(s_c, 16)
            sp.dma_start(wx[:], w_x).then_inc(s_c, 16)
            sp.dma_start(wdt[:], w_dt).then_inc(s_c, 16)
            sp.dma_start(vc[:], vec).then_inc(s_c, 16)
            with sp.Fori(0, B) as b:
                sp.wait_ge(s_in, 1 + b)
                sp.dma_start(xn[:, 0], xn_d[:, bass.ds(b * L, L)]).then_inc(s_x, 16)
                sp.wait_ge(s_sl, 1 + (b + 1) * 4)
                sp.dma_start(xi_d[bass.ds(b, 1)].rearrange("a p n -> p (a n)"),
                             xis[:].rearrange("p h t -> p (h t)")).then_inc(s_st, 16)
                sp.dma_start(sz_d[bass.ds(b, 1)].rearrange("a p n -> p (a n)"),
                             szs[:].rearrange("p h t -> p (h t)")).then_inc(s_st, 16)
            sp.wait_ge(s_st, 1 + B * 32)

        @block.gpsimd
        def _(pool):
            nc.gpsimd.memset(bc[:], 0.0).then_inc(s_bc, 1)

        @block.tensor
        def _(pe):
            mul = nc.tensor.matmul
            pe.wait_ge(s_c, 1 + 64)
            with pe.Fori(0, B) as b:
                pe.wait_ge(s_x, 1 + (b + 1) * 16)
                pe.wait_ge(s_cv, 1 + b * 2 * 4)
                pe.wait_ge(s_sl, 1 + b * 4)
                for m in range(4):
                    w = mul(bank[m][:], win[:, m * P:(m + 1) * P], xn[:, 0], start=True, stop=True)
                w.then_inc(s_in, 1)
                pe.wait_ge(s_sl, 1 + b * 4 + 2)
                pe.wait_ge(s_row, 1 + b * 2)
                for o, c in ((bank[4][0:32, :], slice(0, 32)), (bank[5][0:1, :], slice(32, 33))):
                    for h in range(NH):
                        w = mul(o, wx[:, h, c], xis[:, h], start=h == 0, stop=h == NH - 1)
                w.then_inc(s_xd, 1)
                pe.wait_ge(s_row, 1 + b * 2 + 2)
                pe.wait_ge(s_re, 1 + b * 2)
                for h in range(NH):
                    w = mul(bank[6 + h][:], wdt[:, h * P:(h + 1) * P], dtr[:], start=True, stop=True)
                w.then_inc(s_dtp, 1)

        @block.scalar
        def _(act):
            f = nc.scalar.activation
            act.wait_ge(s_c, 1 + 64)
            act.wait_ge(s_bc, 1 + 1)
            with act.Fori(0, B) as b:
                act.wait_ge(s_st, 1 + b * 32)
                act.wait_ge(s_u, 1 + b * 2)
                act.wait_ge(s_cv, 1 + (b + 1) * 2 * 4)
                for h in range(NH):
                    f(xis[:, h], xcv[:, h], ACT.Silu).then_inc(s_sl, 1)
                act.wait_ge(s_in, 1 + b + 1)
                for h in range(NH):
                    f(szs[:, h], bank[2 + h][:], ACT.Silu).then_inc(s_sl, 1)
                act.wait_ge(s_xd, 1 + b + 1)
                f(bc[0:32, :, bass.ds(b, 1)].rearrange("p t a -> p (t a)"), bank[4][0:32, :], ACT.Copy).then_inc(s_row, 1)
                f(dtr[:], bank[5][0:1, :], ACT.Copy).then_inc(s_row, 1)
                act.wait_ge(s_dtp, 1 + b + 1)
                act.wait_ge(s_sum, 1 + b * 2)
                for h in range(NH):
                    f(ab[:, h], bank[6 + h][:], ACT.Abs, bias=vc[:, h, BDT:BDT + 1]).then_inc(s_abs, 1)
                act.wait_ge(s_abs, 1 + (b + 1) * 2)
                for h in range(NH):
                    f(ab[:, h], ab[:, h], ACT.Exp, scale=-1.0).then_inc(s_ex, 1)
                act.wait_ge(s_ex, 1 + (b + 1) * 2)
                for h in range(NH):
                    f(ab[:, h], ab[:, h], ACT.Ln, bias=1.0).then_inc(s_ln, 1)

        @block.vector
        def _(dve):
            tt, ts, stt = nc.vector.tensor_tensor, nc.vector.tensor_scalar, nc.vector.scalar_tensor_tensor
            dve.wait_ge(s_c, 1 + 64)
            with dve.Fori(0, B) as b:
                dve.wait_ge(s_in, 1 + b + 1)
                dve.wait_ge(s_sl, 1 + b * 4)
                for h in range(NH):
                    ts(xcv[:, h], bank[h][:], vc[:, h, CW + 3:CW + 4], vc[:, h, CB:CB + 1], ALU.mult, ALU.add)\
                        .then_inc(s_cv, 1)
                for k in range(1, 4):
                    for h in range(NH):
                        dve.wait_ge(s_cv, 1 + b * 8 + 2 * k - 1 + h)
                        stt(xcv[:, h, k:L], bank[h][:, 0:L - k], vc[:, h, CW + 3 - k:CW + 4 - k], xcv[:, h, k:L],
                            ALU.mult, ALU.add).then_inc(s_cv, 1)
                dve.wait_ge(s_abs, 1 + (b + 1) * 2)
                for h in range(NH):
                    ts(re[:, h], bank[6 + h][:], vc[:, h, BDT:BDT + 1], 0.0, ALU.add, ALU.max).then_inc(s_re, 1)
                for h in range(NH):
                    dve.wait_ge(s_ln, 1 + b * 2 + h + 1)
                    dve.wait_ge(s_re, 1 + b * 2 + h + 1)
                    tt(re[:, h], re[:, h], ab[:, h], ALU.add).then_inc(s_sum, 1)
                for h in range(NH):
                    dve.wait_ge(s_sum, 1 + b * 2 + h + 1)
                    ts(dt[:, bass.ds(b + h * B, 1)].rearrange("p a t -> p (a t)"), re[:, h], 1e-4, 10.0, ALU.max, ALU.min).then_inc(s_dt, 1)
                for h in range(NH):
                    dve.wait_ge(s_dt, 1 + b * 2 + h + 1)
                    tt(u[:, bass.ds(b + h * B, 1)].rearrange("p a t -> p (a t)"), dt[:, bass.ds(b + h * B, 1)].rearrange("p a t -> p (a t)"),
                       xis[:, h], ALU.mult).then_inc(s_u, 1)


def build_ssm_scan(nc, alog, ident_d, dt, u, bc):
    with ExitStack() as ctx:
        def sb(name, shape):
            return ctx.enter_context(nc.sbuf_tensor(name, shape, F32))

        sems = []

        def sem(name):
            sems.append(ctx.enter_context(nc.semaphore(name)))
            return sems[-1]

        def view(buf):
            return buf.rearrange("p (t g s) -> p t g s", t=TC, g=HB)

        A = sb("n_A", [P, NS])
        lim = sb("n_lim", [P, NS])
        idn = sb("n_idn", [P, P])
        dA = [sb(f"n_dA{i}", [P, TC * W_]) for i in range(2)]
        dB = [sb(f"n_dB{i}", [P, TC * W_]) for i in range(2)]
        H = [sb(f"n_H{i}", [P, TC * W_]) for i in range(2)]
        hC = sb("n_hC", [P, TC * W_])
        Cs = sb("n_Cs", [P, NS * TC * B])
        mt = sb("n_mt", [P, W_])
        carry = sb("n_carry", [P, W_])
        bB = [ctx.enter_context(nc.psum_tensor(f"n_bB{i}", [P, 512], F32)) for i in range(4)]
        bC = [ctx.enter_context(nc.psum_tensor(f"n_bC{i}", [P, 512], F32)) for i in range(2)]
        bY = [ctx.enter_context(nc.psum_tensor(f"n_bY{i}", [P, 512], F32)) for i in range(2)]
        s_c, s_a, s_bB, s_bC, s_dx, s_dA, s_dB, s_cl = (sem(n) for n in ("n_c", "n_a", "n_sB", "n_sC", "n_dx", "n_sA", "n_sdB", "n_cl"))
        s_m, s_s, s_h, s_Cs, s_hC, s_y, s_ye = (sem(n) for n in ("n_m", "n_s", "n_h", "n_sCs", "n_shC", "n_y", "n_ye"))
        NU = NS // SU
        block = ctx.enter_context(nc.Block())

        @block.sync
        def _(sp):
            start_at_one(sp, sems)
            sp.dma_start(A[:], alog).then_inc(s_c, 16)
            sp.dma_start(idn[:], ident_d).then_inc(s_c, 16)

        @block.tensor
        def _(pe):
            mul = nc.tensor.matmul
            pe.wait_ge(s_c, 1 + 32)

            def spread(k, row, banks, done, used, used_at):
                for v in range(NU):
                    if used_at(v) is not None:
                        pe.wait_ge(used, 1 + used_at(v))
                    for i in range(SU):
                        s = row + v * SU + i
                        w = mul(banks[v % len(banks)][:, i * TC * B:(i + 1) * TC * B],
                                idn[:, s:s + 1].broadcast_to([P, P]),
                                bc[:, bass.ds(k * TC, TC), :].rearrange("p t b -> p (t b)"), start=True, stop=True)
                    w.then_inc(done, 1)

            spread(0, 0, bB, s_bB, s_dB, lambda v: None)
            with pe.Fori(0, NCH) as k:
                spread(k, NS, bC, s_bC, s_Cs, lambda v: k * NU + v - 1 if v else k * NU)
                spread((k + 1) % NCH, 0, bB, s_bB, s_dB, lambda v: (k + 1) * NU)
                pe.wait_ge(s_ye, 1 + k)
                pe.wait_ge(s_hC, 1 + k + 1)
                for s in range(NS):
                    w = mul(bY[0][:, 0:TC * HB], idn[:], hC[:, s:TC * W_:NS], start=s == 0, stop=s == NS - 1)
                w.then_inc(s_y, 1)

        @block.scalar
        def _(act):
            f = nc.scalar.activation
            act.wait_ge(s_a, 1 + 1)
            f(A[:], A[:], ACT.Exp).then_inc(s_a, 1)

            def exps(kk, i):
                act.wait_ge(s_dx, 1 + kk + 1)
                f(dA[i][:], dA[i][:], ACT.Exp).then_inc(s_dA, 1)

            exps(0, 0)
            with act.Fori(0, NCH // 2) as k2:
                for i in range(2):
                    k = k2 * 2 + i
                    for v in range(NU):
                        act.wait_ge(s_bC, 1 + k * NU + v + 1)
                        if v == 0:
                            act.wait_ge(s_hC, 1 + k)
                        f(Cs[:, v * 512:(v + 1) * 512], bC[v % 2][:], ACT.Copy).then_inc(s_Cs, 1)
                    exps(k + 1, 1 - i)
                    act.wait_ge(s_y, 1 + k + 1)
                    f(u[:, :, bass.ds(k * TC, TC)], bY[0][:, 0:TC * HB].rearrange("p (t g) -> p g t", t=TC), ACT.Copy)\
                        .then_inc(s_ye, 1)

        @block.gpsimd
        def _(pool):
            with pool.Fori(0, NCH // 2) as k2:
                for i in range(2):
                    k = k2 * 2 + i
                    pool.wait_ge(s_h, 1 + (k + 1) * TC)
                    pool.wait_ge(s_Cs, 1 + (k + 1) * NU)
                    pool.wait_ge(s_y, 1 + k)
                    cv = Cs[:].rearrange("p (s t b) -> p t b s", s=NS, t=TC)
                    for h in range(NH):
                        w = nc.gpsimd.tensor_tensor(view(hC[:])[:, :, h * B:(h + 1) * B, :],
                                                    view(H[i][:])[:, :, h * B:(h + 1) * B, :], cv, ALU.mult)
                    w.then_inc(s_hC, 1)

        @block.vector
        def _(dve):
            tt, ts = nc.vector.tensor_tensor, nc.vector.tensor_scalar
            dve.wait_ge(s_c, 1 + 32)
            nc.vector.memset(carry[:], 0.0).then_inc(s_cl, 1)
            ts(A[:], A[:], 5.0, None, ALU.min).then_inc(s_a, 1)
            dve.wait_ge(s_a, 1 + 2)
            nc.vector.reciprocal(lim[:], A[:]).then_inc(s_a, 1)
            dve.wait_ge(s_a, 1 + 3)
            ts(lim[:], lim[:], 20.0, None, ALU.mult).then_inc(s_a, 1)
            ts(A[:], A[:], -1.0, None, ALU.mult).then_inc(s_a, 1)
            dve.wait_ge(s_a, 1 + 5)

            def decay(k, i, s):
                w = ts(view(dA[i][:])[:, :, :, s], dt[:, :, bass.ds(k * TC, TC)].rearrange("p g t -> p t g"),
                       lim[:, s:s + 1], A[:, s:s + 1], ALU.min, ALU.mult)
                if s == NS - 1:
                    w.then_inc(s_dx, 1)

            def drive(k, kw, i, v):
                dve.wait_ge(s_bB, 1 + kw * NU + v + 1)
                for h in range(NH):
                    w = tt(view(dB[i][:])[:, :, h * B:(h + 1) * B, v * SU:(v + 1) * SU],
                           u[:, h * B:(h + 1) * B, bass.ds(k * TC, TC)].rearrange("p b t -> p t b").unsqueeze(3)
                           .broadcast_to([P, TC, B, SU]),
                           bB[v][:].rearrange("p (s t b) -> p t b s", s=SU, t=TC), ALU.mult)
                w.then_inc(s_dB, 1)

            def clip_drive(kw, i):
                dve.wait_ge(s_dB, 1 + (kw + 1) * NU)
                ts(dB[i][:], dB[i][:], 10.0, -10.0, ALU.min, ALU.max).then_inc(s_cl, 1)

            for s in range(NS):
                decay(0, 0, s)
            for v in range(NU):
                drive(0, 0, 0, v)
            clip_drive(0, 0)
            with dve.Fori(0, NCH // 2) as k2:
                for i in range(2):
                    k = k2 * 2 + i
                    kn = (k + 1) % NCH
                    dve.wait_ge(s_dA, 1 + k + 1)
                    dve.wait_ge(s_cl, 1 + k + 2)
                    dve.wait_ge(s_hC, 1 + (k - 1 if i else k))
                    todo = [lambda s=s: decay(kn, 1 - i, s) for s in range(NS)]
                    todo += [lambda v=v: drive(kn, k + 1, 1 - i, v) for v in range(NU)]
                    todo += [lambda: clip_drive(k + 1, 1 - i)]
                    for t in range(TC):
                        now = slice(t * W_, (t + 1) * W_)
                        if t:
                            prev = H[i][:, (t - 1) * W_:t * W_]
                        elif i:
                            prev = H[0][:, (TC - 1) * W_:TC * W_]
                        else:
                            prev = carry[:]
                        tt(mt[:], prev, dA[i][:, now], ALU.mult).then_inc(s_m, 1)
                        if todo:
                            todo.pop(0)()
                        dve.wait_ge(s_m, 1 + k * TC + t + 1)
                        tt(mt[:], mt[:], dB[i][:, now], ALU.add).then_inc(s_s, 1)
                        if len(todo) > TC - t:
                            todo.pop(0)()
                        dve.wait_ge(s_s, 1 + k * TC + t + 1)
                        ts(H[i][:, now], mt[:], 100.0, -100.0, ALU.min, ALU.max).then_inc(s_h, 1)
                        dve.wait_ge(s_h, 1 + k * TC + t + 1)
                    for job in todo:
                        job()
                    if i:
                        nc.vector.tensor_copy(carry[:], H[1][:, (TC - 1) * W_:TC * W_]).then_inc(s_a, 1)
                        dve.wait_ge(s_a, 1 + k2 + 6)


def build_ssm_output(nc, y, xi_d, sz_d, vec, w_out, ident_d, x1_d, ffn_d, out):
    with ExitStack() as ctx:
        def sb(name, shape):
            return ctx.enter_context(nc.sbuf_tensor(name, shape, F32))

        sems = []

        def sem(name):
            sems.append(ctx.enter_context(nc.semaphore(name)))
            return sems[-1]

        vc = sb("o_vec", [P, NH, NV])
        wo = sb("o_wo", [P, NH, C])
        idn = sb("o_idn", [P, P])
        onesD = sb("o_ones", [P, P])
        xi = sb("o_xi", [P, NH, L])
        sz = sb("o_sz", [P, NH, L])
        ff = sb("o_ff", [P, L])
        x1 = sb("o_x1", [P, T4, C])
        yc = sb("o_yc", [P, NH, L])
        yq = sb("o_yq", [P, NH, L])
        gt = sb("o_gt", [P, NH, L])
        va, rstd, vt = sb("o_va", [P, T4]), sb("o_rstd", [P, T4]), sb("o_vt", [P, T4])
        res = sb("o_res", [P, T4, C])
        bM, bV, bR, bO = (ctx.enter_context(nc.psum_tensor(f"o_b{i}", [P, 512], F32)) for i in range(4))
        s_c, s_ld, s_ini, s_mean, s_yc, s_yq, s_var, s_va, s_rs, s_rb, s_n, s_g, s_o, s_res, s_out = (
            sem("o_" + n) for n in ("c", "ld", "ini", "mean", "yc", "yq", "var", "va", "rs", "rb", "n", "g", "o", "res", "out"))
        block = ctx.enter_context(nc.Block())

        @block.sync
        def _(sp):
            start_at_one(sp, sems)
            sp.dma_start(vc[:], vec).then_inc(s_c, 16)
            sp.dma_start(wo[:], w_out).then_inc(s_c, 16)
            sp.dma_start(idn[:], ident_d).then_inc(s_c, 16)
            with sp.Fori(0, B) as b:
                sp.wait_ge(s_res, 1 + b)
                sp.dma_start(xi[:].rearrange("p h t -> p (h t)"), xi_d[bass.ds(b, 1)].rearrange("a p n -> p (a n)")).then_inc(s_ld, 16)
                sp.dma_start(sz[:].rearrange("p h t -> p (h t)"), sz_d[bass.ds(b, 1)].rearrange("a p n -> p (a n)")).then_inc(s_ld, 16)
                sp.dma_start(ff[:], ffn_d[:, bass.ds(b * L, L)]).then_inc(s_ld, 16)
                sp.dma_start(x1[:], x1_d[bass.ds(b, 1)].rearrange("a (t p) c -> p (a t) c", p=P)).then_inc(s_ld, 16)
                sp.wait_ge(s_res, 1 + b + 1)
                sp.dma_start(out[bass.ds(b, 1)].rearrange("a (t p) c -> p (a t) c", p=P), res[:]).then_inc(s_out, 16)
            sp.wait_ge(s_out, 1 + B * 16)

        @block.gpsimd
        def _(pool):
            nc.gpsimd.memset(onesD[:], 1.0 / DIN).then_inc(s_ini, 1)

        @block.tensor
        def _(pe):
            mul = nc.tensor.matmul
            pe.wait_ge(s_c, 1 + 48)
            pe.wait_ge(s_ini, 1 + 1)
            with pe.Fori(0, B) as b:
                pe.wait_ge(s_yc, 1 + b * 2)
                for h in range(NH):
                    w = mul(bM[:], onesD[:], y[:, bass.ds(b + h * B, 1)].rearrange("p a t -> p (a t)"), start=h == 0, stop=h == NH - 1)
                w.then_inc(s_mean, 1)
                pe.wait_ge(s_yq, 1 + (b + 1) * 2)
                for t in range(T4):
                    for h in range(NH):
                        w = mul(bV[:, t:t + 1], yq[:, h, t * P:(t + 1) * P], onesD[:, 0:1], start=h == 0, stop=h == NH - 1)
                w.then_inc(s_var, 1)
                pe.wait_ge(s_rs, 1 + (b + 1) * RSQRT_STEPS)
                for t in range(T4):
                    w = mul(bR[:, t * P:(t + 1) * P], rstd[:, t:t + 1].broadcast_to([P, P]), idn[:], start=True, stop=True)
                w.then_inc(s_rb, 1)
                pe.wait_ge(s_g, 1 + (b + 1) * 2)
                pe.wait_ge(s_ld, 1 + (b + 1) * 64)
                for t in range(T4):
                    q = slice(t * P, (t + 1) * P)
                    mul(bO[:, q], ff[:, q], idn[:], start=True, stop=False)
                    for h in range(NH):
                        w = mul(bO[:, q], gt[:, h, q], wo[:, h], start=False, stop=h == NH - 1)
                w.then_inc(s_o, 1)

        @block.scalar
        def _(act):
            with act.Fori(0, B) as b:
                for h in range(NH):
                    act.wait_ge(s_yc, 1 + b * 2 + h + 1)
                    nc.scalar.activation(yq[:, h], yc[:, h], ACT.Square).then_inc(s_yq, 1)

        @block.vector
        def _(dve):
            tt, ts, stt = nc.vector.tensor_tensor, nc.vector.tensor_scalar, nc.vector.scalar_tensor_tensor
            dve.wait_ge(s_c, 1 + 48)
            with dve.Fori(0, B) as b:
                dve.wait_ge(s_mean, 1 + b + 1)
                for h in range(NH):
                    tt(yc[:, h], y[:, bass.ds(b + h * B, 1)].rearrange("p a t -> p (a t)"), bM[:], ALU.subtract).then_inc(s_yc, 1)
                dve.wait_ge(s_var, 1 + b + 1)
                ts(va[:], bV[:, 0:T4], 1e-5, None, ALU.add).then_inc(s_va, 1)
                dve.wait_ge(s_va, 1 + b + 1)
                rsqrt(nc, dve, s_rs, b * RSQRT_STEPS, va[:], rstd[:], vt[:])
                dve.wait_ge(s_rb, 1 + b + 1)
                dve.wait_ge(s_ld, 1 + (b + 1) * 64)
                dve.wait_ge(s_o, 1 + b)
                for h in range(NH):
                    tt(yc[:, h], yc[:, h], bR[:], ALU.mult).then_inc(s_n, 1)
                for h in range(NH):
                    dve.wait_ge(s_n, 1 + b * 6 + h + 1)
                    ts(yc[:, h], yc[:, h], vc[:, h, LNW2:LNW2 + 1], vc[:, h, LNB2:LNB2 + 1], ALU.mult, ALU.add).then_inc(s_n, 1)
                for h in range(NH):
                    dve.wait_ge(s_n, 1 + b * 6 + h + 3)
                    stt(yc[:, h], xi[:, h], vc[:, h, DPAR:DPAR + 1], yc[:, h], ALU.mult, ALU.add).then_inc(s_n, 1)
                for h in range(NH):
                    dve.wait_ge(s_n, 1 + b * 6 + h + 5)
                    tt(gt[:, h], yc[:, h], sz[:, h], ALU.mult).then_inc(s_g, 1)
                dve.wait_ge(s_o, 1 + b + 1)
                dve.wait_ge(s_out, 1 + b * 16)
                tt(res[:].rearrange("p t c -> p (t c)"), bO[:], x1[:].rearrange("p t c -> p (t c)"), ALU.add).then_inc(s_res, 1)


def pack_ssm(d):
    def halves(v):
        return v.reshape(NH, P, -1).transpose(1, 0, 2)
    vec = np.concatenate([halves(d["L1_attn_" + n]) for n in ("conv_w", "conv_b", "b_dt", "D_param", "ln_w", "ln_b")], -1)
    wx = d["L1_attn_W_x"]
    wx = np.concatenate([wx[1:], wx[0:1]], 0).T.reshape(NH, P, 33).transpose(1, 0, 2)
    return {"w_in": d["L1_attn_W_in"].T, "w_x": wx, "w_dt": d["L1_attn_W_dt"].T, "vec": vec,
            "alog": np.tile(d["L1_attn_A_log"][None], (P, 1)), "w_out": d["L1_attn_W_out"].T.reshape(NH, P, C).transpose(1, 0, 2)}


H0, D0 = 16, C // 16
E, EM, EI, KC = 8, 4, 64, 4
PAIRS = EM * EI // P
G0 = H0 // HG
SC0 = float(1.0 / np.sqrt(np.float32(D0)))
VCH = 51


def build_layer0(nc, x_d, wqk, bqk, wv, bvr, wo, rows, wr, rbias, tri, wg, wu, wd, cw_d, sel_d, ident_d, x1_d, xn1_d):
    with ExitStack() as ctx:
        def sb(name, shape):
            return ctx.enter_context(nc.sbuf_tensor("a_" + name, shape, F32))

        sems = []

        def sem(name):
            sems.append(ctx.enter_context(nc.semaphore("a_" + name)))
            return sems[-1]

        Wqk, Bqk = sb("Wqk", [P, 2 * G0, P]), sb("Bqk", [P, 2 * G0])
        Wv, Bv, Wo = sb("Wv", [P, C]), sb("Bv", [P, C]), sb("Wo", [P, C])
        row2 = sb("row2", [2, C])
        Wr, Rb, Tri = sb("Wr", [P, E]), sb("Rb", [P, E]), sb("Tri", [P, E * E])
        Wg, Wu, Wd = sb("Wg", [P, EM * EI]), sb("Wu", [P, EM * EI]), sb("Wd", [P, PAIRS, C])
        cw = sb("cw", [P, KC])
        sel = sb("sel", [E, PAIRS, P])
        idn = sb("idn", [P, P])
        ones2 = sb("ones2", [2, P])
        diag = sb("diag", [P, KC, P])
        x = sb("x", [P, T4, C])
        xn = sb("xn", [P, T4, C])
        xnT = sb("xnT", [P, KC - 1 + L])
        pad = sb("pad", [P, 1])
        st6 = sb("st6", [P, T4, 6])
        mv = sb("mv", [P, T4, 2])
        va, rstd, vt = sb("va", [P, T4]), sb("rstd", [P, T4]), sb("vt", [P, T4])
        qk = sb("qk", [P, 2 * G0, L])
        V = sb("V", [P, T4, C])
        Pe = sb("Pe", [P, 2, H0, P])
        mx, nm, su = sb("mx", [P, 2, H0]), sb("nm", [P, 2, H0]), sb("su", [P, 2, H0])
        rc = sb("rc", [P, 2, H0])
        PT = sb("PT", [P, 2, HG, P])
        O = sb("O", [P, 2, C])
        OT = sb("OT", [P, L])
        ex, sg, sbi = sb("ex", [P, T4 * E]), sb("sg", [P, T4 * E]), sb("sbi", [P, T4 * E])
        c1, c2 = sb("c1", [P, T4 * E * E]), sb("c2", [P, T4 * E * E])
        rk, cwt = sb("rk", [P, T4 * E]), sb("cwt", [P, T4 * E])
        ws, aw = sb("ws", [P, T4]), sb("aw", [P, T4])
        cwT = sb("cwT", [E, L])
        gs = sb("gs", [P, PAIRS, L])
        hid = sb("hid", [P, PAIRS, L])
        idt = sb("idt", [P, T4, C])
        x1 = sb("x1", [P, T4, C])
        xn1T = sb("xn1T", [P, L])
        K4 = [ctx.enter_context(nc.psum_tensor(f"a_pK{i}", [P, 512], F32)) for i in range(4)]
        bT = [ctx.enter_context(nc.psum_tensor(f"a_pT{i}", [P, 512], F32)) for i in range(2)]
        bO = ctx.enter_context(nc.psum_tensor("a_pO", [P, 512], F32))
        bA = ctx.enter_context(nc.psum_tensor("a_pA", [P, 512], F32))

        s_c, s_ini, s_x, s_st = sem("c"), sem("ini"), sem("x"), sem("st")
        s_v = sem("chain")
        s_xn, s_xnp, s_xnT = sem("xn"), sem("xnp"), sem("xnT")
        s_qp, s_qk, s_vp, s_V = sem("qp"), sem("qk"), sem("vp"), sem("V")
        s_rp, s_ex = sem("rp"), sem("ex")
        s_cw, s_cwp, s_cwT, s_cb = sem("cw"), sem("cwp"), sem("cwT"), sem("cb")
        s_s, s_nm, s_exp = sem("s"), sem("nm"), sem("exp")
        s_pt, s_pte, s_pv, s_O, s_op, s_OT = sem("pt"), sem("pte"), sem("pv"), sem("O"), sem("op"), sem("OT")
        s_gu, s_gs, s_hid, s_acc, s_x1 = sem("gu"), sem("gs"), sem("hid"), sem("acc"), sem("x1")
        s_xn1, s_x1p, s_x1T = sem("xn1"), sem("x1p"), sem("x1T")
        block = ctx.enter_context(nc.Block())
        NG = T4 * G0

        @block.sync
        def _(sp):
            start_at_one(sp, sems)
            for dst, src in ((idn, ident_d), (Wqk, wqk), (Bqk, bqk), (Wv, wv), (Bv, bvr), (Wo, wo), (row2, rows),
                             (Wr, wr), (Rb, rbias), (Tri, tri), (Wg, wg), (Wu, wu), (Wd, wd), (cw, cw_d), (sel, sel_d)):
                sp.dma_start(dst[:], src).then_inc(s_c, 16)
            with sp.Fori(0, B) as b:
                sp.wait_ge(s_x1, 1 + b)
                sp.dma_start(x[:], x_d[bass.ds(b, 1)].rearrange("a (t p) c -> p (a t) c", p=P)).then_inc(s_x, 16)
                sp.wait_ge(s_x1, 1 + b + 1)
                sp.dma_start(x1_d[bass.ds(b, 1)].rearrange("a (t p) c -> p (a t) c", p=P), x1[:]).then_inc(s_st, 16)
                sp.wait_ge(s_x1T, 1 + b + 1)
                sp.dma_start(xn1_d[:, bass.ds(b * L, L)], xn1T[:]).then_inc(s_st, 16)
            sp.wait_ge(s_st, 1 + B * 32)

        CONSTS = 15 * 16

        @block.gpsimd
        def _(pool):
            nc.gpsimd.memset(xnT[:], 0.0).then_inc(s_ini, 1)
            nc.gpsimd.memset(ones2[:], 1.0).then_inc(s_ini, 1)

        @block.tensor
        def _(pe):
            mul, turn = nc.tensor.matmul, nc.tensor.transpose
            pe.wait_ge(s_c, 1 + CONSTS)
            pe.wait_ge(s_ini, 1 + 2 + KC)
            with pe.Fori(0, B) as b:
                pe.wait_ge(s_xn, 1 + b + 1)
                for t in range(T4):
                    w = turn(bT[0][:, t * P:(t + 1) * P], xn[:, t], idn[:])
                w.then_inc(s_xnp, 1)
                pe.wait_ge(s_xnT, 1 + b + 1)
                xm = xnT[:, KC - 1:KC - 1 + L]
                for g in range(2 * G0):
                    if g >= 4:
                        pe.wait_ge(s_qk, 1 + b * 2 * G0 + g - 3)
                    mul(K4[g % 4][:], Wqk[:, g], xm, start=True, stop=True).then_inc(s_qp, 1)
                for t in range(T4):
                    w = mul(bT[1][:, t * P:(t + 1) * P], xnT[:, KC - 1 + t * P:KC - 1 + (t + 1) * P], Wv[:], start=True, stop=True)
                w.then_inc(s_vp, 1)
                for t in range(T4):
                    w = mul(bO[:, t * E:(t + 1) * E], xnT[:, KC - 1 + t * P:KC - 1 + (t + 1) * P], Wr[:], start=True, stop=True)
                w.then_inc(s_rp, 1)
                pe.wait_ge(s_qk, 1 + (b + 1) * 2 * G0)
                pe.wait_ge(s_ex, 1 + b + 1)
                pe.wait_ge(s_V, 1 + b + 1)

                def scores(t):
                    if t:
                        pe.wait_ge(s_exp, 1 + (b * T4 + t) * H0)
                    for g in range(G0):
                        for h in range(HG):
                            r = slice(32 * h, 32 * h + 32)
                            w = mul(K4[h][:, g * P:(g + 1) * P], qk[r, g, t * P:(t + 1) * P],
                                    qk[r, G0 + g, t * P:(t + 1) * P], start=True, stop=True, tile_position=(32 * h, 0))
                    w.then_inc(s_s, 1)

                def turn_weights(t, g):
                    n = t * G0 + g
                    if g == 0:
                        pe.wait_ge(s_exp, 1 + (b * T4 + t + 1) * H0)
                    if n >= 2:
                        pe.wait_ge(s_pte, 1 + b * NG + n - 1)
                    for h in range(HG):
                        w = turn(bT[n % 2][:, h * P:(h + 1) * P], Pe[:, t % 2, h * G0 + g], idn[:])
                    w.then_inc(s_pt, 1)

                def mix(t, g):
                    n = t * G0 + g
                    pe.wait_ge(s_pte, 1 + b * NG + n + 1)
                    if g == 0 and t:
                        pe.wait_ge(s_O, 1 + b * T4 + t)
                    for h in range(HG):
                        hh = g * HG + h
                        w = mul(bO[:, hh * D0:(hh + 1) * D0], PT[:, n % 2, h], V[:, t, hh * D0:(hh + 1) * D0], start=True, stop=True)
                    w.then_inc(s_pv, 1)

                def turn_out(t):
                    pe.wait_ge(s_O, 1 + b * T4 + t + 1)
                    turn(bA[:, t * P:(t + 1) * P], O[:, t % 2], idn[:]).then_inc(s_op, 1)

                for t in range(T4 + 1):
                    if t < T4:
                        scores(t)
                    if t:
                        for g in range(G0):
                            turn_weights(t - 1, g)
                            if g:
                                mix(t - 1, g - 1)
                            elif t >= 2:
                                turn_out(t - 2)
                        mix(t - 1, G0 - 1)
                pe.wait_ge(s_cw, 1 + b + 1)
                for t in range(T4):
                    w = turn(bT[0][0:E, t * P:(t + 1) * P], cwt[:, t * E:(t + 1) * E], idn[:])
                w.then_inc(s_cwp, 1)
                for m in range(PAIRS):
                    mul(K4[2 * m][:], Wg[:, m * P:(m + 1) * P], xm, start=True, stop=True)
                    mul(K4[2 * m + 1][:], Wu[:, m * P:(m + 1) * P], xm, start=True, stop=True).then_inc(s_gu, 1)
                turn_out(T4 - 1)
                pe.wait_ge(s_cwT, 1 + b + 1)
                for m in range(PAIRS):
                    mul(bT[m][:], sel[:, m], cwT[:], start=True, stop=True).then_inc(s_cb, 1)
                pe.wait_ge(s_OT, 1 + b + 1)
                pe.wait_ge(s_hid, 1 + (b + 1) * PAIRS * 2)
                for t in range(T4):
                    o, q = bA[:, t * P:(t + 1) * P], slice(t * P, (t + 1) * P)
                    for k in range(KC):
                        mul(o, xnT[:, k + t * P:k + (t + 1) * P], diag[:, k], start=k == 0, stop=False)
                    mul(o, ones2[:], row2[:], start=False, stop=False)
                    mul(o, OT[:, q], Wo[:], start=False, stop=False)
                    for m in range(PAIRS):
                        w = mul(o, hid[:, m, q], Wd[:, m], start=False, stop=m == PAIRS - 1)
                w.then_inc(s_acc, 1)
                pe.wait_ge(s_xn1, 1 + b + 1)
                for t in range(T4):
                    w = turn(bO[:, t * P:(t + 1) * P], xn[:, t], idn[:])
                w.then_inc(s_x1p, 1)

        @block.scalar
        def _(act):
            f = nc.scalar.activation
            act.wait_ge(s_c, 1 + CONSTS)
            act.wait_ge(s_ini, 1 + 2)
            with act.Fori(0, B) as b:
                act.wait_ge(s_xnp, 1 + b + 1)
                f(xnT[:, KC - 1:KC - 1 + L], bT[0][:], ACT.Copy).then_inc(s_xnT, 1)
                for g in range(2 * G0):
                    act.wait_ge(s_qp, 1 + b * 2 * G0 + g + 1)
                    f(qk[:, g], K4[g % 4][:], ACT.Identity, bias=Bqk[:, g:g + 1]).then_inc(s_qk, 1)
                act.wait_ge(s_rp, 1 + b + 1)
                f(ex[:], bO[:, 0:T4 * E], ACT.Exp, scale=-1.0).then_inc(s_ex, 1)

                def exps(t):
                    act.wait_ge(s_nm, 1 + b * T4 + t + 1)
                    if t >= 2:
                        act.wait_ge(s_pt, 1 + b * NG + (t - 1) * G0)
                    for i in range(H0):
                        f(Pe[:, t % 2, i], K4[i // G0][:, (i % G0) * P:(i % G0 + 1) * P], ACT.Exp,
                          bias=nm[:, t % 2, i:i + 1], scale=SC0, accum_out=su[:, t % 2, i:i + 1]).then_inc(s_exp, 1)

                for t in range(T4):
                    exps(t)
                for m in range(PAIRS):
                    act.wait_ge(s_gu, 1 + b * PAIRS + m + 1)
                    f(gs[:, m], K4[2 * m][:], ACT.Silu).then_inc(s_gs, 1)
                act.wait_ge(s_op, 1 + (b + 1) * T4)
                f(OT[:], bA[:], ACT.Copy).then_inc(s_OT, 1)
                act.wait_ge(s_x1p, 1 + b + 1)
                act.wait_ge(s_st, 1 + b * 32)
                f(xn1T[:], bO[:], ACT.Copy).then_inc(s_x1T, 1)

        @block.vector
        def _(dve):
            tt, ts, stt = nc.vector.tensor_tensor, nc.vector.tensor_scalar, nc.vector.scalar_tensor_tensor
            red = nc.vector.tensor_reduce
            dve.wait_ge(s_c, 1 + CONSTS)
            dve.wait_ge(s_ini, 1 + 2)
            for k in range(KC):
                ts(diag[:, k], idn[:], cw[:, k:k + 1], None, ALU.mult).then_inc(s_ini, 1)
            with dve.Fori(0, B) as b:
                n = [0]

                def link(ins):
                    n[0] += 1
                    ins.then_inc(s_v, 1)
                    dve.wait_ge(s_v, 1 + b * VCH + n[0])

                def norm(src):
                    for t in range(T4):
                        ins = nc.vector.bn_stats(st6[:, t], src[:, t])
                    link(ins)
                    nc.vector.memset(pad[:], 0.0)
                    for t in range(T4):
                        ins = nc.vector.bn_aggr(mv[:, t], st6[:, t])
                    link(ins)
                    link(ts(va[:], mv[:, :, 1], 1e-5, None, ALU.add))
                    base = b * VCH + n[0]
                    rsqrt(nc, dve, s_v, base, va[:], rstd[:], vt[:])
                    n[0] += RSQRT_STEPS
                    for t in range(T4):
                        ins = ts(xn[:, t], src[:, t], mv[:, t, 0:1], rstd[:, t:t + 1], ALU.subtract, ALU.mult)
                    return ins

                dve.wait_ge(s_x, 1 + (b + 1) * 16)
                dve.wait_ge(s_x1p, 1 + b)
                norm(x).then_inc(s_xn, 1)
                dve.wait_ge(s_vp, 1 + b + 1)
                tt(V[:], bT[1][:].rearrange("p (t c) -> p t c", t=T4), Bv[:].unsqueeze(1).broadcast_to([P, T4, C]), ALU.add)\
                    .then_inc(s_V, 1)
                dve.wait_ge(s_ex, 1 + b + 1)
                ev = [P, T4, E]
                eev = [P, T4, E, E]
                te = lambda a: a.rearrange("p (t e) -> p t e", t=T4)
                tef = lambda a: a.rearrange("p (t e f) -> p t e f", t=T4, e=E)
                link(ts(ex[:], ex[:], 1.0, None, ALU.add))
                link(nc.vector.reciprocal(sg[:], ex[:]))
                link(tt(te(sbi[:]), te(sg[:]), Rb[:].unsqueeze(1).broadcast_to(ev), ALU.add))
                mine = te(sbi[:]).unsqueeze(3).broadcast_to(eev)
                other = te(sbi[:]).unsqueeze(2).broadcast_to(eev)
                tt(tef(c1[:]), other, mine, ALU.is_gt)
                link(tt(tef(c2[:]), other, mine, ALU.is_equal))
                link(tt(c2[:].rearrange("p (t e) -> p t e", t=T4), c2[:].rearrange("p (t e) -> p t e", t=T4),
                        Tri[:].unsqueeze(1).broadcast_to([P, T4, E * E]), ALU.mult))
                link(tt(c1[:], c1[:], c2[:], ALU.add))
                link(red(te(rk[:]), tef(c1[:]), AX, ALU.add))
                link(stt(cwt[:], rk[:], 1.5, sg[:], ALU.is_lt, ALU.mult))
                link(red(ws[:], te(cwt[:]), AX, ALU.add))
                link(ts(ws[:], ws[:], 1e-9, None, ALU.add))
                link(nc.vector.reciprocal(aw[:], ws[:]))
                ins = tt(te(cwt[:]), te(cwt[:]), aw[:].unsqueeze(2).broadcast_to(ev), ALU.mult)
                ins.then_inc(s_cw, 1)
                dve.wait_ge(s_cw, 1 + b + 1)
                link(tt(aw[:], te(cwt[:])[:, :, 4], te(cwt[:])[:, :, 6], ALU.add))
                for t in range(T4):
                    ins = ts(idt[:, t], xn[:, t], 0.0, cwt[:, t * E + 7:t * E + 8], ALU.max, ALU.mult)
                link(ins)
                for t in range(T4):
                    ins = stt(idt[:, t], xn[:, t], aw[:, t:t + 1], idt[:, t], ALU.mult, ALU.add)
                link(ins)
                link(tt(idt[:], idt[:], x[:], ALU.add))

                def maxima(t):
                    dve.wait_ge(s_s, 1 + b * T4 + t + 1)
                    for h in range(HG):
                        ins = red(mx[:, t % 2, h * G0:(h + 1) * G0], K4[h][:].rearrange("p (g j) -> p g j", g=G0), AX, ALU.max)
                    link(ins)
                    if t >= 2:
                        dve.wait_ge(s_exp, 1 + (b * T4 + t - 1) * H0)
                    ts(nm[:, t % 2], mx[:, t % 2], -SC0, None, ALU.mult).then_inc(s_nm, 1)

                def evacuate(t, g):
                    m = t * G0 + g
                    dve.wait_ge(s_pt, 1 + b * NG + m + 1)
                    if m >= 2:
                        dve.wait_ge(s_pv, 1 + b * NG + m - 1)
                    nc.vector.tensor_copy(PT[:, m % 2].rearrange("p h j -> p (h j)"), bT[m % 2][:]).then_inc(s_pte, 1)

                def normalise(t):
                    dve.wait_ge(s_exp, 1 + (b * T4 + t + 1) * H0)
                    link(nc.vector.reciprocal(rc[:, t % 2], su[:, t % 2]))
                    dve.wait_ge(s_pv, 1 + b * NG + (t + 1) * G0)
                    if t >= 2:
                        dve.wait_ge(s_op, 1 + b * T4 + t - 1)
                    tt(O[:, t % 2].rearrange("p (g h d) -> p g h d", g=G0, h=HG),
                       bO[:, 0:C].rearrange("p (g h d) -> p g h d", g=G0, h=HG),
                       rc[:, t % 2].rearrange("p (h g) -> p g h", h=HG).unsqueeze(3).broadcast_to([P, G0, HG, D0]),
                       ALU.mult).then_inc(s_O, 1)

                for t in range(T4 + 1):
                    if t < T4:
                        maxima(t)
                    if t:
                        for g in range(G0):
                            evacuate(t - 1, g)
                        normalise(t - 1)
                dve.wait_ge(s_cwp, 1 + b + 1)
                nc.vector.tensor_copy(cwT[:], bT[0][0:E, :]).then_inc(s_cwT, 1)
                for m in range(PAIRS):
                    dve.wait_ge(s_gs, 1 + b * PAIRS + m + 1)
                    tt(hid[:, m], K4[2 * m + 1][:], gs[:, m], ALU.mult).then_inc(s_hid, 1)
                for m in range(PAIRS):
                    dve.wait_ge(s_cb, 1 + b * PAIRS + m + 1)
                    dve.wait_ge(s_hid, 1 + b * 2 * PAIRS + m + 1)
                    tt(hid[:, m], hid[:, m], bT[m][:], ALU.mult).then_inc(s_hid, 1)
                dve.wait_ge(s_acc, 1 + b + 1)
                dve.wait_ge(s_st, 1 + b * 32)
                tt(x1[:].rearrange("p t c -> p (t c)"), bA[:], idt[:].rearrange("p t c -> p (t c)"), ALU.add).then_inc(s_x1, 1)
                dve.wait_ge(s_x1, 1 + b + 1)
                norm(x1).then_inc(s_xn1, 1)
                assert n[0] == VCH


def pack_layer0(d):
    def heads(w):
        out = np.zeros((w.shape[0], G0, HG, 32), np.float32)
        out[..., 0:D0] = w.reshape(w.shape[0], G0, HG, D0)
        return out.reshape(w.shape[0], G0, P)
    g = lambda n: d["L0_" + n]
    bqk = np.concatenate([heads(g("attn_bq")[None]), heads(g("attn_bk")[None])], 1)
    sel = np.zeros((E, PAIRS, P), np.float32)
    for e in range(EM):
        sel[e, e // 2, (e % 2) * EI:(e % 2 + 1) * EI] = 1.0
    return {"w0_wqk": np.concatenate([heads(g("attn_Wq")), heads(g("attn_Wk"))], 1), "w0_bqk": bqk[0].T,
            "w0_wv": g("attn_Wv"), "w0_bv": np.tile(g("attn_bv"), (P, 1)), "w0_wo": g("attn_Wo"),
            "w0_rows": np.stack([g("attn_bo"), g("ffn_conv_b")]), "w0_wr": g("ffn_Wr"),
            "w0_rb": np.tile(g("ffn_router_bias"), (P, 1)),
            "w0_tri": np.tile(np.tril(np.ones((E, E), np.float32), -1).reshape(1, -1), (P, 1)),
            "w0_wg": g("ffn_Wg").transpose(1, 0, 2).reshape(C, -1), "w0_wu": g("ffn_Wu").transpose(1, 0, 2).reshape(C, -1),
            "w0_wd": g("ffn_Wd").reshape(PAIRS, P, C).transpose(1, 0, 2), "w0_cw": g("ffn_conv_w")[:, 0].T, "w0_sel": sel}


def constants():
    return {"ident": np.eye(P, dtype=np.float32), "tabs": rotary_constants(), "masks": band_masks(),
            "blocks": head_blocks(), "spread": spreads()}


def build(nc, a, out):
    x1_d = nc.dram_tensor("x1_d", [B, L, C], F32, kind="Internal").ap()
    xn1_d = nc.dram_tensor("xn1_d", [C, B * L], F32, kind="Internal").ap()
    ffn_d = nc.dram_tensor("ffn_d", [C, B * L], F32, kind="Internal").ap()
    xi_d = nc.dram_tensor("xi_d", [B, P, NH * L], F32, kind="Internal").ap()
    sz_d = nc.dram_tensor("sz_d", [B, P, NH * L], F32, kind="Internal").ap()
    build_layer0(nc, a["x"], *(a["w0_" + n] for n in ("wqk", "bqk", "wv", "bv", "wo", "rows", "wr", "rb", "tri", "wg",
                                                      "wu", "wd", "cw", "sel")), a["ident"], x1_d, xn1_d)
    build_local(nc, xn1_d, ffn_d, *(a[n] for n in ("tabs", "masks", "blocks", "spread", "f_wqk", "f_wv", "f_wo", "f_w1",
                                                   "f_w2", "f_small")), a["ident"])
    with nc.sbuf_tensor("ssm_dt", [P, HB, L], F32) as dt, nc.sbuf_tensor("ssm_u", [P, HB, L], F32) as u:
        with nc.sbuf_tensor("ssm_bc", [P, L, B], F32) as bc:
            build_ssm_inputs(nc, xn1_d, a["w_in"], a["w_x"], a["w_dt"], a["vec"], dt, u, bc, xi_d, sz_d)
            build_ssm_scan(nc, a["alog"], a["ident"], dt, u, bc)
        build_ssm_output(nc, u, xi_d, sz_d, a["vec"], a["w_out"], a["ident"], x1_d, ffn_d, out)


def pack(d):
    wqk, wv, small = pack_local(d)
    return {"x": d["L0_attn_x"], **constants(), **pack_layer0(d), **pack_ssm(d), "f_wqk": wqk, "f_wv": wv,
            "f_small": small, "f_wo": d["L1_ffn_Wo"], "f_w1": d["L1_ffn_W1"], "f_w2": d["L1_ffn_W2"]}


def kernel(**inputs):
    import concourse.bacc as bacc
    from concourse.bass_utils import run_bass_kernel_spmd

    arrays = {n: np.ascontiguousarray(v) for n, v in pack({n: np.asarray(v) for n, v in inputs.items()}).items()}
    nc = bacc.Bacc("TRN2", target_bir_lowering=False, num_devices=1)
    a = {n: nc.dram_tensor(n, v.shape, F32, kind="ExternalInput").ap() for n, v in arrays.items()}
    out = nc.dram_tensor("out", [B, L, C], F32, kind="ExternalOutput").ap()
    build(nc, a, out)
    return run_bass_kernel_spmd(nc, [arrays], core_ids=[0]).results[0]["out"]
```

```python
import numpy as np
from contextlib import ExitStack

import concourse.bass as bass
from concourse import mybir

F32 = mybir.dt.float32
ALU = mybir.AluOpType
ACT = mybir.ActivationFunctionType
AX = mybir.AxisListType.X

P = 128
C = 128
B, L = 8, 512
T4 = L // P


def start_at_one(eng, sems):
    for s in sems:
        eng.sem_inc(s, 1)


DEPTH = 6
HEADS, DH = 16, 64
INNER = HEADS * DH
HALF = DH // 2
HG = P // HALF
GROUPS = HEADS // HG
WINDOW = 32
DI = int(C * 4 * 2 / 3)
HM = [P, P, DI - 2 * P]
QK_SCALE = 8.0
BIG = 1e30
QS1, QS2, KS1, KS2, NATT = 0, 1, 2, 3, 4
LNG, LNB, B2C, B1A, B1G = 0, 1, 2, 3, 6
NSMALL = NATT + 9


def rotary_constants():
    half = np.arange(0, DH, 2, dtype=np.float32)
    inv = (np.float32(1.0) / np.float32(10000.0) ** (half / np.float32(DH))).astype(np.float32)
    t = np.arange(L, dtype=np.float32)
    fr = t[:, None] * inv[None, :]
    base = (half + np.float32(0.4 * DH)) / np.float32(1.4 * DH)
    power = (t - L // 2) / np.float32(WINDOW // 2)
    sc = base[None, :].astype(np.float32) ** power[:, None].astype(np.float32)
    c, s = np.cos(fr), np.sin(fr)
    tabs = np.stack([c * sc, s * sc, c / sc, s / sc]).transpose(2, 0, 1).astype(np.float32)
    return np.ascontiguousarray(np.tile(tabs, (HG, 1, 1)))


def band_masks():
    i, j = np.arange(P)[:, None], np.arange(P)[None, :]
    own = (j <= i) & (j >= i - WINDOW)
    before = (i < WINDOW) & (j >= P - WINDOW) & (j - (P - WINDOW) >= i)
    m = np.stack([own, own | before], 1)
    return np.where(m, 0.0, -BIG).astype(np.float32)


def head_blocks():
    return np.repeat(np.eye(HG, dtype=np.float32), HALF, 0)


def spreads():
    return np.ascontiguousarray(head_blocks().T)


RSQRT_STEPS = 11


def rsqrt(nc, eng, sem, base, x, y, t):
    ts, stt = nc.vector.tensor_scalar, nc.vector.scalar_tensor_tensor
    xi, yi, ti = x.bitcast(mybir.dt.int32), y.bitcast(mybir.dt.int32), t.bitcast(mybir.dt.int32)
    ts(ti, xi, 1, None, ALU.logical_shift_right).then_inc(sem, 1)
    eng.wait_ge(sem, 1 + base + 1)
    ts(yi, ti, -1.0, float(0x5F3759DF), ALU.mult, ALU.add).then_inc(sem, 1)
    for k in range(3):
        eng.wait_ge(sem, 1 + base + 2 + 3 * k)
        nc.vector.tensor_tensor(t, y, y, ALU.mult).then_inc(sem, 1)
        eng.wait_ge(sem, 1 + base + 3 + 3 * k)
        stt(t, x, -0.5, t, ALU.mult, ALU.mult).then_inc(sem, 1)
        eng.wait_ge(sem, 1 + base + 4 + 3 * k)
        stt(y, t, 1.5, y, ALU.add, ALU.mult).then_inc(sem, 1)
    eng.wait_ge(sem, 1 + base + RSQRT_STEPS)


NEWTON = 15


def root_guess(nc, dve, sem, base, y, x, t, between=(None, None)):
    xi, yi, ti = x.bitcast(mybir.dt.int32), y.bitcast(mybir.dt.int32), t.bitcast(mybir.dt.int32)
    if between[0]:
        between[0]()
    dve.wait_ge(sem, 1 + base + 1)
    nc.vector.tensor_scalar(ti, xi, 1, None, ALU.logical_shift_right).then_inc(sem, 1)
    if between[1]:
        between[1]()
    dve.wait_ge(sem, 1 + base + 2)
    nc.vector.tensor_scalar(yi, ti, -1.0, float(0x5F3759DF - 0x400000), ALU.mult, ALU.add).then_inc(sem, 1)


def root_newton(nc, pool, sem, base, y, x, t, c15):
    tt = nc.gpsimd.tensor_tensor
    for k in range(3):
        pool.wait_ge(sem, 1 + base + 3 + 4 * k)
        tt(t, y, y, ALU.mult).then_inc(sem, 1)
        pool.wait_ge(sem, 1 + base + 4 + 4 * k)
        tt(t, t, x, ALU.mult).then_inc(sem, 1)
        pool.wait_ge(sem, 1 + base + 5 + 4 * k)
        tt(t, c15, t, ALU.subtract).then_inc(sem, 1)
        pool.wait_ge(sem, 1 + base + 6 + 4 * k)
        tt(y, y, t, ALU.mult).then_inc(sem, 1)


def build_local(nc, xin, xout, tabs, masks, blocks, spread, wqk, wv, wo, w1, w2, small, ident_d,
                depth=DEPTH, nb=B):
    assert nb >= 3
    total = depth * nb
    NS = GROUPS * T4
    with ExitStack() as ctx:
        def sb(name, shape):
            return ctx.enter_context(nc.sbuf_tensor(name, shape, F32))

        def ps(name, shape=(P, 512)):
            return ctx.enter_context(nc.psum_tensor(name, list(shape), F32))

        sems = []

        def sem(name):
            sems.append(ctx.enter_context(nc.semaphore(name)))
            return sems[-1]

        xT = sb("xT", [P, nb * L])
        xs = sb("xs", [P, L])
        xf = sb("xf", [P, L])
        Wqk = sb("Wqk", [P, 2 * INNER])
        Wv = sb("Wv", [P, INNER])
        Wo = sb("Wo", [P, INNER // P, C])
        W1 = sb("W1", [P, 2 * DI])
        W2 = sb("W2", [P, 3, C])
        smA = sb("smA", [P, NATT])
        smF = sb("smF", [P, NSMALL - NATT])
        tb = sb("tb", [P, 4, L])
        tl = sb("tl", [P, 8, L])
        mk = sb("mk", [P, 2, P])
        blk = sb("blk", [P, HG])
        spr = sb("spr", [HG, P])
        pad, padA = sb("pad", [P, 1]), sb("padA", [P, 1])
        idn = sb("idn", [P, P])
        onesC = sb("onesC", [P, P])
        sq = sb("sq", [P, 2, 2, L])
        sqs = sb("sqs", [P, 2, L])
        mm = sb("mm", [P, 2, 4, L])
        qk = sb("qk", [P, 2, 2, 2, L])
        V = sb("V", [P, 2, T4, HG * DH])
        Vd = sb("Vd", [P, 2, T4 - 1, HG * DH])
        rq = sb("rq", [P, 2, T4 * HG])
        rk = sb("rk", [P, T4 * HG])
        xk, yk = sb("xk", [P, T4 * HG]), sb("yk", [P, T4 * HG])
        xq_, yq = sb("xq_", [P, T4 * HG]), sb("yq", [P, T4 * HG])
        c15 = sb("c15", [P, T4 * HG])
        rT = sb("rT", [HG, L])
        sp = sb("sp", [P, 2, HG, P])
        mx = sb("mx", [P, 2, HG])
        nm = sb("nm", [P, 2, HG])
        su = sb("su", [P, 2, HG])
        rc = sb("rc", [P, 2, HG])
        PT = sb("PT", [P, 2, HG, P])
        OT = sb("OT", [P, INNER // P, L])
        xc = sb("xc", [P, L])
        xv = sb("xv", [P, L])
        xn = sb("xn", [P, L])
        va = sb("va", [P, T4])
        rstd = sb("rstd", [P, T4])
        vt = sb("vt", [P, T4])
        ge = sb("ge", [P, 3, L])
        hd = sb("hd", [P, 3, L])

        bS = [ps("bS0"), ps("bS1")]
        bT, bO = ps("bT"), ps("bO")
        bA, bB = ps("bA"), ps("bB")
        bM, bW = ps("bM"), ps("bW")
        SS = 2 * P

        s_const, s_ini, s_out = sem("s_const"), sem("s_ini"), sem("s_out")
        s_wA = sem("s_wA")
        s_wO = sem("s_wO")
        s_wF = sem("s_wF")
        s_tab = sem("s_tab")
        s_xs = sem("s_xs")
        s_k, s_q = sem("s_k"), sem("s_q")
        s_sqk, s_sqq = sem("s_sqk"), sem("s_sqq")
        s_kk, s_qq = sem("s_kk"), sem("s_qq")
        s_rotk, s_rotq = sem("s_rotk"), sem("s_rotq")
        s_ropek, s_ropeq = sem("s_ropek"), sem("s_ropeq")
        s_ssk, s_ssq = sem("s_ssk"), sem("s_ssq")
        s_rk, s_rq = sem("s_rk"), sem("s_rq")
        s_rtp = sem("s_rtp")
        s_rT = sem("s_rT")
        s_rb = sem("s_rb")
        s_nrm = sem("s_nrm")
        s_vp = sem("s_vp")
        s_v = sem("s_v")
        s_vd = sem("s_vd")
        s_s = [sem("s_s%d" % h) for h in range(HG)]
        s_mx = sem("s_mx")
        s_nm = sem("s_nm")
        s_exp = sem("s_exp")
        s_rc = sem("s_rc")
        s_pn = sem("s_pn")
        s_pt = sem("s_pt")
        s_pte = sem("s_pte")
        s_pv = sem("s_pv")
        s_ot = sem("s_ot")
        s_wo = sem("s_wo")
        s_x1 = sem("s_x1")
        s_xf = sem("s_xf")
        s_mean, s_xc, s_xv, s_var = sem("s_mean"), sem("s_xc"), sem("s_xv"), sem("s_var")
        s_rf = sem("s_rf")
        s_rbb, s_xh, s_xn = sem("s_rbb"), sem("s_xh"), sem("s_xn")
        s_gate, s_val = sem("s_gate"), sem("s_val")
        s_g0 = sem("s_g0")
        s_ge = sem("s_ge")
        s_hd = sem("s_hd")
        s_w2 = sem("s_w2")
        s_res = sem("s_res")

        CONSTS, WA, WF = 16 * 6, 16 * 3, 16 * 4
        block = ctx.enter_context(nc.Block())

        def past(eng, s, n):
            if not isinstance(n, int) or n > 0:
                eng.wait_ge(s, 1 + n)

        def iterations(eng, steps):
            steps(-1, False, False, True)
            steps(0, False, True, True)
            if total > 2:
                with eng.Fori(1, total - 1) as it:
                    steps(it, True, True, True)
            steps(total - 1, True, True, False)
            steps(total, True, False, False)

        def prepares(n, att, nxt):
            return att if n < NS - T4 else nxt

        @block.sync
        def _(sp_):
            start_at_one(sp_, sems)
            sp_.dma_start(xT[:], xin).then_inc(s_const, 16)
            sp_.dma_start(tb[:], tabs).then_inc(s_const, 16)
            sp_.dma_start(mk[:], masks).then_inc(s_const, 16)
            sp_.dma_start(blk[:], blocks).then_inc(s_const, 16)
            sp_.dma_start(spr[:], spread).then_inc(s_const, 16)
            sp_.dma_start(idn[:], ident_d).then_inc(s_const, 16)
            with sp_.Fori(0, depth) as l:
                sp_.wait_ge(s_vp, 1 + l * (nb * GROUPS * 2))
                sp_.wait_ge(s_tab, 1 + l * (nb * 8))
                sp_.dma_start(Wqk[:], wqk[bass.ds(l, 1)].rearrange("a p n -> p (a n)")).then_inc(s_wA, 16)
                sp_.dma_start(Wv[:], wv[bass.ds(l, 1)].rearrange("a p n -> p (a n)")).then_inc(s_wA, 16)
                sp_.dma_start(smA[:], small[bass.ds(l, 1), :, 0:NATT].rearrange("a p n -> p (a n)")).then_inc(s_wA, 16)
                sp_.wait_ge(s_wo, 1 + l * (nb * GROUPS))
                sp_.dma_start(Wo[:], wo[bass.ds(l, 1)].rearrange("a (k p) n -> p (a k) n", p=P)).then_inc(s_wO, 16)
                sp_.wait_ge(s_res, 1 + l * nb)
                sp_.dma_start(W1[:], w1[bass.ds(l, 1)].rearrange("a p n -> p (a n)")).then_inc(s_wF, 16)
                sp_.dma_start(W2[:, 0:2, :], w2[bass.ds(l, 1), 0:2 * P].rearrange("a (k p) n -> p (a k) n", p=P)).then_inc(s_wF, 16)
                sp_.dma_start(W2[0:HM[2], 2, :], w2[bass.ds(l, 1), 2 * P:DI].rearrange("a p n -> p (a n)")).then_inc(s_wF, 16)
                sp_.dma_start(smF[:], small[bass.ds(l, 1), :, NATT:NSMALL].rearrange("a p n -> p (a n)")).then_inc(s_wF, 16)
            sp_.wait_ge(s_res, 1 + total)
            sp_.dma_start(xout, xT[:]).then_inc(s_out, 16)
            sp_.wait_ge(s_out, 1 + 16)

        @block.tensor
        def _(pe):
            mul = nc.tensor.matmul
            pe.wait_ge(s_const, 1 + CONSTS)
            pe.wait_ge(s_ini, 1 + 4)

            def steps(it, prev, att, nxt):
                def scores(n, h):
                    if not att:
                        return
                    t, par = n % T4, n // T4 % 2
                    if h == 0:
                        if t == 0:
                            past(pe, s_nrm, 4 * it + n // T4 + 1)
                            past(pe, s_ropeq, 4 * it + n // T4 + 1)
                        past(pe, s_mx, (NS * it + n - 1) * HG)
                    else:
                        past(pe, s_s[h - 1], NS * it + n + 1)
                    r = slice(h * HALF, (h + 1) * HALF)
                    for half in range(2):
                        w = mul(bS[n % 2][:, h * P:(h + 1) * P], qk[r, par, 0, half, t * P:(t + 1) * P],
                                qk[r, par, 1, half, t * P:(t + 1) * P],
                                start=half == 0, stop=half == 1, tile_position=(h * HALF, 0))
                    if t:
                        for half in range(2):
                            w = mul(bS[n % 2][0:WINDOW, (h + 1) * P - WINDOW:(h + 1) * P],
                                    qk[r, par, 0, half, t * P:t * P + WINDOW],
                                    qk[r, par, 1, half, t * P - WINDOW:t * P],
                                    start=half == 0, stop=half == 1, tile_position=(h * HALF, 0))
                    w.then_inc(s_s[h], 1)

                def turn(n):
                    if not (att if n >= 0 else prev):
                        return
                    past(pe, s_pn, NS * it + n + 1)
                    past(pe, s_pte, NS * it + n)
                    for h in range(HG):
                        w = nc.tensor.transpose(bT[:, h * P:(h + 1) * P], sp[:, n % 2, h], idn[:])
                    w.then_inc(s_pt, 1)

                def mix(n, heads):
                    if not (att if n >= 0 else prev):
                        return
                    t, par = n % T4, n // T4 % 2
                    if heads[0] == 0:
                        past(pe, s_pte, NS * it + n + 1)
                        past(pe, s_ot, NS * it + n)
                        if t == 0:
                            past(pe, s_v, (4 * it + n // T4 + 1) * 2)
                        if t == 1:
                            past(pe, s_vd, 4 * it + n // T4 + 1)
                        if (n + 2) % T4 == 1 and prepares(n + 2, att, nxt):
                            past(pe, s_rk, (4 * it + (n + 2) // T4 + 1) * NEWTON + 1)
                        if (n + 2) % T4 == 3 and prepares(n + 2, att, nxt):
                            past(pe, s_rq, (4 * it + (n + 2) // T4 + 1) * NEWTON + 1)
                    for h in heads:
                        q = slice(64 * (h % 2), 64 * (h % 2) + 64)
                        v = slice(h * DH, (h + 1) * DH)
                        c = (h // 2) * P
                        w = mul(bO[q, c:c + P], V[:, par, t, v], PT[:, n % 2, h], start=True, stop=True)
                        if t:
                            w = mul(bO[q, c:c + WINDOW], Vd[96:P, par, t - 1, v], PT[96:P, n % 2, h, 0:WINDOW],
                                    start=False, stop=True, tile_position=(96, 64 * (h % 2)), skip_group_check=True)
                    if heads[-1] == HG - 1:
                        w.then_inc(s_pv, 1)

                def project(u, g, first):
                    for half in range(2):
                        c = (2 * (first + g) + half) * P
                        w = mul((bA, bB)[half][:], Wqk[:, c:c + P], xs[:], start=True, stop=True)
                    w.then_inc(s_k if first else s_q, 1)

                def sums(n, kind):
                    past(pe, s_ot, NS * it + n - 2)
                    for t in range(T4):
                        w = mul(bO[:, SS + t * HG:SS + (t + 1) * HG], sqs[:, kind, t * P:(t + 1) * P], blk[:],
                                start=True, stop=True)
                    w.then_inc(s_ssk if kind else s_ssq, 1)

                def output(n_it, g):
                    for k in (2 * g, 2 * g + 1):
                        w = mul(bW[:], Wo[:, k], OT[:, k], start=k == 0, stop=k == INNER // P - 1)
                    w.then_inc(s_wo, 1)

                def side0(n):
                    g, t = (n // T4 + 1) % GROUPS, n % T4
                    u = 4 * it + n // T4 + 1
                    if n == 2 and prev:
                        past(pe, s_ot, NS * it)
                        output(it - 1, GROUPS - 1)
                    if n == 8 and prev:
                        if att:
                            past(pe, s_nrm, 4 * it + 2)
                        mul(bM[:], W1[:, DI + P:DI + 2 * P], xn[:], start=True, stop=True).then_inc(s_gate, 1)
                    if not prepares(n, att, nxt):
                        return
                    if t == 0:
                        if n == NS - T4:
                            past(pe, s_wA, ((it + 1) // nb + 1) * WA)
                            past(pe, s_xs, it + 2)
                        past(pe, s_v, 2 * u)
                        project(u, g, GROUPS)
                    if t == 1:
                        past(pe, s_kk, u + 1)
                        sums(n, 1)
                    if t == 3:
                        past(pe, s_qq, u + 1)
                        sums(n, 0)
                        past(pe, s_rT, u + 1)
                        mul(bM[:], spr[:], rT[:], start=True, stop=True).then_inc(s_rb, 1)
                        past(pe, s_rotq, u + 1)
                        for k in range(T4):
                            w = mul((bA, bB)[k // 2][:, (k % 2) * HG * DH:(k % 2 + 1) * HG * DH], xs[:, k * P:(k + 1) * P],
                                    Wv[:, g * HG * DH:(g + 1) * HG * DH], start=True, stop=True)
                            if k % 2:
                                w.then_inc(s_vp, 1)

                def side1(n):
                    g, t = (n // T4 + 1) % GROUPS, n % T4
                    u = 4 * it + n // T4 + 1
                    if prepares(n, att, nxt):
                        if t == 1:
                            past(pe, s_rotk, u + 1)
                            project(u, g, 0)
                        if t == 2:
                            past(pe, s_rk, (u + 1) * NEWTON)
                            past(pe, s_nrm, u)
                            if n == 10 and prev:
                                past(pe, s_hd, 3 * it - 2)
                            for k in range(T4):
                                w = nc.tensor.transpose(bM[0:HG, k * P:(k + 1) * P], rk[:, k * HG:(k + 1) * HG], idn[:])
                            w.then_inc(s_rtp, 1)
                    if prev:
                        if n == 3:
                            past(pe, s_xf, it)
                            mul(bW[:], onesC[:], xf[:], start=True, stop=True).then_inc(s_mean, 1)
                        if n == 4:
                            past(pe, s_xv, it)
                            for k in range(T4):
                                w = mul(bW[:, k:k + 1], xv[:, k * P:(k + 1) * P], onesC[:, 0:1], start=True, stop=True)
                            w.then_inc(s_var, 1)
                        if n == 6:
                            past(pe, s_rf, it * NEWTON)
                            for k in range(T4):
                                w = mul(bW[:, k * P:(k + 1) * P], rstd[:, k:k + 1].broadcast_to([P, P]), idn[:],
                                        start=True, stop=True)
                            w.then_inc(s_rbb, 1)
                        if n == 7:
                            past(pe, s_xn, it)
                            past(pe, s_wF, ((it - 1) // nb + 1) * WF)
                            mul(bW[:], W1[:, DI:DI + P], xn[:], start=True, stop=True).then_inc(s_gate, 1)
                        if n == 8:
                            past(pe, s_g0, it)
                            mul(bW[0:HM[2], :], W1[:, DI + 2 * P:2 * DI], xn[:], start=True, stop=True).then_inc(s_gate, 1)
                        if n == 9:
                            past(pe, s_ge, 3 * it)
                            mul(bM[:], W1[:, 0:P], xn[:], start=True, stop=True).then_inc(s_val, 1)
                            mul(bW[:], W1[:, P:2 * P], xn[:], start=True, stop=True).then_inc(s_val, 1)
                        if n == 11:
                            past(pe, s_hd, 3 * it - 1)
                            mul(bW[0:HM[2], :], W1[:, 2 * P:DI], xn[:], start=True, stop=True).then_inc(s_val, 1)
                        if n == 12:
                            past(pe, s_hd, 3 * it)
                            for m in range(3):
                                w = mul(bW[:], W2[0:HM[m], m], hd[0:HM[m], m], start=m == 0, stop=m == 2)
                            w.then_inc(s_w2, 1)
                    if att and n >= 13:
                        if n == 13:
                            past(pe, s_wO, (it // nb + 1) * 16)
                            if prev:
                                past(pe, s_res, it)
                        past(pe, s_ot, NS * it + (n - 12) * T4)
                        output(it, n - 13)

                for n in range(NS):
                    scores(n, 0)
                    side0(n)
                    scores(n, 1)
                    mix(n - 2, (0, 1))
                    scores(n, 2)
                    mix(n - 2, (2, 3))
                    scores(n, 3)
                    side1(n)
                    turn(n - 1)

            iterations(pe, steps)

        @block.vector
        def _(dve):
            tt, ts, stt = nc.vector.tensor_tensor, nc.vector.tensor_scalar, nc.vector.scalar_tensor_tensor
            dve.wait_ge(s_const, 1 + CONSTS)
            dve.wait_ge(s_ini, 1 + 4)

            def steps(it, prev, att, nxt):
                def normalise(n):
                    if not (att if n >= 0 else prev):
                        return
                    past(dve, s_exp, (NS * it + n + 1) * HG)
                    nc.vector.reciprocal(rc[:, n % 2], su[:, n % 2]).then_inc(s_rc, 1)
                    past(dve, s_rc, NS * it + n + 1)
                    tt(sp[:, n % 2], sp[:, n % 2], rc[:, n % 2].unsqueeze(2).broadcast_to([P, HG, P]), ALU.mult)\
                        .then_inc(s_pn, 1)

                def maxima(n):
                    past(dve, s_s[HG - 1], NS * it + n + 1)
                    if n % T4 == 0:
                        past(dve, s_rq, (4 * it + n // T4 + 1) * NEWTON)
                    nc.vector.memset(pad[:], 0.0)
                    t, par = n % T4, n // T4 % 2
                    for h in range(HG):
                        nc.vector.tensor_tensor_reduce(
                            sp[:, n % 2, h], bS[n % 2][:, h * P:(h + 1) * P], mk[:, 1 if t else 0],
                            rq[:, par, t * HG + h:t * HG + h + 1], -3e38,
                            ALU.add, ALU.max, mx[:, n % 2, h:h + 1]).then_inc(s_mx, 1)
                    past(dve, s_mx, (NS * it + n + 1) * HG)
                    ts(nm[:, n % 2], mx[:, n % 2], -QK_SCALE, None, ALU.mult).then_inc(s_nm, 1)

                def rotate(kind, i):
                    w = tt(mm[:, kind, i], (bA, bB, bB, bA)[i][:], tl[:, 4 * kind + i], ALU.mult)
                    if i == 3:
                        w.then_inc(s_rotk if kind else s_rotq, 1)

                def tables(kind):
                    cols = ((KS1, KS2, KS2, KS1) if kind else (QS1, QS2, QS2, QS1))
                    past(dve, s_wA, ((it + 1) // nb + 1) * WA)
                    for i in range(4):
                        ts(tl[:, 4 * kind + i], tb[:, 2 * kind + i % 2], smA[:, cols[i]:cols[i] + 1], None, ALU.mult)\
                            .then_inc(s_tab, 1)

                for n in range(NS):
                    g, t = (n // T4 + 1) % GROUPS, n % T4
                    u = 4 * it + n // T4 + 1
                    par = (n // T4 + 1) % 2
                    prep = prepares(n, att, nxt)
                    normalise(n - 1)
                    if n == 12 and nxt:
                        tables(0)
                        tables(1)
                    if prep and t == 1:
                        past(dve, s_ssk, u + 1)
                        past(dve, s_rk, u * NEWTON)
                        past(dve, s_rtp, u)
                        ts(xk[:], bO[:, SS:SS + T4 * HG], 1e-24, 0.5, ALU.max, ALU.mult).then_inc(s_rk, 1)
                        past(dve, s_sqk, u + 1)
                        past(dve, s_ropek, u)
                        if n == 13:
                            past(dve, s_tab, (it + 2) * 8)
                        root_guess(nc, dve, s_rk, u * NEWTON, rk[:], xk[:], yk[:],
                                   (lambda: rotate(1, 0), lambda: rotate(1, 1)))
                        rotate(1, 2)
                        rotate(1, 3)
                    if n == 10 and prev:
                        past(dve, s_val, 3 * it - 2)
                        past(dve, s_ge, 3 * it)
                        stt(hd[:, 0], bM[:], smF[:, B1A:B1A + 1], ge[:, 0], ALU.add, ALU.mult).then_inc(s_hd, 1)
                    if prep and t == 2:
                        past(dve, s_sqq, u + 1)
                        past(dve, s_ropeq, u)
                        for i in range(4):
                            rotate(0, i)
                    if prep and t == 3:
                        past(dve, s_ssq, u + 1)
                        past(dve, s_rq, u * NEWTON)
                        ts(xq_[:], bO[:, SS:SS + T4 * HG], 1e-24, 0.5, ALU.max, ALU.mult).then_inc(s_rq, 1)

                        def norm(half):
                            past(dve, s_rb, u + 1)
                            past(dve, s_ropek, u + 1)
                            return tt(qk[:, par, 1, half], qk[:, par, 1, half], bM[:], ALU.mult)
                        root_guess(nc, dve, s_rq, u * NEWTON, rq[:, par], xq_[:], yq[:])
                        norm(0)
                        norm(1).then_inc(s_nrm, 1)
                    if prev:
                        xb = xT[:, bass.ds((it - 1) % nb * L, L)]
                        if n == 3:
                            past(dve, s_wo, 4 * it)
                            tt(xb, bW[:], xb, ALU.add).then_inc(s_x1, 1)
                        if n == 4:
                            past(dve, s_mean, it)
                            tt(xc[:], xf[:], bW[:], ALU.subtract).then_inc(s_xc, 1)
                        if n == 5:
                            past(dve, s_var, it)
                            ts(va[:], bW[:, 0:T4], 1e-5, 0.5, ALU.add, ALU.mult).then_inc(s_rf, 1)
                            root_guess(nc, dve, s_rf, (it - 1) * NEWTON, rstd[:], va[:], vt[:])
                        if n == 7:
                            past(dve, s_rbb, it)
                            tt(xc[:], xc[:], bW[:], ALU.mult).then_inc(s_xh, 1)
                            past(dve, s_xh, it)
                            past(dve, s_wF, ((it - 1) // nb + 1) * WF)
                            ts(xn[:], xc[:], smF[:, LNG:LNG + 1], smF[:, LNB:LNB + 1], ALU.mult, ALU.add).then_inc(s_xn, 1)
                        if n == 12:
                            k = HM[2]
                            past(dve, s_val, 3 * it)
                            stt(hd[0:k, 2], bW[0:k, :], smF[0:k, B1A + 2:B1A + 3], ge[0:k, 2], ALU.add, ALU.mult)\
                                .then_inc(s_hd, 1)
                        if n == 13:
                            past(dve, s_w2, it)
                            stt(xb, bW[:], smF[:, B2C:B2C + 1], xb, ALU.add, ALU.add).then_inc(s_res, 1)
                    if att:
                        maxima(n)
                    if n == 10 and prev:
                        past(dve, s_val, 3 * it - 1)
                        stt(hd[:, 1], bW[:], smF[:, B1A + 1:B1A + 2], ge[:, 1], ALU.add, ALU.mult).then_inc(s_hd, 1)

            iterations(dve, steps)

        @block.scalar
        def _(act):
            f = nc.scalar.activation
            act.wait_ge(s_const, 1 + CONSTS)
            act.wait_ge(s_ini, 1 + 4)

            def steps(it, prev, att, nxt):
                def exps(n):
                    if not (att if n >= 0 else prev):
                        return
                    past(act, s_nm, NS * it + n + 1)
                    for h in range(HG):
                        f(sp[:, n % 2, h], sp[:, n % 2, h], ACT.Exp, bias=nm[:, n % 2, h:h + 1], scale=QK_SCALE,
                          accum_out=su[:, n % 2, h:h + 1]).then_inc(s_exp, 1)

                def turned(n):
                    if not (att if n >= 0 else prev):
                        return
                    past(act, s_pt, NS * it + n + 1)
                    past(act, s_pv, NS * it + n - 1)
                    f(PT[:, n % 2], bT[:].rearrange("p (h q) -> p h q", h=HG), ACT.Copy).then_inc(s_pte, 1)

                def mixed(n):
                    if not (att if n >= 0 else prev):
                        return
                    g, t = n // T4 % GROUPS, n % T4
                    past(act, s_pv, NS * it + n + 1)
                    if t == 0:
                        past(act, s_wo, 4 * (it if n >= 0 else it - 1) + g - 3)
                    f(OT[:, 2 * g:2 * g + 2, t * P:(t + 1) * P],
                      bO[:, 0:2 * P].rearrange("p (h q) -> p h q", h=2), ACT.Copy).then_inc(s_ot, 1)

                def shift(dst, seq, s):
                    f(padA[:], blk[:, 0:1], ACT.Copy)
                    f(dst[0:64, :], xT[0:64, bass.ds(seq * L, L)], ACT.Copy)
                    f(dst[64:P, 1:L], xT[64:P, bass.ds(seq * L, L - 1)], ACT.Copy).then_inc(s, 1)

                for n in range(NS):
                    t = n % T4
                    u = 4 * it + n // T4 + 1
                    par = (n // T4 + 1) % 2
                    prep = prepares(n, att, nxt)
                    exps(n - 1)
                    turned(n - 2)
                    if prep and t == 0:
                        past(act, s_k, u + 1)
                        past(act, s_kk, u)
                        f(sq[:, 1, 0], bA[:], ACT.Square)
                        f(sq[:, 1, 1], bB[:], ACT.Square).then_inc(s_sqk, 1)
                    if prep and t == 2:
                        past(act, s_q, u + 1)
                        past(act, s_qq, u)
                        f(sq[:, 0, 0], bA[:], ACT.Square)
                        f(sq[:, 0, 1], bB[:], ACT.Square).then_inc(s_sqq, 1)
                    if n == 4 and prev:
                        past(act, s_xc, it)
                        f(xv[:], xc[:], ACT.Square).then_inc(s_xv, 1)
                    if n == 8 and prev:
                        past(act, s_gate, 3 * it - 2)
                        f(ge[:, 0], bW[:], ACT.Copy).then_inc(s_g0, 1)
                    if prep and t == 3:
                        past(act, s_pv, 4 * (u - 1))
                        for k in range(2):
                            past(act, s_vp, 2 * u + k + 1)
                            f(V[:, par, 2 * k:2 * k + 2], (bA, bB)[k][:].rearrange("p (t d) -> p t d", t=2), ACT.Copy)\
                                .then_inc(s_v, 1)
                    if n == 9 and prev:
                        past(act, s_gate, 3 * it)
                        past(act, s_g0, it)
                        for m, src in ((0, ge[:, 0]), (1, bM[:]), (2, bW[0:HM[2], :])):
                            k = HM[m]
                            f(ge[0:k, m], src, ACT.Gelu, bias=smF[0:k, B1G + m:B1G + m + 1]).then_inc(s_ge, 1)
                    mixed(n - 2)
                    if prep and t == 2:
                        past(act, s_rtp, u + 1)
                        past(act, s_rb, u)
                        f(rT[:], bM[0:HG, :], ACT.Copy).then_inc(s_rT, 1)
                    if n == 3 and prev:
                        past(act, s_x1, it)
                        shift(xf, (it - 1) % nb, s_xf)
                    if n == 11 and nxt:
                        past(act, s_vp, 2 * (u + 1))
                        past(act, s_res, it - 1)
                        shift(xs, (it + 1) % nb, s_xs)

            iterations(act, steps)

        @block.gpsimd
        def _(pool):
            nc.gpsimd.memset(xs[:], 0.0).then_inc(s_ini, 1)
            nc.gpsimd.memset(xf[:], 0.0).then_inc(s_ini, 1)
            nc.gpsimd.memset(onesC[:], 1.0 / C).then_inc(s_ini, 1)
            nc.gpsimd.memset(c15[:], 1.5).then_inc(s_ini, 1)
            pool.wait_ge(s_ini, 1 + 4)
            pool.wait_ge(s_const, 1 + CONSTS)
            tt = nc.gpsimd.tensor_tensor

            def steps(it, prev, att, nxt):
                for n in range(NS):
                    t = n % T4
                    u = 4 * it + n // T4 + 1
                    par = (n // T4 + 1) % 2
                    prep = prepares(n, att, nxt)
                    if prep and t == 0:
                        past(pool, s_sqk, u + 1)
                        past(pool, s_ssk, u)
                        tt(sqs[:, 1], sq[:, 1, 0], sq[:, 1, 1], ALU.add).then_inc(s_kk, 1)
                    if prep and t == 1:
                        root_newton(nc, pool, s_rk, u * NEWTON, rk[:], xk[:], yk[:], c15[:])
                        past(pool, s_rotk, u + 1)
                        past(pool, s_s[HG - 1], 4 * (u - 1))
                        tt(qk[:, par, 1, 0], mm[:, 1, 0], mm[:, 1, 1], ALU.subtract)
                        tt(qk[:, par, 1, 1], mm[:, 1, 2], mm[:, 1, 3], ALU.add).then_inc(s_ropek, 1)
                    if n == 5 and prev:
                        root_newton(nc, pool, s_rf, (it - 1) * NEWTON, rstd[:], va[:], vt[:], c15[:, 0:T4])
                    if prep and t == 2:
                        past(pool, s_sqq, u + 1)
                        past(pool, s_ssq, u)
                        tt(sqs[:, 0], sq[:, 0, 0], sq[:, 0, 1], ALU.add).then_inc(s_qq, 1)
                        past(pool, s_rotq, u + 1)
                        tt(qk[:, par, 0, 0], mm[:, 0, 0], mm[:, 0, 1], ALU.subtract)
                        tt(qk[:, par, 0, 1], mm[:, 0, 2], mm[:, 0, 3], ALU.add).then_inc(s_ropeq, 1)
                    if prep and t == 3:
                        root_newton(nc, pool, s_rq, u * NEWTON, rq[:, par], xq_[:], yq[:], c15[:])
                        past(pool, s_v, 2 * (u + 1))
                        tt(Vd[:, par], V[:, par, 0:T4 - 1], V[:, par, 1:T4], ALU.subtract).then_inc(s_vd, 1)

            iterations(pool, steps)


def pack_local(d):
    def split(w):
        return w.reshape(DEPTH, C, GROUPS, HG, 2, HALF).transpose(0, 1, 2, 4, 3, 5).reshape(DEPTH, C, INNER)
    w = d["L1_ffn_Wqkv"]
    wqk = np.concatenate([split(w[:, :, 0:INNER]), split(w[:, :, INNER:2 * INNER])], -1)
    sm = np.zeros((DEPTH, P, NSMALL), np.float32)
    for c, v in ((QS1, d["L1_ffn_q_scale"]), (KS1, d["L1_ffn_k_scale"])):
        for half in range(2):
            sm[:, :, c + half] = np.tile(v[:, half * HALF:(half + 1) * HALF], (1, HG))
    sm[:, :, NATT + LNG], sm[:, :, NATT + LNB], sm[:, :, NATT + B2C] = d["L1_ffn_ln_g"], d["L1_ffn_ln_b"], d["L1_ffn_b2"]
    for m in range(3):
        sm[:, 0:HM[m], NATT + B1A + m] = d["L1_ffn_b1"][:, m * P:m * P + HM[m]]
        sm[:, 0:HM[m], NATT + B1G + m] = d["L1_ffn_b1"][:, DI + m * P:DI + m * P + HM[m]]
    return wqk, np.ascontiguousarray(w[:, :, 2 * INNER:]), sm


DIN = 2 * C
NH = DIN // P
NS = 16
TC = 16
HB = NH * B
W_ = HB * NS
NCH = L // TC
SU = 4
CW, CB, BDT, DPAR, LNW2, LNB2 = 0, 4, 5, 6, 7, 8
NV = 9


def build_ssm_inputs(nc, xn_d, w_in, w_x, w_dt, vec, dt, u, bc, xi_d, sz_d):
    with ExitStack() as ctx:
        def sb(name, shape):
            return ctx.enter_context(nc.sbuf_tensor(name, shape, F32))

        sems = []

        def sem(name):
            sems.append(ctx.enter_context(nc.semaphore(name)))
            return sems[-1]

        xn = sb("m_xn", [P, 2, L])
        win = sb("m_win", [P, 2 * DIN])
        wx = sb("m_wx", [P, NH, 33])
        wdt = sb("m_wdt", [1, DIN])
        vc = sb("m_vec", [P, NH, NV])
        xcv = sb("m_xcv", [P, NH, L])
        xis = sb("m_xis", [P, NH, L])
        szs = sb("m_szs", [P, NH, L])
        dtr = sb("m_dtr", [1, L])
        ab = sb("m_ab", [P, NH, L])
        re = sb("m_re", [P, NH, L])
        bank = [ctx.enter_context(nc.psum_tensor(f"m_b{i}", [P, 512], F32)) for i in range(8)]
        s_c, s_x, s_in, s_cv, s_sl, s_st = (sem(n) for n in ("m_c", "m_x", "m_in", "m_cv", "m_sl", "m_st"))
        s_xd, s_row, s_dtp, s_abs, s_ex, s_ln = (sem(n) for n in ("m_xd", "m_row", "m_dtp", "m_abs", "m_ex", "m_ln"))
        s_bc = sem("m_zero")
        s_re, s_sum, s_dt, s_u = (sem(n) for n in ("m_re", "m_sum", "m_dt", "m_u"))
        block = ctx.enter_context(nc.Block())

        @block.sync
        def _(sp):
            start_at_one(sp, sems)
            sp.dma_start(win[:], w_in).then_inc(s_c, 16)
            sp.dma_start(wx[:], w_x).then_inc(s_c, 16)
            sp.dma_start(wdt[:], w_dt).then_inc(s_c, 16)
            sp.dma_start(vc[:], vec).then_inc(s_c, 16)
            with sp.Fori(0, B) as b:
                sp.wait_ge(s_in, 1 + b)
                sp.dma_start(xn[:, 0], xn_d[:, bass.ds(b * L, L)]).then_inc(s_x, 16)
                sp.wait_ge(s_sl, 1 + (b + 1) * 4)
                sp.dma_start(xi_d[bass.ds(b, 1)].rearrange("a p n -> p (a n)"),
                             xis[:].rearrange("p h t -> p (h t)")).then_inc(s_st, 16)
                sp.dma_start(sz_d[bass.ds(b, 1)].rearrange("a p n -> p (a n)"),
                             szs[:].rearrange("p h t -> p (h t)")).then_inc(s_st, 16)
            sp.wait_ge(s_st, 1 + B * 32)

        @block.gpsimd
        def _(pool):
            nc.gpsimd.memset(bc[:], 0.0).then_inc(s_bc, 1)

        @block.tensor
        def _(pe):
            mul = nc.tensor.matmul
            pe.wait_ge(s_c, 1 + 64)
            with pe.Fori(0, B) as b:
                pe.wait_ge(s_x, 1 + (b + 1) * 16)
                pe.wait_ge(s_cv, 1 + b * 2 * 4)
                pe.wait_ge(s_sl, 1 + b * 4)
                for m in range(4):
                    w = mul(bank[m][:], win[:, m * P:(m + 1) * P], xn[:, 0], start=True, stop=True)
                w.then_inc(s_in, 1)
                pe.wait_ge(s_sl, 1 + b * 4 + 2)
                pe.wait_ge(s_row, 1 + b * 2)
                for o, c in ((bank[4][0:32, :], slice(0, 32)), (bank[5][0:1, :], slice(32, 33))):
                    for h in range(NH):
                        w = mul(o, wx[:, h, c], xis[:, h], start=h == 0, stop=h == NH - 1)
                w.then_inc(s_xd, 1)
                pe.wait_ge(s_row, 1 + b * 2 + 2)
                pe.wait_ge(s_re, 1 + b * 2)
                for h in range(NH):
                    w = mul(bank[6 + h][:], wdt[:, h * P:(h + 1) * P], dtr[:], start=True, stop=True)
                w.then_inc(s_dtp, 1)

        @block.scalar
        def _(act):
            f = nc.scalar.activation
            act.wait_ge(s_c, 1 + 64)
            act.wait_ge(s_bc, 1 + 1)
            with act.Fori(0, B) as b:
                act.wait_ge(s_st, 1 + b * 32)
                act.wait_ge(s_u, 1 + b * 2)
                act.wait_ge(s_cv, 1 + (b + 1) * 2 * 4)
                for h in range(NH):
                    f(xis[:, h], xcv[:, h], ACT.Silu).then_inc(s_sl, 1)
                act.wait_ge(s_in, 1 + b + 1)
                for h in range(NH):
                    f(szs[:, h], bank[2 + h][:], ACT.Silu).then_inc(s_sl, 1)
                act.wait_ge(s_xd, 1 + b + 1)
                f(bc[0:32, :, bass.ds(b, 1)].rearrange("p t a -> p (t a)"), bank[4][0:32, :], ACT.Copy).then_inc(s_row, 1)
                f(dtr[:], bank[5][0:1, :], ACT.Copy).then_inc(s_row, 1)
                act.wait_ge(s_dtp, 1 + b + 1)
                act.wait_ge(s_sum, 1 + b * 2)
                for h in range(NH):
                    f(ab[:, h], bank[6 + h][:], ACT.Abs, bias=vc[:, h, BDT:BDT + 1]).then_inc(s_abs, 1)
                act.wait_ge(s_abs, 1 + (b + 1) * 2)
                for h in range(NH):
                    f(ab[:, h], ab[:, h], ACT.Exp, scale=-1.0).then_inc(s_ex, 1)
                act.wait_ge(s_ex, 1 + (b + 1) * 2)
                for h in range(NH):
                    f(ab[:, h], ab[:, h], ACT.Ln, bias=1.0).then_inc(s_ln, 1)

        @block.vector
        def _(dve):
            tt, ts, stt = nc.vector.tensor_tensor, nc.vector.tensor_scalar, nc.vector.scalar_tensor_tensor
            dve.wait_ge(s_c, 1 + 64)
            with dve.Fori(0, B) as b:
                dve.wait_ge(s_in, 1 + b + 1)
                dve.wait_ge(s_sl, 1 + b * 4)
                for h in range(NH):
                    ts(xcv[:, h], bank[h][:], vc[:, h, CW + 3:CW + 4], vc[:, h, CB:CB + 1], ALU.mult, ALU.add)\
                        .then_inc(s_cv, 1)
                for k in range(1, 4):
                    for h in range(NH):
                        dve.wait_ge(s_cv, 1 + b * 8 + 2 * k - 1 + h)
                        stt(xcv[:, h, k:L], bank[h][:, 0:L - k], vc[:, h, CW + 3 - k:CW + 4 - k], xcv[:, h, k:L],
                            ALU.mult, ALU.add).then_inc(s_cv, 1)
                dve.wait_ge(s_abs, 1 + (b + 1) * 2)
                for h in range(NH):
                    ts(re[:, h], bank[6 + h][:], vc[:, h, BDT:BDT + 1], 0.0, ALU.add, ALU.max).then_inc(s_re, 1)
                for h in range(NH):
                    dve.wait_ge(s_ln, 1 + b * 2 + h + 1)
                    dve.wait_ge(s_re, 1 + b * 2 + h + 1)
                    tt(re[:, h], re[:, h], ab[:, h], ALU.add).then_inc(s_sum, 1)
                for h in range(NH):
                    dve.wait_ge(s_sum, 1 + b * 2 + h + 1)
                    ts(dt[:, bass.ds(b + h * B, 1)].rearrange("p a t -> p (a t)"), re[:, h], 1e-4, 10.0, ALU.max, ALU.min).then_inc(s_dt, 1)
                for h in range(NH):
                    dve.wait_ge(s_dt, 1 + b * 2 + h + 1)
                    tt(u[:, bass.ds(b + h * B, 1)].rearrange("p a t -> p (a t)"), dt[:, bass.ds(b + h * B, 1)].rearrange("p a t -> p (a t)"),
                       xis[:, h], ALU.mult).then_inc(s_u, 1)


def build_ssm_scan(nc, alog, ident_d, dt, u, bc):
    with ExitStack() as ctx:
        def sb(name, shape):
            return ctx.enter_context(nc.sbuf_tensor(name, shape, F32))

        sems = []

        def sem(name):
            sems.append(ctx.enter_context(nc.semaphore(name)))
            return sems[-1]

        def view(buf):
            return buf.rearrange("p (t g s) -> p t g s", t=TC, g=HB)

        A = sb("n_A", [P, NS])
        lim = sb("n_lim", [P, NS])
        idn = sb("n_idn", [P, P])
        dA = [sb(f"n_dA{i}", [P, TC * W_]) for i in range(2)]
        dB = [sb(f"n_dB{i}", [P, TC * W_]) for i in range(2)]
        H = [sb(f"n_H{i}", [P, TC * W_]) for i in range(2)]
        hC = sb("n_hC", [P, TC * W_])
        Cs = sb("n_Cs", [P, NS * TC * B])
        mt = sb("n_mt", [P, W_])
        carry = sb("n_carry", [P, W_])
        bB = [ctx.enter_context(nc.psum_tensor(f"n_bB{i}", [P, 512], F32)) for i in range(4)]
        bC = [ctx.enter_context(nc.psum_tensor(f"n_bC{i}", [P, 512], F32)) for i in range(2)]
        bY = [ctx.enter_context(nc.psum_tensor(f"n_bY{i}", [P, 512], F32)) for i in range(2)]
        s_c, s_a, s_bB, s_bC, s_dx, s_dA, s_dB, s_cl = (sem(n) for n in ("n_c", "n_a", "n_sB", "n_sC", "n_dx", "n_sA", "n_sdB", "n_cl"))
        s_m, s_s, s_h, s_Cs, s_hC, s_y, s_ye = (sem(n) for n in ("n_m", "n_s", "n_h", "n_sCs", "n_shC", "n_y", "n_ye"))
        NU = NS // SU
        block = ctx.enter_context(nc.Block())

        @block.sync
        def _(sp):
            start_at_one(sp, sems)
            sp.dma_start(A[:], alog).then_inc(s_c, 16)
            sp.dma_start(idn[:], ident_d).then_inc(s_c, 16)

        @block.tensor
        def _(pe):
            mul = nc.tensor.matmul
            pe.wait_ge(s_c, 1 + 32)

            def spread(k, row, banks, done, used, used_at):
                for v in range(NU):
                    if used_at(v) is not None:
                        pe.wait_ge(used, 1 + used_at(v))
                    for i in range(SU):
                        s = row + v * SU + i
                        w = mul(banks[v % len(banks)][:, i * TC * B:(i + 1) * TC * B],
                                idn[:, s:s + 1].broadcast_to([P, P]),
                                bc[:, bass.ds(k * TC, TC), :].rearrange("p t b -> p (t b)"), start=True, stop=True)
                    w.then_inc(done, 1)

            spread(0, 0, bB, s_bB, s_dB, lambda v: None)
            with pe.Fori(0, NCH) as k:
                spread(k, NS, bC, s_bC, s_Cs, lambda v: k * NU + v - 1 if v else k * NU)
                spread((k + 1) % NCH, 0, bB, s_bB, s_dB, lambda v: (k + 1) * NU)
                pe.wait_ge(s_ye, 1 + k)
                pe.wait_ge(s_hC, 1 + k + 1)
                for s in range(NS):
                    w = mul(bY[0][:, 0:TC * HB], idn[:], hC[:, s:TC * W_:NS], start=s == 0, stop=s == NS - 1)
                w.then_inc(s_y, 1)

        @block.scalar
        def _(act):
            f = nc.scalar.activation
            act.wait_ge(s_a, 1 + 1)
            f(A[:], A[:], ACT.Exp).then_inc(s_a, 1)

            def exps(kk, i):
                act.wait_ge(s_dx, 1 + kk + 1)
                f(dA[i][:], dA[i][:], ACT.Exp).then_inc(s_dA, 1)

            exps(0, 0)
            with act.Fori(0, NCH // 2) as k2:
                for i in range(2):
                    k = k2 * 2 + i
                    for v in range(NU):
                        act.wait_ge(s_bC, 1 + k * NU + v + 1)
                        if v == 0:
                            act.wait_ge(s_hC, 1 + k)
                        f(Cs[:, v * 512:(v + 1) * 512], bC[v % 2][:], ACT.Copy).then_inc(s_Cs, 1)
                    exps(k + 1, 1 - i)
                    act.wait_ge(s_y, 1 + k + 1)
                    f(u[:, :, bass.ds(k * TC, TC)], bY[0][:, 0:TC * HB].rearrange("p (t g) -> p g t", t=TC), ACT.Copy)\
                        .then_inc(s_ye, 1)

        @block.gpsimd
        def _(pool):
            with pool.Fori(0, NCH // 2) as k2:
                for i in range(2):
                    k = k2 * 2 + i
                    pool.wait_ge(s_h, 1 + (k + 1) * TC)
                    pool.wait_ge(s_Cs, 1 + (k + 1) * NU)
                    pool.wait_ge(s_y, 1 + k)
                    cv = Cs[:].rearrange("p (s t b) -> p t b s", s=NS, t=TC)
                    for h in range(NH):
                        w = nc.gpsimd.tensor_tensor(view(hC[:])[:, :, h * B:(h + 1) * B, :],
                                                    view(H[i][:])[:, :, h * B:(h + 1) * B, :], cv, ALU.mult)
                    w.then_inc(s_hC, 1)

        @block.vector
        def _(dve):
            tt, ts = nc.vector.tensor_tensor, nc.vector.tensor_scalar
            dve.wait_ge(s_c, 1 + 32)
            nc.vector.memset(carry[:], 0.0).then_inc(s_cl, 1)
            ts(A[:], A[:], 5.0, None, ALU.min).then_inc(s_a, 1)
            dve.wait_ge(s_a, 1 + 2)
            nc.vector.reciprocal(lim[:], A[:]).then_inc(s_a, 1)
            dve.wait_ge(s_a, 1 + 3)
            ts(lim[:], lim[:], 20.0, None, ALU.mult).then_inc(s_a, 1)
            ts(A[:], A[:], -1.0, None, ALU.mult).then_inc(s_a, 1)
            dve.wait_ge(s_a, 1 + 5)

            def decay(k, i, s):
                w = ts(view(dA[i][:])[:, :, :, s], dt[:, :, bass.ds(k * TC, TC)].rearrange("p g t -> p t g"),
                       lim[:, s:s + 1], A[:, s:s + 1], ALU.min, ALU.mult)
                if s == NS - 1:
                    w.then_inc(s_dx, 1)

            def drive(k, kw, i, v):
                dve.wait_ge(s_bB, 1 + kw * NU + v + 1)
                for h in range(NH):
                    w = tt(view(dB[i][:])[:, :, h * B:(h + 1) * B, v * SU:(v + 1) * SU],
                           u[:, h * B:(h + 1) * B, bass.ds(k * TC, TC)].rearrange("p b t -> p t b").unsqueeze(3)
                           .broadcast_to([P, TC, B, SU]),
                           bB[v][:].rearrange("p (s t b) -> p t b s", s=SU, t=TC), ALU.mult)
                w.then_inc(s_dB, 1)

            def clip_drive(kw, i):
                dve.wait_ge(s_dB, 1 + (kw + 1) * NU)
                ts(dB[i][:], dB[i][:], 10.0, -10.0, ALU.min, ALU.max).then_inc(s_cl, 1)

            for s in range(NS):
                decay(0, 0, s)
            for v in range(NU):
                drive(0, 0, 0, v)
            clip_drive(0, 0)
            with dve.Fori(0, NCH // 2) as k2:
                for i in range(2):
                    k = k2 * 2 + i
                    kn = (k + 1) % NCH
                    dve.wait_ge(s_dA, 1 + k + 1)
                    dve.wait_ge(s_cl, 1 + k + 2)
                    dve.wait_ge(s_hC, 1 + (k - 1 if i else k))
                    todo = [lambda s=s: decay(kn, 1 - i, s) for s in range(NS)]
                    todo += [lambda v=v: drive(kn, k + 1, 1 - i, v) for v in range(NU)]
                    todo += [lambda: clip_drive(k + 1, 1 - i)]
                    for t in range(TC):
                        now = slice(t * W_, (t + 1) * W_)
                        if t:
                            prev = H[i][:, (t - 1) * W_:t * W_]
                        elif i:
                            prev = H[0][:, (TC - 1) * W_:TC * W_]
                        else:
                            prev = carry[:]
                        tt(mt[:], prev, dA[i][:, now], ALU.mult).then_inc(s_m, 1)
                        if todo:
                            todo.pop(0)()
                        dve.wait_ge(s_m, 1 + k * TC + t + 1)
                        tt(mt[:], mt[:], dB[i][:, now], ALU.add).then_inc(s_s, 1)
                        if len(todo) > TC - t:
                            todo.pop(0)()
                        dve.wait_ge(s_s, 1 + k * TC + t + 1)
                        ts(H[i][:, now], mt[:], 100.0, -100.0, ALU.min, ALU.max).then_inc(s_h, 1)
                        dve.wait_ge(s_h, 1 + k * TC + t + 1)
                    for job in todo:
                        job()
                    if i:
                        nc.vector.tensor_copy(carry[:], H[1][:, (TC - 1) * W_:TC * W_]).then_inc(s_a, 1)
                        dve.wait_ge(s_a, 1 + k2 + 6)


def build_ssm_output(nc, y, xi_d, sz_d, vec, w_out, ident_d, x1_d, ffn_d, out):
    with ExitStack() as ctx:
        def sb(name, shape):
            return ctx.enter_context(nc.sbuf_tensor(name, shape, F32))

        sems = []

        def sem(name):
            sems.append(ctx.enter_context(nc.semaphore(name)))
            return sems[-1]

        vc = sb("o_vec", [P, NH, NV])
        wo = sb("o_wo", [P, NH, C])
        idn = sb("o_idn", [P, P])
        onesD = sb("o_ones", [P, P])
        xi = sb("o_xi", [P, NH, L])
        sz = sb("o_sz", [P, NH, L])
        ff = sb("o_ff", [P, L])
        x1 = sb("o_x1", [P, T4, C])
        yc = sb("o_yc", [P, NH, L])
        yq = sb("o_yq", [P, NH, L])
        gt = sb("o_gt", [P, NH, L])
        va, rstd, vt = sb("o_va", [P, T4]), sb("o_rstd", [P, T4]), sb("o_vt", [P, T4])
        res = sb("o_res", [P, T4, C])
        bM, bV, bR, bO = (ctx.enter_context(nc.psum_tensor(f"o_b{i}", [P, 512], F32)) for i in range(4))
        s_c, s_ld, s_ini, s_mean, s_yc, s_yq, s_var, s_va, s_rs, s_rb, s_n, s_g, s_o, s_res, s_out = (
            sem("o_" + n) for n in ("c", "ld", "ini", "mean", "yc", "yq", "var", "va", "rs", "rb", "n", "g", "o", "res", "out"))
        block = ctx.enter_context(nc.Block())

        @block.sync
        def _(sp):
            start_at_one(sp, sems)
            sp.dma_start(vc[:], vec).then_inc(s_c, 16)
            sp.dma_start(wo[:], w_out).then_inc(s_c, 16)
            sp.dma_start(idn[:], ident_d).then_inc(s_c, 16)
            with sp.Fori(0, B) as b:
                sp.wait_ge(s_res, 1 + b)
                sp.dma_start(xi[:].rearrange("p h t -> p (h t)"), xi_d[bass.ds(b, 1)].rearrange("a p n -> p (a n)")).then_inc(s_ld, 16)
                sp.dma_start(sz[:].rearrange("p h t -> p (h t)"), sz_d[bass.ds(b, 1)].rearrange("a p n -> p (a n)")).then_inc(s_ld, 16)
                sp.dma_start(ff[:], ffn_d[:, bass.ds(b * L, L)]).then_inc(s_ld, 16)
                sp.dma_start(x1[:], x1_d[bass.ds(b, 1)].rearrange("a (t p) c -> p (a t) c", p=P)).then_inc(s_ld, 16)
                sp.wait_ge(s_res, 1 + b + 1)
                sp.dma_start(out[bass.ds(b, 1)].rearrange("a (t p) c -> p (a t) c", p=P), res[:]).then_inc(s_out, 16)
            sp.wait_ge(s_out, 1 + B * 16)

        @block.gpsimd
        def _(pool):
            nc.gpsimd.memset(onesD[:], 1.0 / DIN).then_inc(s_ini, 1)

        @block.tensor
        def _(pe):
            mul = nc.tensor.matmul
            pe.wait_ge(s_c, 1 + 48)
            pe.wait_ge(s_ini, 1 + 1)
            with pe.Fori(0, B) as b:
                pe.wait_ge(s_yc, 1 + b * 2)
                for h in range(NH):
                    w = mul(bM[:], onesD[:], y[:, bass.ds(b + h * B, 1)].rearrange("p a t -> p (a t)"), start=h == 0, stop=h == NH - 1)
                w.then_inc(s_mean, 1)
                pe.wait_ge(s_yq, 1 + (b + 1) * 2)
                for t in range(T4):
                    for h in range(NH):
                        w = mul(bV[:, t:t + 1], yq[:, h, t * P:(t + 1) * P], onesD[:, 0:1], start=h == 0, stop=h == NH - 1)
                w.then_inc(s_var, 1)
                pe.wait_ge(s_rs, 1 + (b + 1) * RSQRT_STEPS)
                for t in range(T4):
                    w = mul(bR[:, t * P:(t + 1) * P], rstd[:, t:t + 1].broadcast_to([P, P]), idn[:], start=True, stop=True)
                w.then_inc(s_rb, 1)
                pe.wait_ge(s_g, 1 + (b + 1) * 2)
                pe.wait_ge(s_ld, 1 + (b + 1) * 64)
                for t in range(T4):
                    q = slice(t * P, (t + 1) * P)
                    mul(bO[:, q], ff[:, q], idn[:], start=True, stop=False)
                    for h in range(NH):
                        w = mul(bO[:, q], gt[:, h, q], wo[:, h], start=False, stop=h == NH - 1)
                w.then_inc(s_o, 1)

        @block.scalar
        def _(act):
            with act.Fori(0, B) as b:
                for h in range(NH):
                    act.wait_ge(s_yc, 1 + b * 2 + h + 1)
                    nc.scalar.activation(yq[:, h], yc[:, h], ACT.Square).then_inc(s_yq, 1)

        @block.vector
        def _(dve):
            tt, ts, stt = nc.vector.tensor_tensor, nc.vector.tensor_scalar, nc.vector.scalar_tensor_tensor
            dve.wait_ge(s_c, 1 + 48)
            with dve.Fori(0, B) as b:
                dve.wait_ge(s_mean, 1 + b + 1)
                for h in range(NH):
                    tt(yc[:, h], y[:, bass.ds(b + h * B, 1)].rearrange("p a t -> p (a t)"), bM[:], ALU.subtract).then_inc(s_yc, 1)
                dve.wait_ge(s_var, 1 + b + 1)
                ts(va[:], bV[:, 0:T4], 1e-5, None, ALU.add).then_inc(s_va, 1)
                dve.wait_ge(s_va, 1 + b + 1)
                rsqrt(nc, dve, s_rs, b * RSQRT_STEPS, va[:], rstd[:], vt[:])
                dve.wait_ge(s_rb, 1 + b + 1)
                dve.wait_ge(s_ld, 1 + (b + 1) * 64)
                dve.wait_ge(s_o, 1 + b)
                for h in range(NH):
                    tt(yc[:, h], yc[:, h], bR[:], ALU.mult).then_inc(s_n, 1)
                for h in range(NH):
                    dve.wait_ge(s_n, 1 + b * 6 + h + 1)
                    ts(yc[:, h], yc[:, h], vc[:, h, LNW2:LNW2 + 1], vc[:, h, LNB2:LNB2 + 1], ALU.mult, ALU.add).then_inc(s_n, 1)
                for h in range(NH):
                    dve.wait_ge(s_n, 1 + b * 6 + h + 3)
                    stt(yc[:, h], xi[:, h], vc[:, h, DPAR:DPAR + 1], yc[:, h], ALU.mult, ALU.add).then_inc(s_n, 1)
                for h in range(NH):
                    dve.wait_ge(s_n, 1 + b * 6 + h + 5)
                    tt(gt[:, h], yc[:, h], sz[:, h], ALU.mult).then_inc(s_g, 1)
                dve.wait_ge(s_o, 1 + b + 1)
                dve.wait_ge(s_out, 1 + b * 16)
                tt(res[:].rearrange("p t c -> p (t c)"), bO[:], x1[:].rearrange("p t c -> p (t c)"), ALU.add).then_inc(s_res, 1)


def pack_ssm(d):
    def halves(v):
        return v.reshape(NH, P, -1).transpose(1, 0, 2)
    vec = np.concatenate([halves(d["L1_attn_" + n]) for n in ("conv_w", "conv_b", "b_dt", "D_param", "ln_w", "ln_b")], -1)
    wx = d["L1_attn_W_x"]
    wx = np.concatenate([wx[1:], wx[0:1]], 0).T.reshape(NH, P, 33).transpose(1, 0, 2)
    return {"w_in": d["L1_attn_W_in"].T, "w_x": wx, "w_dt": d["L1_attn_W_dt"].T, "vec": vec,
            "alog": np.tile(d["L1_attn_A_log"][None], (P, 1)), "w_out": d["L1_attn_W_out"].T.reshape(NH, P, C).transpose(1, 0, 2)}


H0, D0 = 16, C // 16
E, EM, EI, KC = 8, 4, 64, 4
PAIRS = EM * EI // P
G0 = H0 // HG
SC0 = float(1.0 / np.sqrt(np.float32(D0)))
VCH = 51


def build_layer0(nc, x_d, wqk, bqk, wv, bvr, wo, rows, wr, rbias, tri, wg, wu, wd, cw_d, sel_d, ident_d, x1_d, xn1_d):
    with ExitStack() as ctx:
        def sb(name, shape):
            return ctx.enter_context(nc.sbuf_tensor("a_" + name, shape, F32))

        sems = []

        def sem(name):
            sems.append(ctx.enter_context(nc.semaphore("a_" + name)))
            return sems[-1]

        Wqk, Bqk = sb("Wqk", [P, 2 * G0, P]), sb("Bqk", [P, 2 * G0])
        Wv, Bv, Wo = sb("Wv", [P, C]), sb("Bv", [P, C]), sb("Wo", [P, C])
        row2 = sb("row2", [2, C])
        Wr, Rb, Tri = sb("Wr", [P, E]), sb("Rb", [P, E]), sb("Tri", [P, E * E])
        Wg, Wu, Wd = sb("Wg", [P, EM * EI]), sb("Wu", [P, EM * EI]), sb("Wd", [P, PAIRS, C])
        cw = sb("cw", [P, KC])
        sel = sb("sel", [E, PAIRS, P])
        idn = sb("idn", [P, P])
        ones2 = sb("ones2", [2, P])
        diag = sb("diag", [P, KC, P])
        x = sb("x", [P, T4, C])
        xn = sb("xn", [P, T4, C])
        xnT = sb("xnT", [P, KC - 1 + L])
        pad = sb("pad", [P, 1])
        st6 = sb("st6", [P, T4, 6])
        mv = sb("mv", [P, T4, 2])
        va, rstd, vt = sb("va", [P, T4]), sb("rstd", [P, T4]), sb("vt", [P, T4])
        qk = sb("qk", [P, 2 * G0, L])
        V = sb("V", [P, T4, C])
        Pe = sb("Pe", [P, 2, H0, P])
        mx, nm, su = sb("mx", [P, 2, H0]), sb("nm", [P, 2, H0]), sb("su", [P, 2, H0])
        rc = sb("rc", [P, 2, H0])
        PT = sb("PT", [P, 2, HG, P])
        O = sb("O", [P, 2, C])
        OT = sb("OT", [P, L])
        ex, sg, sbi = sb("ex", [P, T4 * E]), sb("sg", [P, T4 * E]), sb("sbi", [P, T4 * E])
        c1, c2 = sb("c1", [P, T4 * E * E]), sb("c2", [P, T4 * E * E])
        rk, cwt = sb("rk", [P, T4 * E]), sb("cwt", [P, T4 * E])
        ws, aw = sb("ws", [P, T4]), sb("aw", [P, T4])
        cwT = sb("cwT", [E, L])
        gs = sb("gs", [P, PAIRS, L])
        hid = sb("hid", [P, PAIRS, L])
        idt = sb("idt", [P, T4, C])
        x1 = sb("x1", [P, T4, C])
        xn1T = sb("xn1T", [P, L])
        K4 = [ctx.enter_context(nc.psum_tensor(f"a_pK{i}", [P, 512], F32)) for i in range(4)]
        bT = [ctx.enter_context(nc.psum_tensor(f"a_pT{i}", [P, 512], F32)) for i in range(2)]
        bO = ctx.enter_context(nc.psum_tensor("a_pO", [P, 512], F32))
        bA = ctx.enter_context(nc.psum_tensor("a_pA", [P, 512], F32))

        s_c, s_ini, s_x, s_st = sem("c"), sem("ini"), sem("x"), sem("st")
        s_v = sem("chain")
        s_xn, s_xnp, s_xnT = sem("xn"), sem("xnp"), sem("xnT")
        s_qp, s_qk, s_vp, s_V = sem("qp"), sem("qk"), sem("vp"), sem("V")
        s_rp, s_ex = sem("rp"), sem("ex")
        s_cw, s_cwp, s_cwT, s_cb = sem("cw"), sem("cwp"), sem("cwT"), sem("cb")
        s_s, s_nm, s_exp = sem("s"), sem("nm"), sem("exp")
        s_pt, s_pte, s_pv, s_O, s_op, s_OT = sem("pt"), sem("pte"), sem("pv"), sem("O"), sem("op"), sem("OT")
        s_gu, s_gs, s_hid, s_acc, s_x1 = sem("gu"), sem("gs"), sem("hid"), sem("acc"), sem("x1")
        s_xn1, s_x1p, s_x1T = sem("xn1"), sem("x1p"), sem("x1T")
        block = ctx.enter_context(nc.Block())
        NG = T4 * G0

        @block.sync
        def _(sp):
            start_at_one(sp, sems)
            for dst, src in ((idn, ident_d), (Wqk, wqk), (Bqk, bqk), (Wv, wv), (Bv, bvr), (Wo, wo), (row2, rows),
                             (Wr, wr), (Rb, rbias), (Tri, tri), (Wg, wg), (Wu, wu), (Wd, wd), (cw, cw_d), (sel, sel_d)):
                sp.dma_start(dst[:], src).then_inc(s_c, 16)
            with sp.Fori(0, B) as b:
                sp.wait_ge(s_x1, 1 + b)
                sp.dma_start(x[:], x_d[bass.ds(b, 1)].rearrange("a (t p) c -> p (a t) c", p=P)).then_inc(s_x, 16)
                sp.wait_ge(s_x1, 1 + b + 1)
                sp.dma_start(x1_d[bass.ds(b, 1)].rearrange("a (t p) c -> p (a t) c", p=P), x1[:]).then_inc(s_st, 16)
                sp.wait_ge(s_x1T, 1 + b + 1)
                sp.dma_start(xn1_d[:, bass.ds(b * L, L)], xn1T[:]).then_inc(s_st, 16)
            sp.wait_ge(s_st, 1 + B * 32)

        CONSTS = 15 * 16

        @block.gpsimd
        def _(pool):
            nc.gpsimd.memset(xnT[:], 0.0).then_inc(s_ini, 1)
            nc.gpsimd.memset(ones2[:], 1.0).then_inc(s_ini, 1)

        @block.tensor
        def _(pe):
            mul, turn = nc.tensor.matmul, nc.tensor.transpose
            pe.wait_ge(s_c, 1 + CONSTS)
            pe.wait_ge(s_ini, 1 + 2 + KC)
            with pe.Fori(0, B) as b:
                pe.wait_ge(s_xn, 1 + b + 1)
                for t in range(T4):
                    w = turn(bT[0][:, t * P:(t + 1) * P], xn[:, t], idn[:])
                w.then_inc(s_xnp, 1)
                pe.wait_ge(s_xnT, 1 + b + 1)
                xm = xnT[:, KC - 1:KC - 1 + L]
                for g in range(2 * G0):
                    if g >= 4:
                        pe.wait_ge(s_qk, 1 + b * 2 * G0 + g - 3)
                    mul(K4[g % 4][:], Wqk[:, g], xm, start=True, stop=True).then_inc(s_qp, 1)
                for t in range(T4):
                    w = mul(bT[1][:, t * P:(t + 1) * P], xnT[:, KC - 1 + t * P:KC - 1 + (t + 1) * P], Wv[:], start=True, stop=True)
                w.then_inc(s_vp, 1)
                for t in range(T4):
                    w = mul(bO[:, t * E:(t + 1) * E], xnT[:, KC - 1 + t * P:KC - 1 + (t + 1) * P], Wr[:], start=True, stop=True)
                w.then_inc(s_rp, 1)
                pe.wait_ge(s_qk, 1 + (b + 1) * 2 * G0)
                pe.wait_ge(s_ex, 1 + b + 1)
                pe.wait_ge(s_V, 1 + b + 1)

                def scores(t):
                    if t:
                        pe.wait_ge(s_exp, 1 + (b * T4 + t) * H0)
                    for g in range(G0):
                        for h in range(HG):
                            r = slice(32 * h, 32 * h + 32)
                            w = mul(K4[h][:, g * P:(g + 1) * P], qk[r, g, t * P:(t + 1) * P],
                                    qk[r, G0 + g, t * P:(t + 1) * P], start=True, stop=True, tile_position=(32 * h, 0))
                    w.then_inc(s_s, 1)

                def turn_weights(t, g):
                    n = t * G0 + g
                    if g == 0:
                        pe.wait_ge(s_exp, 1 + (b * T4 + t + 1) * H0)
                    if n >= 2:
                        pe.wait_ge(s_pte, 1 + b * NG + n - 1)
                    for h in range(HG):
                        w = turn(bT[n % 2][:, h * P:(h + 1) * P], Pe[:, t % 2, h * G0 + g], idn[:])
                    w.then_inc(s_pt, 1)

                def mix(t, g):
                    n = t * G0 + g
                    pe.wait_ge(s_pte, 1 + b * NG + n + 1)
                    if g == 0 and t:
                        pe.wait_ge(s_O, 1 + b * T4 + t)
                    for h in range(HG):
                        hh = g * HG + h
                        w = mul(bO[:, hh * D0:(hh + 1) * D0], PT[:, n % 2, h], V[:, t, hh * D0:(hh + 1) * D0], start=True, stop=True)
                    w.then_inc(s_pv, 1)

                def turn_out(t):
                    pe.wait_ge(s_O, 1 + b * T4 + t + 1)
                    turn(bA[:, t * P:(t + 1) * P], O[:, t % 2], idn[:]).then_inc(s_op, 1)

                for t in range(T4 + 1):
                    if t < T4:
                        scores(t)
                    if t:
                        for g in range(G0):
                            turn_weights(t - 1, g)
                            if g:
                                mix(t - 1, g - 1)
                            elif t >= 2:
                                turn_out(t - 2)
                        mix(t - 1, G0 - 1)
                pe.wait_ge(s_cw, 1 + b + 1)
                for t in range(T4):
                    w = turn(bT[0][0:E, t * P:(t + 1) * P], cwt[:, t * E:(t + 1) * E], idn[:])
                w.then_inc(s_cwp, 1)
                for m in range(PAIRS):
                    mul(K4[2 * m][:], Wg[:, m * P:(m + 1) * P], xm, start=True, stop=True)
                    mul(K4[2 * m + 1][:], Wu[:, m * P:(m + 1) * P], xm, start=True, stop=True).then_inc(s_gu, 1)
                turn_out(T4 - 1)
                pe.wait_ge(s_cwT, 1 + b + 1)
                for m in range(PAIRS):
                    mul(bT[m][:], sel[:, m], cwT[:], start=True, stop=True).then_inc(s_cb, 1)
                pe.wait_ge(s_OT, 1 + b + 1)
                pe.wait_ge(s_hid, 1 + (b + 1) * PAIRS * 2)
                for t in range(T4):
                    o, q = bA[:, t * P:(t + 1) * P], slice(t * P, (t + 1) * P)
                    for k in range(KC):
                        mul(o, xnT[:, k + t * P:k + (t + 1) * P], diag[:, k], start=k == 0, stop=False)
                    mul(o, ones2[:], row2[:], start=False, stop=False)
                    mul(o, OT[:, q], Wo[:], start=False, stop=False)
                    for m in range(PAIRS):
                        w = mul(o, hid[:, m, q], Wd[:, m], start=False, stop=m == PAIRS - 1)
                w.then_inc(s_acc, 1)
                pe.wait_ge(s_xn1, 1 + b + 1)
                for t in range(T4):
                    w = turn(bO[:, t * P:(t + 1) * P], xn[:, t], idn[:])
                w.then_inc(s_x1p, 1)

        @block.scalar
        def _(act):
            f = nc.scalar.activation
            act.wait_ge(s_c, 1 + CONSTS)
            act.wait_ge(s_ini, 1 + 2)
            with act.Fori(0, B) as b:
                act.wait_ge(s_xnp, 1 + b + 1)
                f(xnT[:, KC - 1:KC - 1 + L], bT[0][:], ACT.Copy).then_inc(s_xnT, 1)
                for g in range(2 * G0):
                    act.wait_ge(s_qp, 1 + b * 2 * G0 + g + 1)
                    f(qk[:, g], K4[g % 4][:], ACT.Identity, bias=Bqk[:, g:g + 1]).then_inc(s_qk, 1)
                act.wait_ge(s_rp, 1 + b + 1)
                f(ex[:], bO[:, 0:T4 * E], ACT.Exp, scale=-1.0).then_inc(s_ex, 1)

                def exps(t):
                    act.wait_ge(s_nm, 1 + b * T4 + t + 1)
                    if t >= 2:
                        act.wait_ge(s_pt, 1 + b * NG + (t - 1) * G0)
                    for i in range(H0):
                        f(Pe[:, t % 2, i], K4[i // G0][:, (i % G0) * P:(i % G0 + 1) * P], ACT.Exp,
                          bias=nm[:, t % 2, i:i + 1], scale=SC0, accum_out=su[:, t % 2, i:i + 1]).then_inc(s_exp, 1)

                for t in range(T4):
                    exps(t)
                for m in range(PAIRS):
                    act.wait_ge(s_gu, 1 + b * PAIRS + m + 1)
                    f(gs[:, m], K4[2 * m][:], ACT.Silu).then_inc(s_gs, 1)
                act.wait_ge(s_op, 1 + (b + 1) * T4)
                f(OT[:], bA[:], ACT.Copy).then_inc(s_OT, 1)
                act.wait_ge(s_x1p, 1 + b + 1)
                act.wait_ge(s_st, 1 + b * 32)
                f(xn1T[:], bO[:], ACT.Copy).then_inc(s_x1T, 1)

        @block.vector
        def _(dve):
            tt, ts, stt = nc.vector.tensor_tensor, nc.vector.tensor_scalar, nc.vector.scalar_tensor_tensor
            red = nc.vector.tensor_reduce
            dve.wait_ge(s_c, 1 + CONSTS)
            dve.wait_ge(s_ini, 1 + 2)
            for k in range(KC):
                ts(diag[:, k], idn[:], cw[:, k:k + 1], None, ALU.mult).then_inc(s_ini, 1)
            with dve.Fori(0, B) as b:
                n = [0]

                def link(ins):
                    n[0] += 1
                    ins.then_inc(s_v, 1)
                    dve.wait_ge(s_v, 1 + b * VCH + n[0])

                def norm(src):
                    for t in range(T4):
                        ins = nc.vector.bn_stats(st6[:, t], src[:, t])
                    link(ins)
                    nc.vector.memset(pad[:], 0.0)
                    for t in range(T4):
                        ins = nc.vector.bn_aggr(mv[:, t], st6[:, t])
                    link(ins)
                    link(ts(va[:], mv[:, :, 1], 1e-5, None, ALU.add))
                    base = b * VCH + n[0]
                    rsqrt(nc, dve, s_v, base, va[:], rstd[:], vt[:])
                    n[0] += RSQRT_STEPS
                    for t in range(T4):
                        ins = ts(xn[:, t], src[:, t], mv[:, t, 0:1], rstd[:, t:t + 1], ALU.subtract, ALU.mult)
                    return ins

                dve.wait_ge(s_x, 1 + (b + 1) * 16)
                dve.wait_ge(s_x1p, 1 + b)
                norm(x).then_inc(s_xn, 1)
                dve.wait_ge(s_vp, 1 + b + 1)
                tt(V[:], bT[1][:].rearrange("p (t c) -> p t c", t=T4), Bv[:].unsqueeze(1).broadcast_to([P, T4, C]), ALU.add)\
                    .then_inc(s_V, 1)
                dve.wait_ge(s_ex, 1 + b + 1)
                ev = [P, T4, E]
                eev = [P, T4, E, E]
                te = lambda a: a.rearrange("p (t e) -> p t e", t=T4)
                tef = lambda a: a.rearrange("p (t e f) -> p t e f", t=T4, e=E)
                link(ts(ex[:], ex[:], 1.0, None, ALU.add))
                link(nc.vector.reciprocal(sg[:], ex[:]))
                link(tt(te(sbi[:]), te(sg[:]), Rb[:].unsqueeze(1).broadcast_to(ev), ALU.add))
                mine = te(sbi[:]).unsqueeze(3).broadcast_to(eev)
                other = te(sbi[:]).unsqueeze(2).broadcast_to(eev)
                tt(tef(c1[:]), other, mine, ALU.is_gt)
                link(tt(tef(c2[:]), other, mine, ALU.is_equal))
                link(tt(c2[:].rearrange("p (t e) -> p t e", t=T4), c2[:].rearrange("p (t e) -> p t e", t=T4),
                        Tri[:].unsqueeze(1).broadcast_to([P, T4, E * E]), ALU.mult))
                link(tt(c1[:], c1[:], c2[:], ALU.add))
                link(red(te(rk[:]), tef(c1[:]), AX, ALU.add))
                link(stt(cwt[:], rk[:], 1.5, sg[:], ALU.is_lt, ALU.mult))
                link(red(ws[:], te(cwt[:]), AX, ALU.add))
                link(ts(ws[:], ws[:], 1e-9, None, ALU.add))
                link(nc.vector.reciprocal(aw[:], ws[:]))
                ins = tt(te(cwt[:]), te(cwt[:]), aw[:].unsqueeze(2).broadcast_to(ev), ALU.mult)
                ins.then_inc(s_cw, 1)
                dve.wait_ge(s_cw, 1 + b + 1)
                link(tt(aw[:], te(cwt[:])[:, :, 4], te(cwt[:])[:, :, 6], ALU.add))
                for t in range(T4):
                    ins = ts(idt[:, t], xn[:, t], 0.0, cwt[:, t * E + 7:t * E + 8], ALU.max, ALU.mult)
                link(ins)
                for t in range(T4):
                    ins = stt(idt[:, t], xn[:, t], aw[:, t:t + 1], idt[:, t], ALU.mult, ALU.add)
                link(ins)
                link(tt(idt[:], idt[:], x[:], ALU.add))

                def maxima(t):
                    dve.wait_ge(s_s, 1 + b * T4 + t + 1)
                    for h in range(HG):
                        ins = red(mx[:, t % 2, h * G0:(h + 1) * G0], K4[h][:].rearrange("p (g j) -> p g j", g=G0), AX, ALU.max)
                    link(ins)
                    if t >= 2:
                        dve.wait_ge(s_exp, 1 + (b * T4 + t - 1) * H0)
                    ts(nm[:, t % 2], mx[:, t % 2], -SC0, None, ALU.mult).then_inc(s_nm, 1)

                def evacuate(t, g):
                    m = t * G0 + g
                    dve.wait_ge(s_pt, 1 + b * NG + m + 1)
                    if m >= 2:
                        dve.wait_ge(s_pv, 1 + b * NG + m - 1)
                    nc.vector.tensor_copy(PT[:, m % 2].rearrange("p h j -> p (h j)"), bT[m % 2][:]).then_inc(s_pte, 1)

                def normalise(t):
                    dve.wait_ge(s_exp, 1 + (b * T4 + t + 1) * H0)
                    link(nc.vector.reciprocal(rc[:, t % 2], su[:, t % 2]))
                    dve.wait_ge(s_pv, 1 + b * NG + (t + 1) * G0)
                    if t >= 2:
                        dve.wait_ge(s_op, 1 + b * T4 + t - 1)
                    tt(O[:, t % 2].rearrange("p (g h d) -> p g h d", g=G0, h=HG),
                       bO[:, 0:C].rearrange("p (g h d) -> p g h d", g=G0, h=HG),
                       rc[:, t % 2].rearrange("p (h g) -> p g h", h=HG).unsqueeze(3).broadcast_to([P, G0, HG, D0]),
                       ALU.mult).then_inc(s_O, 1)

                for t in range(T4 + 1):
                    if t < T4:
                        maxima(t)
                    if t:
                        for g in range(G0):
                            evacuate(t - 1, g)
                        normalise(t - 1)
                dve.wait_ge(s_cwp, 1 + b + 1)
                nc.vector.tensor_copy(cwT[:], bT[0][0:E, :]).then_inc(s_cwT, 1)
                for m in range(PAIRS):
                    dve.wait_ge(s_gs, 1 + b * PAIRS + m + 1)
                    tt(hid[:, m], K4[2 * m + 1][:], gs[:, m], ALU.mult).then_inc(s_hid, 1)
                for m in range(PAIRS):
                    dve.wait_ge(s_cb, 1 + b * PAIRS + m + 1)
                    dve.wait_ge(s_hid, 1 + b * 2 * PAIRS + m + 1)
                    tt(hid[:, m], hid[:, m], bT[m][:], ALU.mult).then_inc(s_hid, 1)
                dve.wait_ge(s_acc, 1 + b + 1)
                dve.wait_ge(s_st, 1 + b * 32)
                tt(x1[:].rearrange("p t c -> p (t c)"), bA[:], idt[:].rearrange("p t c -> p (t c)"), ALU.add).then_inc(s_x1, 1)
                dve.wait_ge(s_x1, 1 + b + 1)
                norm(x1).then_inc(s_xn1, 1)
                assert n[0] == VCH


def pack_layer0(d):
    def heads(w):
        out = np.zeros((w.shape[0], G0, HG, 32), np.float32)
        out[..., 0:D0] = w.reshape(w.shape[0], G0, HG, D0)
        return out.reshape(w.shape[0], G0, P)
    g = lambda n: d["L0_" + n]
    bqk = np.concatenate([heads(g("attn_bq")[None]), heads(g("attn_bk")[None])], 1)
    sel = np.zeros((E, PAIRS, P), np.float32)
    for e in range(EM):
        sel[e, e // 2, (e % 2) * EI:(e % 2 + 1) * EI] = 1.0
    return {"w0_wqk": np.concatenate([heads(g("attn_Wq")), heads(g("attn_Wk"))], 1), "w0_bqk": bqk[0].T,
            "w0_wv": g("attn_Wv"), "w0_bv": np.tile(g("attn_bv"), (P, 1)), "w0_wo": g("attn_Wo"),
            "w0_rows": np.stack([g("attn_bo"), g("ffn_conv_b")]), "w0_wr": g("ffn_Wr"),
            "w0_rb": np.tile(g("ffn_router_bias"), (P, 1)),
            "w0_tri": np.tile(np.tril(np.ones((E, E), np.float32), -1).reshape(1, -1), (P, 1)),
            "w0_wg": g("ffn_Wg").transpose(1, 0, 2).reshape(C, -1), "w0_wu": g("ffn_Wu").transpose(1, 0, 2).reshape(C, -1),
            "w0_wd": g("ffn_Wd").reshape(PAIRS, P, C).transpose(1, 0, 2), "w0_cw": g("ffn_conv_w")[:, 0].T, "w0_sel": sel}


def constants():
    return {"ident": np.eye(P, dtype=np.float32), "tabs": rotary_constants(), "masks": band_masks(),
            "blocks": head_blocks(), "spread": spreads()}


def build(nc, a, out):
    x1_d = nc.dram_tensor("x1_d", [B, L, C], F32, kind="Internal").ap()
    xn1_d = nc.dram_tensor("xn1_d", [C, B * L], F32, kind="Internal").ap()
    ffn_d = nc.dram_tensor("ffn_d", [C, B * L], F32, kind="Internal").ap()
    xi_d = nc.dram_tensor("xi_d", [B, P, NH * L], F32, kind="Internal").ap()
    sz_d = nc.dram_tensor("sz_d", [B, P, NH * L], F32, kind="Internal").ap()
    build_layer0(nc, a["x"], *(a["w0_" + n] for n in ("wqk", "bqk", "wv", "bv", "wo", "rows", "wr", "rb", "tri", "wg",
                                                      "wu", "wd", "cw", "sel")), a["ident"], x1_d, xn1_d)
    build_local(nc, xn1_d, ffn_d, *(a[n] for n in ("tabs", "masks", "blocks", "spread", "f_wqk", "f_wv", "f_wo", "f_w1",
                                                   "f_w2", "f_small")), a["ident"])
    with nc.sbuf_tensor("ssm_dt", [P, HB, L], F32) as dt, nc.sbuf_tensor("ssm_u", [P, HB, L], F32) as u:
        with nc.sbuf_tensor("ssm_bc", [P, L, B], F32) as bc:
            build_ssm_inputs(nc, xn1_d, a["w_in"], a["w_x"], a["w_dt"], a["vec"], dt, u, bc, xi_d, sz_d)
            build_ssm_scan(nc, a["alog"], a["ident"], dt, u, bc)
        build_ssm_output(nc, u, xi_d, sz_d, a["vec"], a["w_out"], a["ident"], x1_d, ffn_d, out)


def pack(d):
    wqk, wv, small = pack_local(d)
    return {"x": d["L0_attn_x"], **constants(), **pack_layer0(d), **pack_ssm(d), "f_wqk": wqk, "f_wv": wv,
            "f_small": small, "f_wo": d["L1_ffn_Wo"], "f_w1": d["L1_ffn_W1"], "f_w2": d["L1_ffn_W2"]}


def kernel(**inputs):
    import concourse.bacc as bacc
    from concourse.bass_utils import run_bass_kernel_spmd

    arrays = {n: np.ascontiguousarray(v) for n, v in pack({n: np.asarray(v) for n, v in inputs.items()}).items()}
    nc = bacc.Bacc("TRN2", target_bir_lowering=False, num_devices=1)
    a = {n: nc.dram_tensor(n, v.shape, F32, kind="ExternalInput").ap() for n, v in arrays.items()}
    out = nc.dram_tensor("out", [B, L, C], F32, kind="ExternalOutput").ap()
    build(nc, a, out)
    return run_bass_kernel_spmd(nc, [arrays], core_ids=[0]).results[0]["out"]
```

```python
import numpy as np
from contextlib import ExitStack

import concourse.bass as bass
from concourse import mybir

F32 = mybir.dt.float32
ALU = mybir.AluOpType
ACT = mybir.ActivationFunctionType
AX = mybir.AxisListType.X

P = 128
C = 128
B, L = 8, 512
T4 = L // P


def start_at_one(eng, sems):
    for s in sems:
        eng.sem_inc(s, 1)


DEPTH = 6
HEADS, DH = 16, 64
INNER = HEADS * DH
HALF = DH // 2
HG = P // HALF
GROUPS = HEADS // HG
WINDOW = 32
DI = int(C * 4 * 2 / 3)
HM = [P, P, DI - 2 * P]
QK_SCALE = 8.0
BIG = 1e30
UW = HG * DH
TW = 4 * DH
NR = T4 * 2 * HG
LNG, LNB, B2C, B1A, B1G = 0, 1, 2, 3, 6
NSMALL = 9


def rotary_constants():
    half = np.arange(0, DH, 2, dtype=np.float32)
    inv = (np.float32(1.0) / np.float32(10000.0) ** (half / np.float32(DH))).astype(np.float32)
    t = np.arange(L, dtype=np.float32)
    fr = t[:, None] * inv[None, :]
    base = (half + np.float32(0.4 * DH)) / np.float32(1.4 * DH)
    power = (t - L // 2) / np.float32(WINDOW // 2)
    sc = base[None, :].astype(np.float32) ** power[:, None].astype(np.float32)
    c, s = np.cos(fr), np.sin(fr)
    tabs = np.concatenate([c * sc, c * sc, c / sc, c / sc, -s * sc, s * sc, -s / sc, s / sc], 1).astype(np.float32)
    return np.ascontiguousarray(tabs.reshape(T4, P, TW).transpose(1, 0, 2))


def band_masks():
    i, j = np.arange(P)[:, None], np.arange(P)[None, :]
    own = (j <= i) & (j >= i - WINDOW)
    before = (i < WINDOW) & (j >= P - WINDOW) & (j - (P - WINDOW) >= i)
    m = np.stack([own, own | before], 1)
    return np.where(m, 0.0, -BIG).astype(np.float32)


RSQRT_STEPS = 11


def rsqrt(nc, eng, sem, base, x, y, t):
    ts, stt = nc.vector.tensor_scalar, nc.vector.scalar_tensor_tensor
    xi, yi, ti = x.bitcast(mybir.dt.int32), y.bitcast(mybir.dt.int32), t.bitcast(mybir.dt.int32)
    ts(ti, xi, 1, None, ALU.logical_shift_right).then_inc(sem, 1)
    eng.wait_ge(sem, 1 + base + 1)
    ts(yi, ti, -1.0, float(0x5F3759DF), ALU.mult, ALU.add).then_inc(sem, 1)
    for k in range(3):
        eng.wait_ge(sem, 1 + base + 2 + 3 * k)
        nc.vector.tensor_tensor(t, y, y, ALU.mult).then_inc(sem, 1)
        eng.wait_ge(sem, 1 + base + 3 + 3 * k)
        stt(t, x, -0.5, t, ALU.mult, ALU.mult).then_inc(sem, 1)
        eng.wait_ge(sem, 1 + base + 4 + 3 * k)
        stt(y, t, 1.5, y, ALU.add, ALU.mult).then_inc(sem, 1)
    eng.wait_ge(sem, 1 + base + RSQRT_STEPS)


NEWTON = 15


def root_guess(nc, dve, sem, base, y, x, t):
    xi, yi, ti = x.bitcast(mybir.dt.int32), y.bitcast(mybir.dt.int32), t.bitcast(mybir.dt.int32)
    dve.wait_ge(sem, 1 + base + 1)
    nc.vector.tensor_scalar(ti, xi, 1, None, ALU.logical_shift_right).then_inc(sem, 1)
    dve.wait_ge(sem, 1 + base + 2)
    nc.vector.tensor_scalar(yi, ti, -1.0, float(0x5F3759DF - 0x400000), ALU.mult, ALU.add).then_inc(sem, 1)


def root_newton(nc, pool, sem, base, y, x, t, c15):
    tt = nc.gpsimd.tensor_tensor
    for k in range(3):
        pool.wait_ge(sem, 1 + base + 3 + 4 * k)
        tt(t, y, y, ALU.mult).then_inc(sem, 1)
        pool.wait_ge(sem, 1 + base + 4 + 4 * k)
        tt(t, t, x, ALU.mult).then_inc(sem, 1)
        pool.wait_ge(sem, 1 + base + 5 + 4 * k)
        tt(t, c15, t, ALU.subtract).then_inc(sem, 1)
        pool.wait_ge(sem, 1 + base + 6 + 4 * k)
        tt(y, y, t, ALU.mult).then_inc(sem, 1)


def build_local(nc, xin, xout, tabs, masks, wqk, wv, wo, w1, w2, scales, small, ident_d,
                depth=DEPTH, nb=B):
    assert nb >= 3
    total = depth * nb
    NS = GROUPS * T4
    with ExitStack() as ctx:
        def sb(name, shape):
            return ctx.enter_context(nc.sbuf_tensor(name, shape, F32))

        def ps(name, shape=(P, 512)):
            return ctx.enter_context(nc.psum_tensor(name, list(shape), F32))

        sems = []

        def sem(name):
            sems.append(ctx.enter_context(nc.semaphore(name)))
            return sems[-1]

        xT = sb("xT", [P, nb * L])
        xs = sb("xs", [P, L])
        xf = sb("xf", [P, L])
        Wqk = sb("Wqk", [P, 2 * INNER])
        Wv = sb("Wv", [P, INNER])
        Wo = sb("Wo", [P, INNER // P, C])
        W1 = sb("W1", [P, 2 * DI])
        W2 = sb("W2", [P, 3, C])
        sc = sb("sc", [P, TW])
        smF = sb("smF", [P, NSMALL])
        tb = sb("tb", [P, T4, TW])
        tl = sb("tl", [P, T4, TW])
        mk = sb("mk", [P, 2, P])
        pad, padA = sb("pad", [P, 1]), sb("padA", [P, 1])
        idn = sb("idn", [P, P])
        onesC = sb("onesC", [P, P])
        sq = sb("sq", [P, 2, 2 * UW])
        sqh = sb("sqh", [P, 2, 2 * HG, HALF])
        mm = sb("mm", [P, 2, 2, 2 * UW])
        rot = sb("rot", [P, T4, 2 * UW])
        qk = sb("qk", [P, 2, 2, 2, L])
        V = sb("V", [P, 2, T4, UW])
        Vd = sb("Vd", [P, 2, T4 - 1, UW])
        ir = sb("ir", [P, 2, NR])
        ss, xr, yr, c15 = (sb(n, [P, NR]) for n in ("ss", "xr", "yr", "c15"))
        sp = sb("sp", [P, 2, HG, P])
        mx = sb("mx", [P, 2, HG])
        nm = sb("nm", [P, 2, HG])
        su = sb("su", [P, 2, HG])
        rc = sb("rc", [P, 2, HG])
        PT = sb("PT", [P, 2, HG, P])
        OT = sb("OT", [P, INNER // P, L])
        xc = sb("xc", [P, L])
        xv = sb("xv", [P, L])
        xn = sb("xn", [P, L])
        va = sb("va", [P, T4])
        rstd = sb("rstd", [P, T4])
        vt = sb("vt", [P, T4])
        ge = sb("ge", [P, 3, L])
        hd = sb("hd", [P, 3, L])

        bS = [ps("bS0"), ps("bS1")]
        bT, bO = ps("bT"), ps("bO")
        bA, bB = ps("bA"), ps("bB")
        bM, bW = ps("bM"), ps("bW")

        s_const, s_ini, s_out = sem("s_const"), sem("s_ini"), sem("s_out")
        s_wT = sem("s_wT")
        s_wA = sem("s_wA")
        s_wV = sem("s_wV")
        s_wO = sem("s_wO")
        s_wF = sem("s_wF")
        s_tab = sem("s_tab")
        s_xs = sem("s_xs")
        s_qk = sem("s_qk")
        s_sq = sem("s_sq")
        s_ha = sem("s_ha")
        s_ss = sem("s_ss")
        s_rot = sem("s_rot")
        s_rope = sem("s_rope")
        s_ir = sem("s_ir")
        s_kn = sem("s_kn")
        s_qt, s_kt = sem("s_qt"), sem("s_kt")
        s_qe, s_ke = sem("s_qe"), sem("s_ke")
        s_vp = sem("s_vp")
        s_v = sem("s_v")
        s_vd = sem("s_vd")
        s_s = [sem("s_s0"), sem("s_s1")]
        s_mx = sem("s_mx")
        s_nm = sem("s_nm")
        s_exp = sem("s_exp")
        s_rc = sem("s_rc")
        s_pn = sem("s_pn")
        s_pt = sem("s_pt")
        s_pte = sem("s_pte")
        s_pv = sem("s_pv")
        s_ot = sem("s_ot")
        s_wo = sem("s_wo")
        s_x1 = sem("s_x1")
        s_xf = sem("s_xf")
        s_mean, s_xc, s_xv, s_var = sem("s_mean"), sem("s_xc"), sem("s_xv"), sem("s_var")
        s_rf = sem("s_rf")
        s_rbb, s_xh, s_xn = sem("s_rbb"), sem("s_xh"), sem("s_xn")
        s_gate, s_val = sem("s_gate"), sem("s_val")
        s_g0 = sem("s_g0")
        s_ge = sem("s_ge")
        s_hd = sem("s_hd")
        s_w2 = sem("s_w2")
        s_res = sem("s_res")

        CONSTS, WF = 16 * 4, 16 * 4
        block = ctx.enter_context(nc.Block())

        def past(eng, s, n):
            if not isinstance(n, int) or n > 0:
                eng.wait_ge(s, 1 + n)

        def iterations(eng, steps):
            steps(-1, False, False, True)
            steps(0, False, True, True)
            if total > 2:
                with eng.Fori(1, total - 1) as it:
                    steps(it, True, True, True)
            steps(total - 1, True, True, False)
            steps(total, True, False, False)

        def prepares(n, att, nxt):
            return att if n < NS - T4 else nxt

        def begins(n, att, nxt):
            return n % T4 == T4 - 1 and (att if n < NS - T4 - 1 else nxt)

        @block.sync
        def _(sp_):
            start_at_one(sp_, sems)
            sp_.dma_start(xT[:], xin).then_inc(s_const, 16)
            sp_.dma_start(tb[:], tabs).then_inc(s_const, 16)
            sp_.dma_start(mk[:], masks).then_inc(s_const, 16)
            sp_.dma_start(idn[:], ident_d).then_inc(s_const, 16)
            with sp_.Fori(0, depth) as l:
                sp_.wait_ge(s_tab, 1 + l * nb)
                sp_.dma_start(sc[:], scales[bass.ds(l, 1)].rearrange("a p n -> p (a n)")).then_inc(s_wT, 16)
                sp_.wait_ge(s_qk, 1 + l * (nb * GROUPS * T4))
                sp_.dma_start(Wqk[:], wqk[bass.ds(l, 1)].rearrange("a p n -> p (a n)")).then_inc(s_wA, 16)
                sp_.wait_ge(s_vp, 1 + l * (nb * GROUPS * 2))
                sp_.dma_start(Wv[:], wv[bass.ds(l, 1)].rearrange("a p n -> p (a n)")).then_inc(s_wV, 16)
                sp_.wait_ge(s_wo, 1 + l * (nb * GROUPS))
                sp_.dma_start(Wo[:], wo[bass.ds(l, 1)].rearrange("a (k p) n -> p (a k) n", p=P)).then_inc(s_wO, 16)
                sp_.wait_ge(s_res, 1 + l * nb)
                sp_.dma_start(W1[:], w1[bass.ds(l, 1)].rearrange("a p n -> p (a n)")).then_inc(s_wF, 16)
                sp_.dma_start(W2[:, 0:2, :], w2[bass.ds(l, 1), 0:2 * P].rearrange("a (k p) n -> p (a k) n", p=P)).then_inc(s_wF, 16)
                sp_.dma_start(W2[0:HM[2], 2, :], w2[bass.ds(l, 1), 2 * P:DI].rearrange("a p n -> p (a n)")).then_inc(s_wF, 16)
                sp_.dma_start(smF[:], small[bass.ds(l, 1)].rearrange("a p n -> p (a n)")).then_inc(s_wF, 16)
            sp_.wait_ge(s_res, 1 + total)
            sp_.dma_start(xout, xT[:]).then_inc(s_out, 16)
            sp_.wait_ge(s_out, 1 + 16)

        @block.tensor
        def _(pe):
            mul = nc.tensor.matmul
            pe.wait_ge(s_const, 1 + CONSTS)
            pe.wait_ge(s_ini, 1 + 4)

            def steps(it, prev, att, nxt):
                def scores(n, odd):
                    if not att:
                        return
                    t, par, U = n % T4, n // T4 % 2, 4 * it + n // T4
                    if odd:
                        past(pe, s_s[0], NS * it + n + 1)
                    else:
                        past(pe, s_mx, (NS * it + n - 1) * HG)
                    r = slice(odd * DH, (odd + 1) * DH)
                    for pair in range(2):
                        h = 2 * pair + odd
                        if t == 0 and not odd:
                            past(pe, s_qe, 2 * U + 2)
                            past(pe, s_ke, 2 * U + pair + 1)
                        w = mul(bS[n % 2][:, h * P:(h + 1) * P], qk[r, par, 0, pair, t * P:(t + 1) * P],
                                qk[r, par, 1, pair, t * P:(t + 1) * P], start=True, stop=True,
                                tile_position=(odd * DH, 0))
                        if t:
                            w = mul(bS[n % 2][0:WINDOW, (h + 1) * P - WINDOW:(h + 1) * P],
                                    qk[r, par, 0, pair, t * P:t * P + WINDOW],
                                    qk[r, par, 1, pair, t * P - WINDOW:t * P], start=True, stop=True,
                                    tile_position=(odd * DH, 0))
                    w.then_inc(s_s[odd], 1)

                def turn(n):
                    if not (att if n >= 0 else prev):
                        return
                    past(pe, s_pn, NS * it + n + 1)
                    past(pe, s_pte, NS * it + n)
                    for h in range(HG):
                        w = nc.tensor.transpose(bT[:, h * P:(h + 1) * P], sp[:, n % 2, h], idn[:])
                    w.then_inc(s_pt, 1)

                def mix(n, heads):
                    if not (att if n >= 0 else prev):
                        return
                    t, par = n % T4, n // T4 % 2
                    if heads[0] == 0:
                        past(pe, s_pte, NS * it + n + 1)
                        past(pe, s_ot, NS * it + n)
                        if t == 0:
                            past(pe, s_v, (4 * it + n // T4 + 1) * 2)
                        if t == 1:
                            past(pe, s_vd, 4 * it + n // T4 + 1)
                    for h in heads:
                        q = slice(64 * (h % 2), 64 * (h % 2) + 64)
                        v = slice(h * DH, (h + 1) * DH)
                        c = (h // 2) * P
                        w = mul(bO[q, c:c + P], V[:, par, t, v], PT[:, n % 2, h], start=True, stop=True)
                        if t:
                            w = mul(bO[q, c:c + WINDOW], Vd[96:P, par, t - 1, v], PT[96:P, n % 2, h, 0:WINDOW],
                                    start=False, stop=True, tile_position=(96, 64 * (h % 2)), skip_group_check=True)
                    if heads[-1] == HG - 1:
                        w.then_inc(s_pv, 1)

                def project(u, g, j):
                    mul((bA, bB)[j % 2][:], xs[:, j * P:(j + 1) * P], Wqk[:, g * 2 * UW:(g + 1) * 2 * UW],
                        start=True, stop=True).then_inc(s_qk, 1)

                def values(g, half):
                    for k in range(2):
                        j = 2 * half + k
                        w = mul((bA, bB)[half][:, k * UW:(k + 1) * UW], xs[:, j * P:(j + 1) * P],
                                Wv[:, g * UW:(g + 1) * UW], start=True, stop=True)
                    w.then_inc(s_vp, 1)

                def transpose(bank, c, s):
                    for j in range(T4):
                        w = nc.tensor.transpose(bank[:, j * P:(j + 1) * P], rot[:, j, c * P:(c + 1) * P], idn[:])
                    w.then_inc(s, 1)

                def output(g):
                    for k in (2 * g, 2 * g + 1):
                        w = mul(bW[:], Wo[:, k], OT[:, k], start=k == 0, stop=k == INNER // P - 1)
                    w.then_inc(s_wo, 1)

                def side0(n):
                    g, t = (n // T4 + 1) % GROUPS, n % T4
                    u = 4 * it + n // T4 + 1
                    if n == 2 and prev:
                        past(pe, s_ot, NS * it)
                        output(GROUPS - 1)
                    if not prepares(n, att, nxt):
                        return
                    if t == 0:
                        past(pe, s_ke, 2 * u - 1)
                        project(u, g, 1)
                    if t == 1:
                        past(pe, s_rot, 4 * u + 2)
                        project(u, g, 3)
                    if t == 2:
                        past(pe, s_rot, 4 * u + 4)
                        values(g, 1)
                    if t == 3:
                        past(pe, s_rope, 4 * u + 4)
                        past(pe, s_ke, 2 * u)
                        if n == 11 and prev:
                            past(pe, s_hd, 3 * it - 2)
                        transpose(bM, 0, s_qt)
                        past(pe, s_v, 2 * u + 1)
                        transpose(bA, 1, s_qt)

                def side1(n):
                    if n == 10 and prev:
                        past(pe, s_ge, 3 * it)
                        mul(bM[:], W1[:, 0:P], xn[:], start=True, stop=True).then_inc(s_val, 1)
                    g, t = (n // T4 + 1) % GROUPS, n % T4
                    u = 4 * it + n // T4 + 1
                    if prepares(n, att, nxt):
                        if t == 0:
                            past(pe, s_rot, 4 * u + 1)
                            project(u, g, 2)
                        if t == 1:
                            past(pe, s_rot, 4 * u + 3)
                            if n == 13:
                                past(pe, s_wV, ((it + 1) // nb + 1) * 16)
                            values(g, 0)
                        if t == 3:
                            past(pe, s_kn, u + 1)
                            past(pe, s_v, 2 * u + 2)
                            transpose(bB, 2, s_kt)
                            past(pe, s_qe, 2 * u + 1)
                            transpose(bM, 3, s_kt)
                    if begins(n, att, nxt):
                        if n == 11:
                            past(pe, s_wA, ((it + 1) // nb + 1) * 16)
                            past(pe, s_xs, it + 2)
                        past(pe, s_qe, 2 * u + 2)
                        project(u + 1, (g + 1) % GROUPS, 0)
                    if prev:
                        if n == 3:
                            past(pe, s_xf, it)
                            mul(bW[:], onesC[:], xf[:], start=True, stop=True).then_inc(s_mean, 1)
                        if n == 4:
                            past(pe, s_xv, it)
                            for k in range(T4):
                                w = mul(bW[:, k:k + 1], xv[:, k * P:(k + 1) * P], onesC[:, 0:1], start=True, stop=True)
                            w.then_inc(s_var, 1)
                        if n == 6:
                            past(pe, s_rf, it * NEWTON)
                            for k in range(T4):
                                w = mul(bW[:, k * P:(k + 1) * P], rstd[:, k:k + 1].broadcast_to([P, P]), idn[:],
                                        start=True, stop=True)
                            w.then_inc(s_rbb, 1)
                        if n == 7:
                            past(pe, s_xn, it)
                            past(pe, s_wF, ((it - 1) // nb + 1) * WF)
                            mul(bW[:], W1[:, DI:DI + P], xn[:], start=True, stop=True).then_inc(s_gate, 1)
                        if n == 8:
                            if att:
                                past(pe, s_ke, 8 * it + 6)
                            mul(bM[:], W1[:, DI + P:DI + 2 * P], xn[:], start=True, stop=True).then_inc(s_gate, 1)
                            past(pe, s_g0, it)
                            mul(bW[0:HM[2], :], W1[:, DI + 2 * P:2 * DI], xn[:], start=True, stop=True).then_inc(s_gate, 1)
                        if n == 10:
                            mul(bW[:], W1[:, P:2 * P], xn[:], start=True, stop=True).then_inc(s_val, 1)
                        if n == 11:
                            past(pe, s_hd, 3 * it - 1)
                            mul(bW[0:HM[2], :], W1[:, 2 * P:DI], xn[:], start=True, stop=True).then_inc(s_val, 1)
                        if n == 12:
                            past(pe, s_hd, 3 * it)
                            for m in range(3):
                                w = mul(bW[:], W2[0:HM[m], m], hd[0:HM[m], m], start=m == 0, stop=m == 2)
                            w.then_inc(s_w2, 1)
                    if att and n >= 13:
                        if n == 13:
                            past(pe, s_wO, (it // nb + 1) * 16)
                            if prev:
                                past(pe, s_res, it)
                        past(pe, s_ot, NS * it + (n - 12) * T4)
                        output(n - 13)

                for n in range(NS):
                    if n % T4 == 0:
                        side0(n)
                        mix(n - 2, (0, 1))
                        scores(n, 0)
                        mix(n - 2, (2, 3))
                        scores(n, 1)
                    else:
                        scores(n, 0)
                        side0(n)
                        mix(n - 2, (0, 1))
                        scores(n, 1)
                        mix(n - 2, (2, 3))
                    if n % T4 == 2:
                        side1(n)
                        turn(n - 1)
                    else:
                        turn(n - 1)
                        side1(n)

            iterations(pe, steps)

        @block.vector
        def _(dve):
            tt, ts, stt = nc.vector.tensor_tensor, nc.vector.tensor_scalar, nc.vector.scalar_tensor_tensor
            dve.wait_ge(s_const, 1 + CONSTS)
            dve.wait_ge(s_ini, 1 + 4)

            def steps(it, prev, att, nxt):
                def normalise(n):
                    if not (att if n >= 0 else prev):
                        return
                    past(dve, s_exp, (NS * it + n + 1) * HG)
                    nc.vector.reciprocal(rc[:, n % 2], su[:, n % 2]).then_inc(s_rc, 1)
                    past(dve, s_rc, NS * it + n + 1)
                    tt(sp[:, n % 2], sp[:, n % 2], rc[:, n % 2].unsqueeze(2).broadcast_to([P, HG, P]), ALU.mult)\
                        .then_inc(s_pn, 1)

                def maxima(n):
                    past(dve, s_s[1], NS * it + n + 1)
                    if n % T4 == 0:
                        past(dve, s_ir, (4 * it + n // T4 + 1) * NEWTON)
                    nc.vector.memset(pad[:], 0.0)
                    t, par = n % T4, n // T4 % 2
                    for h in range(HG):
                        nc.vector.tensor_tensor_reduce(
                            sp[:, n % 2, h], bS[n % 2][:, h * P:(h + 1) * P], mk[:, 1 if t else 0],
                            ir[:, par, 2 * t * HG + h:2 * t * HG + h + 1], -3e38,
                            ALU.add, ALU.max, mx[:, n % 2, h:h + 1]).then_inc(s_mx, 1)
                    past(dve, s_mx, (NS * it + n + 1) * HG)
                    ts(nm[:, n % 2], mx[:, n % 2], -QK_SCALE, None, ALU.mult).then_inc(s_nm, 1)

                def rotate(u, j):
                    past(dve, s_sq, 4 * u + j + 1)
                    past(dve, s_rope, 4 * u + j - 1)

                    def heads(a):
                        return a.rearrange("p (k h d) -> p k h d", k=2, h=HG)

                    def table(i, half):
                        d = slice(half * HALF, (half + 1) * HALF) if half < 2 else slice(0, DH)
                        a = tl[:, j].rearrange("p (i k d) -> p i k d", i=2, k=2)[:, i, :, d]
                        return a.unsqueeze(2).broadcast_to([P, 2, HG, HALF if half < 2 else DH])
                    src, m0, m1 = heads((bA, bB)[j % 2][:]), heads(mm[:, j % 2, 0]), heads(mm[:, j % 2, 1])
                    tt(m0, src, table(0, 2), ALU.mult)
                    tt(m1[:, :, :, 0:HALF], src[:, :, :, HALF:DH], table(1, 0), ALU.mult)
                    tt(m1[:, :, :, HALF:DH], src[:, :, :, 0:HALF], table(1, 1), ALU.mult).then_inc(s_rot, 1)

                def sums(u, j):
                    past(dve, s_ha, 4 * u + j + 1)
                    nc.vector.tensor_reduce(ss[:, 2 * j * HG:2 * (j + 1) * HG], sqh[:, j % 2], AX, ALU.add).then_inc(s_ss, 1)

                for n in range(NS):
                    g, t = (n // T4 + 1) % GROUPS, n % T4
                    u = 4 * it + n // T4 + 1
                    par = (n // T4 + 1) % 2
                    prep = prepares(n, att, nxt)
                    if att and t == 0:
                        U = u - 1
                        past(dve, s_s[1], 4 * (U - 1))
                        for k in range(2):
                            past(dve, s_kt, 2 * U + k + 1)
                            nc.vector.tensor_copy(qk[:, 1 - par, 1, k], (bB, bM)[k][:]).then_inc(s_ke, 1)
                    if prep and t == 0:
                        if n == 12:
                            past(dve, s_tab, it + 2)
                        rotate(u, 0)
                    if prep and t == 1:
                        rotate(u, 2)
                    if prep and t == 2:
                        sums(u, 3)
                        past(dve, s_ss, 4 * u + 4)
                        past(dve, s_ir, u * NEWTON)
                        ts(xr[:], ss[:], 1e-24, 0.5, ALU.max, ALU.mult).then_inc(s_ir, 1)
                        root_guess(nc, dve, s_ir, u * NEWTON, ir[:, par], xr[:], yr[:])
                    if prev and n == 4:
                        past(dve, s_mean, it)
                        tt(xc[:], xf[:], bW[:], ALU.subtract).then_inc(s_xc, 1)
                    if prev and n == 5:
                        past(dve, s_var, it)
                        ts(va[:], bW[:, 0:T4], 1e-5, 0.5, ALU.add, ALU.mult).then_inc(s_rf, 1)
                        root_guess(nc, dve, s_rf, (it - 1) * NEWTON, rstd[:], va[:], vt[:])
                    if n == 11 and prev:
                        past(dve, s_val, 3 * it - 1)
                        past(dve, s_ge, 3 * it - 1)
                        stt(hd[:, 1], bW[:], smF[:, B1A + 1:B1A + 2], ge[:, 1], ALU.add, ALU.mult).then_inc(s_hd, 1)
                    normalise(n - 1)
                    if n == 12 and prev:
                        k = HM[2]
                        past(dve, s_val, 3 * it)
                        stt(hd[0:k, 2], bW[0:k, :], smF[0:k, B1A + 2:B1A + 3], ge[0:k, 2], ALU.add, ALU.mult)\
                            .then_inc(s_hd, 1)
                    if n == 11 and nxt:
                        past(dve, s_wT, ((it + 1) // nb + 1) * 16)
                        tt(tl[:], tb[:], sc[:].unsqueeze(1).broadcast_to([P, T4, TW]), ALU.mult).then_inc(s_tab, 1)
                    if prep and t == 1:
                        sums(u, 1)
                    if n == 2 and prev:
                        past(dve, s_wo, 4 * it)
                        xb = xT[:, bass.ds((it - 1) % nb * L, L)]
                        tt(xb, bW[:], xb, ALU.add).then_inc(s_x1, 1)
                    if prev:
                        xb = xT[:, bass.ds((it - 1) % nb * L, L)]
                        if n == 7:
                            past(dve, s_rbb, it)
                            tt(xc[:], xc[:], bW[:], ALU.mult).then_inc(s_xh, 1)
                            past(dve, s_xh, it)
                            past(dve, s_wF, ((it - 1) // nb + 1) * WF)
                            ts(xn[:], xc[:], smF[:, LNG:LNG + 1], smF[:, LNB:LNB + 1], ALU.mult, ALU.add).then_inc(s_xn, 1)
                        if n == 13:
                            past(dve, s_w2, it)
                            stt(xb, bW[:], smF[:, B2C:B2C + 1], xb, ALU.add, ALU.add).then_inc(s_res, 1)
                    if att:
                        maxima(n)
                    if prep and t < 2:
                        rotate(u, 2 * t + 1)
                        sums(u, 2 * t)
                    if n == 10 and prev:
                        past(dve, s_val, 3 * it - 2)
                        past(dve, s_ge, 3 * it - 2)
                        stt(hd[:, 0], bM[:], smF[:, B1A:B1A + 1], ge[:, 0], ALU.add, ALU.mult).then_inc(s_hd, 1)

            iterations(dve, steps)

        @block.scalar
        def _(act):
            f = nc.scalar.activation
            act.wait_ge(s_const, 1 + CONSTS)
            act.wait_ge(s_ini, 1 + 4)

            def steps(it, prev, att, nxt):
                def exps(n):
                    if not (att if n >= 0 else prev):
                        return
                    past(act, s_nm, NS * it + n + 1)
                    for h in range(HG):
                        f(sp[:, n % 2, h], sp[:, n % 2, h], ACT.Exp, bias=nm[:, n % 2, h:h + 1], scale=QK_SCALE,
                          accum_out=su[:, n % 2, h:h + 1]).then_inc(s_exp, 1)

                def turned(n):
                    if not (att if n >= 0 else prev):
                        return
                    past(act, s_pt, NS * it + n + 1)
                    past(act, s_pv, NS * it + n - 1)
                    f(PT[:, n % 2], bT[:].rearrange("p (h q) -> p h q", h=HG), ACT.Copy).then_inc(s_pte, 1)

                def mixed(n):
                    if not (att if n >= 0 else prev):
                        return
                    g, t = n // T4 % GROUPS, n % T4
                    past(act, s_pv, NS * it + n + 1)
                    if t == 0:
                        past(act, s_wo, 4 * (it if n >= 0 else it - 1) + g - 3)
                    f(OT[:, 2 * g:2 * g + 2, t * P:(t + 1) * P],
                      bO[:, 0:2 * P].rearrange("p (h q) -> p h q", h=2), ACT.Copy).then_inc(s_ot, 1)

                def shift(dst, seq, s):
                    f(padA[:], idn[:, 0:1], ACT.Copy)
                    f(dst[0:64, :], xT[0:64, bass.ds(seq * L, L)], ACT.Copy)
                    f(dst[64:P, 1:L], xT[64:P, bass.ds(seq * L, L - 1)], ACT.Copy).then_inc(s, 1)

                def squares(u, j):
                    past(act, s_qk, 4 * u + j + 1)
                    past(act, s_ha, 4 * u + j - 1)
                    f(sq[:, j % 2], (bA, bB)[j % 2][:], ACT.Square).then_inc(s_sq, 1)

                def values(u, par, k):
                    past(act, s_pv, 4 * (u - 1))
                    past(act, s_vp, 2 * u + k + 1)
                    f(V[:, par, 2 * k:2 * k + 2], (bA, bB)[k][:].rearrange("p (t d) -> p t d", t=2), ACT.Copy)\
                        .then_inc(s_v, 1)

                for n in range(NS):
                    t = n % T4
                    u = 4 * it + n // T4 + 1
                    par = (n // T4 + 1) % 2
                    prep = prepares(n, att, nxt)
                    if prep and t < 2:
                        squares(u, 2 * t)
                    turned(n - 2)
                    exps(n - 1)
                    if prep and t == 2:
                        values(u, par, 0)
                    if n == 4 and prev:
                        past(act, s_xc, it)
                        f(xv[:], xc[:], ACT.Square).then_inc(s_xv, 1)
                    if n == 8 and prev:
                        past(act, s_gate, 3 * it - 2)
                        f(ge[:, 0], bW[:], ACT.Copy).then_inc(s_g0, 1)
                    if prep and t < 2:
                        squares(u, 2 * t + 1)
                    if prep and t == 2:
                        values(u, par, 1)
                    if prep and t == 3:
                        past(act, s_s[1], 4 * (u - 1))
                        for k in range(2):
                            past(act, s_qt, 2 * u + k + 1)
                            f(qk[:, par, 0, k], (bM, bA)[k][:], ACT.Copy).then_inc(s_qe, 1)
                    if n == 9 and prev:
                        past(act, s_gate, 3 * it)
                        past(act, s_g0, it)
                        for m, src in ((0, ge[:, 0]), (1, bM[:]), (2, bW[0:HM[2], :])):
                            k = HM[m]
                            f(ge[0:k, m], src, ACT.Gelu, bias=smF[0:k, B1G + m:B1G + m + 1]).then_inc(s_ge, 1)
                    mixed(n - 2)
                    if n == 2 and prev:
                        past(act, s_x1, it)
                        shift(xf, (it - 1) % nb, s_xf)
                    if n == 10 and nxt:
                        past(act, s_vp, 8 * (it + 1))
                        past(act, s_res, it - 1)
                        shift(xs, (it + 1) % nb, s_xs)

            iterations(act, steps)

        @block.gpsimd
        def _(pool):
            nc.gpsimd.memset(xs[:], 0.0).then_inc(s_ini, 1)
            nc.gpsimd.memset(xf[:], 0.0).then_inc(s_ini, 1)
            nc.gpsimd.memset(onesC[:], 1.0 / C).then_inc(s_ini, 1)
            nc.gpsimd.memset(c15[:], 1.5).then_inc(s_ini, 1)
            pool.wait_ge(s_ini, 1 + 4)
            pool.wait_ge(s_const, 1 + CONSTS)
            tt = nc.gpsimd.tensor_tensor

            def steps(it, prev, att, nxt):
                for n in range(NS):
                    t = n % T4
                    u = 4 * it + n // T4 + 1
                    par = (n // T4 + 1) % 2
                    prep = prepares(n, att, nxt)
                    if n == 5 and prev:
                        root_newton(nc, pool, s_rf, (it - 1) * NEWTON, rstd[:], va[:], vt[:], c15[:, 0:T4])
                    if prep and t < 2:
                        for j in (2 * t, 2 * t + 1):
                            past(pool, s_sq, 4 * u + j + 1)
                            past(pool, s_ss, 4 * u + j - 1)
                            a = sq[:, j % 2].rearrange("p (h d) -> p h d", d=DH)
                            tt(sqh[:, j % 2], a[:, :, 0:HALF], a[:, :, HALF:DH], ALU.add).then_inc(s_ha, 1)
                            past(pool, s_rot, 4 * u + j + 1)
                            past(pool, s_kt, 2 * u)
                            tt(rot[:, j], mm[:, j % 2, 0], mm[:, j % 2, 1], ALU.add).then_inc(s_rope, 1)
                    if prep and t == 2:
                        root_newton(nc, pool, s_ir, u * NEWTON, ir[:, par], xr[:], yr[:], c15[:])
                        past(pool, s_ir, (u + 1) * NEWTON)
                        past(pool, s_rope, 4 * u + 4)
                        keys = rot[:, :, UW:2 * UW].rearrange("p t (h d) -> p t h d", h=HG)
                        inv = ir[:, par].rearrange("p (t k h) -> p t k h", k=2, h=HG)[:, :, 1]
                        tt(keys, keys, inv.unsqueeze(3).broadcast_to([P, T4, HG, DH]), ALU.mult).then_inc(s_kn, 1)
                    if prep and t == 3:
                        past(pool, s_v, 2 * (u + 1))
                        tt(Vd[:, par], V[:, par, 0:T4 - 1], V[:, par, 1:T4], ALU.subtract).then_inc(s_vd, 1)

            iterations(pool, steps)


def pack_local(d):
    w = d["L1_ffn_Wqkv"]
    wqk = w[:, :, 0:2 * INNER].reshape(DEPTH, C, 2, GROUPS, UW).transpose(0, 1, 3, 2, 4).reshape(DEPTH, C, 2 * INNER)
    qs, ks = d["L1_ffn_q_scale"], d["L1_ffn_k_scale"]
    other = np.r_[HALF:DH, 0:HALF]
    sc = np.concatenate([qs, ks, qs[:, other], ks[:, other]], 1)
    scales = np.ascontiguousarray(np.broadcast_to(sc[:, None, :], (DEPTH, P, TW)))
    sm = np.zeros((DEPTH, P, NSMALL), np.float32)
    sm[:, :, LNG], sm[:, :, LNB], sm[:, :, B2C] = d["L1_ffn_ln_g"], d["L1_ffn_ln_b"], d["L1_ffn_b2"]
    for m in range(3):
        sm[:, 0:HM[m], B1A + m] = d["L1_ffn_b1"][:, m * P:m * P + HM[m]]
        sm[:, 0:HM[m], B1G + m] = d["L1_ffn_b1"][:, DI + m * P:DI + m * P + HM[m]]
    return np.ascontiguousarray(wqk), np.ascontiguousarray(w[:, :, 2 * INNER:]), scales, sm


DIN = 2 * C
NH = DIN // P
NS = 16
TC = 16
HB = NH * B
W_ = HB * NS
NCH = L // TC
SU = 4
CW, CB, BDT, DPAR, LNW2, LNB2 = 0, 4, 5, 6, 7, 8
NV = 9


def build_ssm_inputs(nc, xn_d, w_in, w_x, w_dt, vec, dt, u, bc, xi_d, sz_d):
    with ExitStack() as ctx:
        def sb(name, shape):
            return ctx.enter_context(nc.sbuf_tensor(name, shape, F32))

        sems = []

        def sem(name):
            sems.append(ctx.enter_context(nc.semaphore(name)))
            return sems[-1]

        xn = sb("m_xn", [P, 2, L])
        win = sb("m_win", [P, 2 * DIN])
        wx = sb("m_wx", [P, NH, 33])
        wdt = sb("m_wdt", [1, DIN])
        vc = sb("m_vec", [P, NH, NV])
        xcv = sb("m_xcv", [P, NH, L])
        xis = sb("m_xis", [P, NH, L])
        szs = sb("m_szs", [P, NH, L])
        dtr = sb("m_dtr", [1, L])
        ab = sb("m_ab", [P, NH, L])
        re = sb("m_re", [P, NH, L])
        bank = [ctx.enter_context(nc.psum_tensor(f"m_b{i}", [P, 512], F32)) for i in range(8)]
        s_c, s_x, s_in, s_cv, s_sl, s_st = (sem(n) for n in ("m_c", "m_x", "m_in", "m_cv", "m_sl", "m_st"))
        s_xd, s_row, s_dtp, s_abs, s_ex, s_ln = (sem(n) for n in ("m_xd", "m_row", "m_dtp", "m_abs", "m_ex", "m_ln"))
        s_bc = sem("m_zero")
        s_re, s_sum, s_dt, s_u = (sem(n) for n in ("m_re", "m_sum", "m_dt", "m_u"))
        block = ctx.enter_context(nc.Block())

        @block.sync
        def _(sp):
            start_at_one(sp, sems)
            sp.dma_start(win[:], w_in).then_inc(s_c, 16)
            sp.dma_start(wx[:], w_x).then_inc(s_c, 16)
            sp.dma_start(wdt[:], w_dt).then_inc(s_c, 16)
            sp.dma_start(vc[:], vec).then_inc(s_c, 16)
            with sp.Fori(0, B) as b:
                sp.wait_ge(s_in, 1 + b)
                sp.dma_start(xn[:, 0], xn_d[:, bass.ds(b * L, L)]).then_inc(s_x, 16)
                sp.wait_ge(s_sl, 1 + (b + 1) * 4)
                sp.dma_start(xi_d[bass.ds(b, 1)].rearrange("a p n -> p (a n)"),
                             xis[:].rearrange("p h t -> p (h t)")).then_inc(s_st, 16)
                sp.dma_start(sz_d[bass.ds(b, 1)].rearrange("a p n -> p (a n)"),
                             szs[:].rearrange("p h t -> p (h t)")).then_inc(s_st, 16)
            sp.wait_ge(s_st, 1 + B * 32)

        @block.gpsimd
        def _(pool):
            nc.gpsimd.memset(bc[:], 0.0).then_inc(s_bc, 1)

        @block.tensor
        def _(pe):
            mul = nc.tensor.matmul
            pe.wait_ge(s_c, 1 + 64)
            with pe.Fori(0, B) as b:
                pe.wait_ge(s_x, 1 + (b + 1) * 16)
                pe.wait_ge(s_cv, 1 + b * 2 * 4)
                pe.wait_ge(s_sl, 1 + b * 4)
                for m in range(4):
                    w = mul(bank[m][:], win[:, m * P:(m + 1) * P], xn[:, 0], start=True, stop=True)
                w.then_inc(s_in, 1)
                pe.wait_ge(s_sl, 1 + b * 4 + 2)
                pe.wait_ge(s_row, 1 + b * 2)
                for o, c in ((bank[4][0:32, :], slice(0, 32)), (bank[5][0:1, :], slice(32, 33))):
                    for h in range(NH):
                        w = mul(o, wx[:, h, c], xis[:, h], start=h == 0, stop=h == NH - 1)
                w.then_inc(s_xd, 1)
                pe.wait_ge(s_row, 1 + b * 2 + 2)
                pe.wait_ge(s_re, 1 + b * 2)
                for h in range(NH):
                    w = mul(bank[6 + h][:], wdt[:, h * P:(h + 1) * P], dtr[:], start=True, stop=True)
                w.then_inc(s_dtp, 1)

        @block.scalar
        def _(act):
            f = nc.scalar.activation
            act.wait_ge(s_c, 1 + 64)
            act.wait_ge(s_bc, 1 + 1)
            with act.Fori(0, B) as b:
                act.wait_ge(s_st, 1 + b * 32)
                act.wait_ge(s_u, 1 + b * 2)
                act.wait_ge(s_cv, 1 + (b + 1) * 2 * 4)
                for h in range(NH):
                    f(xis[:, h], xcv[:, h], ACT.Silu).then_inc(s_sl, 1)
                act.wait_ge(s_in, 1 + b + 1)
                for h in range(NH):
                    f(szs[:, h], bank[2 + h][:], ACT.Silu).then_inc(s_sl, 1)
                act.wait_ge(s_xd, 1 + b + 1)
                f(bc[0:32, :, bass.ds(b, 1)].rearrange("p t a -> p (t a)"), bank[4][0:32, :], ACT.Copy).then_inc(s_row, 1)
                f(dtr[:], bank[5][0:1, :], ACT.Copy).then_inc(s_row, 1)
                act.wait_ge(s_dtp, 1 + b + 1)
                act.wait_ge(s_sum, 1 + b * 2)
                for h in range(NH):
                    f(ab[:, h], bank[6 + h][:], ACT.Abs, bias=vc[:, h, BDT:BDT + 1]).then_inc(s_abs, 1)
                act.wait_ge(s_abs, 1 + (b + 1) * 2)
                for h in range(NH):
                    f(ab[:, h], ab[:, h], ACT.Exp, scale=-1.0).then_inc(s_ex, 1)
                act.wait_ge(s_ex, 1 + (b + 1) * 2)
                for h in range(NH):
                    f(ab[:, h], ab[:, h], ACT.Ln, bias=1.0).then_inc(s_ln, 1)

        @block.vector
        def _(dve):
            tt, ts, stt = nc.vector.tensor_tensor, nc.vector.tensor_scalar, nc.vector.scalar_tensor_tensor
            dve.wait_ge(s_c, 1 + 64)
            with dve.Fori(0, B) as b:
                dve.wait_ge(s_in, 1 + b + 1)
                dve.wait_ge(s_sl, 1 + b * 4)
                for h in range(NH):
                    ts(xcv[:, h], bank[h][:], vc[:, h, CW + 3:CW + 4], vc[:, h, CB:CB + 1], ALU.mult, ALU.add)\
                        .then_inc(s_cv, 1)
                for k in range(1, 4):
                    for h in range(NH):
                        dve.wait_ge(s_cv, 1 + b * 8 + 2 * k - 1 + h)
                        stt(xcv[:, h, k:L], bank[h][:, 0:L - k], vc[:, h, CW + 3 - k:CW + 4 - k], xcv[:, h, k:L],
                            ALU.mult, ALU.add).then_inc(s_cv, 1)
                dve.wait_ge(s_abs, 1 + (b + 1) * 2)
                for h in range(NH):
                    ts(re[:, h], bank[6 + h][:], vc[:, h, BDT:BDT + 1], 0.0, ALU.add, ALU.max).then_inc(s_re, 1)
                for h in range(NH):
                    dve.wait_ge(s_ln, 1 + b * 2 + h + 1)
                    dve.wait_ge(s_re, 1 + b * 2 + h + 1)
                    tt(re[:, h], re[:, h], ab[:, h], ALU.add).then_inc(s_sum, 1)
                for h in range(NH):
                    dve.wait_ge(s_sum, 1 + b * 2 + h + 1)
                    ts(dt[:, bass.ds(b + h * B, 1)].rearrange("p a t -> p (a t)"), re[:, h], 1e-4, 10.0, ALU.max, ALU.min).then_inc(s_dt, 1)
                for h in range(NH):
                    dve.wait_ge(s_dt, 1 + b * 2 + h + 1)
                    tt(u[:, bass.ds(b + h * B, 1)].rearrange("p a t -> p (a t)"), dt[:, bass.ds(b + h * B, 1)].rearrange("p a t -> p (a t)"),
                       xis[:, h], ALU.mult).then_inc(s_u, 1)


def build_ssm_scan(nc, alog, ident_d, dt, u, bc):
    with ExitStack() as ctx:
        def sb(name, shape):
            return ctx.enter_context(nc.sbuf_tensor(name, shape, F32))

        sems = []

        def sem(name):
            sems.append(ctx.enter_context(nc.semaphore(name)))
            return sems[-1]

        def view(buf):
            return buf.rearrange("p (t g s) -> p t g s", t=TC, g=HB)

        A = sb("n_A", [P, NS])
        lim = sb("n_lim", [P, NS])
        idn = sb("n_idn", [P, P])
        dA = [sb(f"n_dA{i}", [P, TC * W_]) for i in range(2)]
        dB = [sb(f"n_dB{i}", [P, TC * W_]) for i in range(2)]
        H = [sb(f"n_H{i}", [P, TC * W_]) for i in range(2)]
        hC = sb("n_hC", [P, TC * W_])
        Cs = sb("n_Cs", [P, NS * TC * B])
        mt = sb("n_mt", [P, W_])
        carry = sb("n_carry", [P, W_])
        bB = [ctx.enter_context(nc.psum_tensor(f"n_bB{i}", [P, 512], F32)) for i in range(4)]
        bC = [ctx.enter_context(nc.psum_tensor(f"n_bC{i}", [P, 512], F32)) for i in range(2)]
        bY = [ctx.enter_context(nc.psum_tensor(f"n_bY{i}", [P, 512], F32)) for i in range(2)]
        s_c, s_a, s_bB, s_bC, s_dx, s_dA, s_dB, s_cl = (sem(n) for n in ("n_c", "n_a", "n_sB", "n_sC", "n_dx", "n_sA", "n_sdB", "n_cl"))
        s_m, s_s, s_h, s_Cs, s_hC, s_y, s_ye = (sem(n) for n in ("n_m", "n_s", "n_h", "n_sCs", "n_shC", "n_y", "n_ye"))
        NU = NS // SU
        HC0 = 1
        block = ctx.enter_context(nc.Block())

        @block.sync
        def _(sp):
            start_at_one(sp, sems)
            sp.sem_inc(s_hC, HC0)
            sp.dma_start(A[:], alog).then_inc(s_c, 16)
            sp.dma_start(idn[:], ident_d).then_inc(s_c, 16)

        @block.tensor
        def _(pe):
            mul = nc.tensor.matmul
            pe.wait_ge(s_c, 1 + 32)

            def spread(k, row, banks, done, used, used_at):
                for v in range(NU):
                    if used_at(v) is not None:
                        pe.wait_ge(used, 1 + used_at(v))
                    for i in range(SU):
                        s = row + v * SU + i
                        w = mul(banks[v % len(banks)][:, i * TC * B:(i + 1) * TC * B],
                                idn[:, s:s + 1].broadcast_to([P, P]),
                                bc[:, bass.ds(k * TC, TC), :].rearrange("p t b -> p (t b)"), start=True, stop=True)
                    w.then_inc(done, 1)

            def states(k):
                pe.wait_ge(s_ye, 1 + k)
                pe.wait_ge(s_hC, 1 + HC0 + k + 1)
                for s in range(NS):
                    w = mul(bY[0][:, 0:TC * HB], idn[:], hC[:, s:TC * W_:NS], start=s == 0, stop=s == NS - 1)
                w.then_inc(s_y, 1)

            spread(0, 0, bB, s_bB, s_dB, lambda v: None)
            spread(1, 0, bB, s_bB, s_dB, lambda v: NU)
            spread(0, NS, bC, s_bC, s_Cs, lambda v: v - 1 if v > 1 else None)
            with pe.Fori(1, NCH) as k:
                spread((k + 1) % NCH, 0, bB, s_bB, s_dB, lambda v: (k + 1) * NU)
                states(k - 1)
                spread(k, NS, bC, s_bC, s_Cs, lambda v: k * NU + v - 1 if v else k * NU)
            states(NCH - 1)

        @block.scalar
        def _(act):
            f = nc.scalar.activation
            act.wait_ge(s_a, 1 + 1)
            f(A[:], A[:], ACT.Exp).then_inc(s_a, 1)

            def exps(kk, i):
                act.wait_ge(s_dx, 1 + kk + 1)
                f(dA[i][:], dA[i][:], ACT.Exp).then_inc(s_dA, 1)

            exps(0, 0)
            def sums(k):
                act.wait_ge(s_y, 1 + k + 1)
                f(u[:, :, bass.ds(k * TC, TC)], bY[0][:, 0:TC * HB].rearrange("p (t g) -> p g t", t=TC), ACT.Copy)\
                    .then_inc(s_ye, 1)

            def pair(k2, first):
                for i in range(2):
                    k = k2 * 2 + i
                    exps(k + 1, 1 - i)
                    if i or not first:
                        sums(k - 1)
                    for v in range(NU):
                        act.wait_ge(s_bC, 1 + k * NU + v + 1)
                        if v == 0:
                            act.wait_ge(s_hC, 1 + HC0 + k)
                        f(Cs[:, v * 512:(v + 1) * 512], bC[v % 2][:], ACT.Copy).then_inc(s_Cs, 1)

            pair(0, True)
            with act.Fori(1, NCH // 2) as k2:
                pair(k2, False)
            sums(NCH - 1)

        @block.gpsimd
        def _(pool):
            with pool.Fori(0, NCH // 2) as k2:
                for i in range(2):
                    k = k2 * 2 + i
                    pool.wait_ge(s_h, 1 + (k + 1) * TC)
                    pool.wait_ge(s_Cs, 1 + (k + 1) * NU)
                    pool.wait_ge(s_y, 1 + k)
                    cv = Cs[:].rearrange("p (s t b) -> p t b s", s=NS, t=TC)
                    for h in range(NH):
                        w = nc.gpsimd.tensor_tensor(view(hC[:])[:, :, h * B:(h + 1) * B, :],
                                                    view(H[i][:])[:, :, h * B:(h + 1) * B, :], cv, ALU.mult)
                    w.then_inc(s_hC, 1)

        @block.vector
        def _(dve):
            tt, ts = nc.vector.tensor_tensor, nc.vector.tensor_scalar
            dve.wait_ge(s_c, 1 + 32)
            nc.vector.memset(carry[:], 0.0).then_inc(s_cl, 1)
            ts(A[:], A[:], 5.0, None, ALU.min).then_inc(s_a, 1)
            dve.wait_ge(s_a, 1 + 2)
            nc.vector.reciprocal(lim[:], A[:]).then_inc(s_a, 1)
            dve.wait_ge(s_a, 1 + 3)
            ts(lim[:], lim[:], 20.0, None, ALU.mult).then_inc(s_a, 1)
            ts(A[:], A[:], -1.0, None, ALU.mult).then_inc(s_a, 1)
            dve.wait_ge(s_a, 1 + 5)

            def decay(k, i, s):
                w = ts(view(dA[i][:])[:, :, :, s], dt[:, :, bass.ds(k * TC, TC)].rearrange("p g t -> p t g"),
                       lim[:, s:s + 1], A[:, s:s + 1], ALU.min, ALU.mult)
                if s == NS - 1:
                    w.then_inc(s_dx, 1)

            def drive(k, kw, i, v):
                dve.wait_ge(s_bB, 1 + kw * NU + v + 1)
                for h in range(NH):
                    w = tt(view(dB[i][:])[:, :, h * B:(h + 1) * B, v * SU:(v + 1) * SU],
                           u[:, h * B:(h + 1) * B, bass.ds(k * TC, TC)].rearrange("p b t -> p t b").unsqueeze(3)
                           .broadcast_to([P, TC, B, SU]),
                           bB[v][:].rearrange("p (s t b) -> p t b s", s=SU, t=TC), ALU.mult)
                w.then_inc(s_dB, 1)

            def clip_drive(kw, i):
                dve.wait_ge(s_dB, 1 + (kw + 1) * NU)
                ts(dB[i][:], dB[i][:], 10.0, -10.0, ALU.min, ALU.max).then_inc(s_cl, 1)

            for s in range(NS):
                decay(0, 0, s)
            for v in range(NU):
                drive(0, 0, 0, v)
            clip_drive(0, 0)
            with dve.Fori(0, NCH // 2) as k2:
                for i in range(2):
                    k = k2 * 2 + i
                    kn = (k + 1) % NCH
                    dve.wait_ge(s_dA, 1 + k + 1)
                    dve.wait_ge(s_cl, 1 + k + 2)
                    dve.wait_ge(s_hC, 1 + HC0 + k - 1)
                    todo = [lambda s=s: decay(kn, 1 - i, s) for s in range(NS)]
                    todo += [lambda v=v: drive(kn, k + 1, 1 - i, v) for v in range(NU)]
                    todo += [lambda: clip_drive(k + 1, 1 - i)]
                    for t in range(TC):
                        now = slice(t * W_, (t + 1) * W_)
                        if t:
                            prev = H[i][:, (t - 1) * W_:t * W_]
                        elif i:
                            prev = H[0][:, (TC - 1) * W_:TC * W_]
                        else:
                            prev = carry[:]
                        tt(mt[:], prev, dA[i][:, now], ALU.mult).then_inc(s_m, 1)
                        if todo:
                            todo.pop(0)()
                        dve.wait_ge(s_m, 1 + k * TC + t + 1)
                        tt(mt[:], mt[:], dB[i][:, now], ALU.add).then_inc(s_s, 1)
                        if len(todo) > TC - t:
                            todo.pop(0)()
                        dve.wait_ge(s_s, 1 + k * TC + t + 1)
                        ts(H[i][:, now], mt[:], 100.0, -100.0, ALU.min, ALU.max).then_inc(s_h, 1)
                        dve.wait_ge(s_h, 1 + k * TC + t + 1)
                    for job in todo:
                        job()
                    if i:
                        nc.vector.tensor_copy(carry[:], H[1][:, (TC - 1) * W_:TC * W_]).then_inc(s_a, 1)
                        dve.wait_ge(s_a, 1 + k2 + 6)


def build_ssm_output(nc, y, xi_d, sz_d, vec, w_out, ident_d, x1_d, ffn_d, out):
    with ExitStack() as ctx:
        def sb(name, shape):
            return ctx.enter_context(nc.sbuf_tensor(name, shape, F32))

        sems = []

        def sem(name):
            sems.append(ctx.enter_context(nc.semaphore(name)))
            return sems[-1]

        vc = sb("o_vec", [P, NH, NV])
        wo = sb("o_wo", [P, NH, C])
        idn = sb("o_idn", [P, P])
        onesD = sb("o_ones", [P, P])
        xi = sb("o_xi", [P, NH, L])
        sz = sb("o_sz", [P, NH, L])
        ff = sb("o_ff", [P, L])
        x1 = sb("o_x1", [P, T4, C])
        yc = sb("o_yc", [P, NH, L])
        yq = sb("o_yq", [P, NH, L])
        gt = sb("o_gt", [P, NH, L])
        va, rstd, vt = sb("o_va", [P, T4]), sb("o_rstd", [P, T4]), sb("o_vt", [P, T4])
        res = sb("o_res", [P, T4, C])
        bM, bV, bR, bO = (ctx.enter_context(nc.psum_tensor(f"o_b{i}", [P, 512], F32)) for i in range(4))
        s_c, s_ld, s_ini, s_mean, s_yc, s_yq, s_var, s_va, s_rs, s_rb, s_n, s_g, s_o, s_res, s_out = (
            sem("o_" + n) for n in ("c", "ld", "ini", "mean", "yc", "yq", "var", "va", "rs", "rb", "n", "g", "o", "res", "out"))
        block = ctx.enter_context(nc.Block())

        @block.sync
        def _(sp):
            start_at_one(sp, sems)
            sp.dma_start(vc[:], vec).then_inc(s_c, 16)
            sp.dma_start(wo[:], w_out).then_inc(s_c, 16)
            sp.dma_start(idn[:], ident_d).then_inc(s_c, 16)
            with sp.Fori(0, B) as b:
                sp.wait_ge(s_res, 1 + b)
                sp.dma_start(xi[:].rearrange("p h t -> p (h t)"), xi_d[bass.ds(b, 1)].rearrange("a p n -> p (a n)")).then_inc(s_ld, 16)
                sp.dma_start(sz[:].rearrange("p h t -> p (h t)"), sz_d[bass.ds(b, 1)].rearrange("a p n -> p (a n)")).then_inc(s_ld, 16)
                sp.dma_start(ff[:], ffn_d[:, bass.ds(b * L, L)]).then_inc(s_ld, 16)
                sp.dma_start(x1[:], x1_d[bass.ds(b, 1)].rearrange("a (t p) c -> p (a t) c", p=P)).then_inc(s_ld, 16)
                sp.wait_ge(s_res, 1 + b + 1)
                sp.dma_start(out[bass.ds(b, 1)].rearrange("a (t p) c -> p (a t) c", p=P), res[:]).then_inc(s_out, 16)
            sp.wait_ge(s_out, 1 + B * 16)

        @block.gpsimd
        def _(pool):
            nc.gpsimd.memset(onesD[:], 1.0 / DIN).then_inc(s_ini, 1)

        @block.tensor
        def _(pe):
            mul = nc.tensor.matmul
            pe.wait_ge(s_c, 1 + 48)
            pe.wait_ge(s_ini, 1 + 1)
            with pe.Fori(0, B) as b:
                pe.wait_ge(s_yc, 1 + b * 2)
                for h in range(NH):
                    w = mul(bM[:], onesD[:], y[:, bass.ds(b + h * B, 1)].rearrange("p a t -> p (a t)"), start=h == 0, stop=h == NH - 1)
                w.then_inc(s_mean, 1)
                pe.wait_ge(s_yq, 1 + (b + 1) * 2)
                for t in range(T4):
                    for h in range(NH):
                        w = mul(bV[:, t:t + 1], yq[:, h, t * P:(t + 1) * P], onesD[:, 0:1], start=h == 0, stop=h == NH - 1)
                w.then_inc(s_var, 1)
                pe.wait_ge(s_rs, 1 + (b + 1) * RSQRT_STEPS)
                for t in range(T4):
                    w = mul(bR[:, t * P:(t + 1) * P], rstd[:, t:t + 1].broadcast_to([P, P]), idn[:], start=True, stop=True)
                w.then_inc(s_rb, 1)
                pe.wait_ge(s_g, 1 + (b + 1) * 2)
                pe.wait_ge(s_ld, 1 + (b + 1) * 64)
                for t in range(T4):
                    q = slice(t * P, (t + 1) * P)
                    mul(bO[:, q], ff[:, q], idn[:], start=True, stop=False)
                    for h in range(NH):
                        w = mul(bO[:, q], gt[:, h, q], wo[:, h], start=False, stop=h == NH - 1)
                w.then_inc(s_o, 1)

        @block.scalar
        def _(act):
            with act.Fori(0, B) as b:
                for h in range(NH):
                    act.wait_ge(s_yc, 1 + b * 2 + h + 1)
                    nc.scalar.activation(yq[:, h], yc[:, h], ACT.Square).then_inc(s_yq, 1)

        @block.vector
        def _(dve):
            tt, ts, stt = nc.vector.tensor_tensor, nc.vector.tensor_scalar, nc.vector.scalar_tensor_tensor
            dve.wait_ge(s_c, 1 + 48)
            with dve.Fori(0, B) as b:
                dve.wait_ge(s_mean, 1 + b + 1)
                for h in range(NH):
                    tt(yc[:, h], y[:, bass.ds(b + h * B, 1)].rearrange("p a t -> p (a t)"), bM[:], ALU.subtract).then_inc(s_yc, 1)
                dve.wait_ge(s_var, 1 + b + 1)
                ts(va[:], bV[:, 0:T4], 1e-5, None, ALU.add).then_inc(s_va, 1)
                dve.wait_ge(s_va, 1 + b + 1)
                rsqrt(nc, dve, s_rs, b * RSQRT_STEPS, va[:], rstd[:], vt[:])
                dve.wait_ge(s_rb, 1 + b + 1)
                dve.wait_ge(s_ld, 1 + (b + 1) * 64)
                dve.wait_ge(s_o, 1 + b)
                for h in range(NH):
                    tt(yc[:, h], yc[:, h], bR[:], ALU.mult).then_inc(s_n, 1)
                for h in range(NH):
                    dve.wait_ge(s_n, 1 + b * 6 + h + 1)
                    ts(yc[:, h], yc[:, h], vc[:, h, LNW2:LNW2 + 1], vc[:, h, LNB2:LNB2 + 1], ALU.mult, ALU.add).then_inc(s_n, 1)
                for h in range(NH):
                    dve.wait_ge(s_n, 1 + b * 6 + h + 3)
                    stt(yc[:, h], xi[:, h], vc[:, h, DPAR:DPAR + 1], yc[:, h], ALU.mult, ALU.add).then_inc(s_n, 1)
                for h in range(NH):
                    dve.wait_ge(s_n, 1 + b * 6 + h + 5)
                    tt(gt[:, h], yc[:, h], sz[:, h], ALU.mult).then_inc(s_g, 1)
                dve.wait_ge(s_o, 1 + b + 1)
                dve.wait_ge(s_out, 1 + b * 16)
                tt(res[:].rearrange("p t c -> p (t c)"), bO[:], x1[:].rearrange("p t c -> p (t c)"), ALU.add).then_inc(s_res, 1)


def pack_ssm(d):
    def halves(v):
        return v.reshape(NH, P, -1).transpose(1, 0, 2)
    vec = np.concatenate([halves(d["L1_attn_" + n]) for n in ("conv_w", "conv_b", "b_dt", "D_param", "ln_w", "ln_b")], -1)
    wx = d["L1_attn_W_x"]
    wx = np.concatenate([wx[1:], wx[0:1]], 0).T.reshape(NH, P, 33).transpose(1, 0, 2)
    return {"w_in": d["L1_attn_W_in"].T, "w_x": wx, "w_dt": d["L1_attn_W_dt"].T, "vec": vec,
            "alog": np.tile(d["L1_attn_A_log"][None], (P, 1)), "w_out": d["L1_attn_W_out"].T.reshape(NH, P, C).transpose(1, 0, 2)}


H0, D0 = 16, C // 16
E, EM, EI, KC = 8, 4, 64, 4
PAIRS = EM * EI // P
G0 = H0 // HG
SC0 = float(1.0 / np.sqrt(np.float32(D0)))
VCH = 51


def build_layer0(nc, x_d, wqk, bqk, wv, bvr, wo, rows, wr, rbias, tri, wg, wu, wd, cw_d, sel_d, ident_d, x1_d, xn1_d):
    with ExitStack() as ctx:
        def sb(name, shape):
            return ctx.enter_context(nc.sbuf_tensor("a_" + name, shape, F32))

        sems = []

        def sem(name):
            sems.append(ctx.enter_context(nc.semaphore("a_" + name)))
            return sems[-1]

        Wqk, Bqk = sb("Wqk", [P, 2 * G0, P]), sb("Bqk", [P, 2 * G0])
        Wv, Bv, Wo = sb("Wv", [P, C]), sb("Bv", [P, C]), sb("Wo", [P, C])
        row2 = sb("row2", [2, C])
        Wr, Rb, Tri = sb("Wr", [P, E]), sb("Rb", [P, E]), sb("Tri", [P, E * E])
        Wg, Wu, Wd = sb("Wg", [P, EM * EI]), sb("Wu", [P, EM * EI]), sb("Wd", [P, PAIRS, C])
        cw = sb("cw", [P, KC])
        sel = sb("sel", [E, PAIRS, P])
        idn = sb("idn", [P, P])
        ones2 = sb("ones2", [2, P])
        diag = sb("diag", [P, KC, P])
        x = sb("x", [P, T4, C])
        xn = sb("xn", [P, T4, C])
        xnT = sb("xnT", [P, KC - 1 + L])
        pad = sb("pad", [P, 1])
        st6 = sb("st6", [P, T4, 6])
        mv = sb("mv", [P, T4, 2])
        va, rstd, vt = sb("va", [P, T4]), sb("rstd", [P, T4]), sb("vt", [P, T4])
        qk = sb("qk", [P, 2 * G0, L])
        V = sb("V", [P, T4, C])
        Pe = sb("Pe", [P, 2, H0, P])
        mx, nm, su = sb("mx", [P, 2, H0]), sb("nm", [P, 2, H0]), sb("su", [P, 2, H0])
        rc = sb("rc", [P, 2, H0])
        PT = sb("PT", [P, 2, HG, P])
        O = sb("O", [P, 2, C])
        OT = sb("OT", [P, L])
        ex, sg, sbi = sb("ex", [P, T4 * E]), sb("sg", [P, T4 * E]), sb("sbi", [P, T4 * E])
        c1, c2 = sb("c1", [P, T4 * E * E]), sb("c2", [P, T4 * E * E])
        rk, cwt = sb("rk", [P, T4 * E]), sb("cwt", [P, T4 * E])
        ws, aw = sb("ws", [P, T4]), sb("aw", [P, T4])
        cwT = sb("cwT", [E, L])
        gs = sb("gs", [P, PAIRS, L])
        hid = sb("hid", [P, PAIRS, L])
        idt = sb("idt", [P, T4, C])
        x1 = sb("x1", [P, T4, C])
        xn1T = sb("xn1T", [P, L])
        K4 = [ctx.enter_context(nc.psum_tensor(f"a_pK{i}", [P, 512], F32)) for i in range(4)]
        bT = [ctx.enter_context(nc.psum_tensor(f"a_pT{i}", [P, 512], F32)) for i in range(2)]
        bO = ctx.enter_context(nc.psum_tensor("a_pO", [P, 512], F32))
        bA = ctx.enter_context(nc.psum_tensor("a_pA", [P, 512], F32))

        s_c, s_ini, s_x, s_st = sem("c"), sem("ini"), sem("x"), sem("st")
        s_v = sem("chain")
        s_xn, s_xnp, s_xnT = sem("xn"), sem("xnp"), sem("xnT")
        s_qp, s_qk, s_vp, s_V = sem("qp"), sem("qk"), sem("vp"), sem("V")
        s_rp, s_ex = sem("rp"), sem("ex")
        s_cw, s_cwp, s_cwT, s_cb = sem("cw"), sem("cwp"), sem("cwT"), sem("cb")
        s_s, s_nm, s_exp = sem("s"), sem("nm"), sem("exp")
        s_pt, s_pte, s_pv, s_O, s_op, s_OT = sem("pt"), sem("pte"), sem("pv"), sem("O"), sem("op"), sem("OT")
        s_gu, s_gs, s_hid, s_acc, s_x1 = sem("gu"), sem("gs"), sem("hid"), sem("acc"), sem("x1")
        s_xn1, s_x1p, s_x1T = sem("xn1"), sem("x1p"), sem("x1T")
        block = ctx.enter_context(nc.Block())
        NG = T4 * G0

        @block.sync
        def _(sp):
            start_at_one(sp, sems)
            for dst, src in ((idn, ident_d), (Wqk, wqk), (Bqk, bqk), (Wv, wv), (Bv, bvr), (Wo, wo), (row2, rows),
                             (Wr, wr), (Rb, rbias), (Tri, tri), (Wg, wg), (Wu, wu), (Wd, wd), (cw, cw_d), (sel, sel_d)):
                sp.dma_start(dst[:], src).then_inc(s_c, 16)
            with sp.Fori(0, B) as b:
                sp.wait_ge(s_x1, 1 + b)
                sp.dma_start(x[:], x_d[bass.ds(b, 1)].rearrange("a (t p) c -> p (a t) c", p=P)).then_inc(s_x, 16)
                sp.wait_ge(s_x1, 1 + b + 1)
                sp.dma_start(x1_d[bass.ds(b, 1)].rearrange("a (t p) c -> p (a t) c", p=P), x1[:]).then_inc(s_st, 16)
                sp.wait_ge(s_x1T, 1 + b + 1)
                sp.dma_start(xn1_d[:, bass.ds(b * L, L)], xn1T[:]).then_inc(s_st, 16)
            sp.wait_ge(s_st, 1 + B * 32)

        CONSTS = 15 * 16

        @block.gpsimd
        def _(pool):
            nc.gpsimd.memset(xnT[:], 0.0).then_inc(s_ini, 1)
            nc.gpsimd.memset(ones2[:], 1.0).then_inc(s_ini, 1)

        @block.tensor
        def _(pe):
            mul, turn = nc.tensor.matmul, nc.tensor.transpose
            pe.wait_ge(s_c, 1 + CONSTS)
            pe.wait_ge(s_ini, 1 + 2 + KC)
            with pe.Fori(0, B) as b:
                pe.wait_ge(s_xn, 1 + b + 1)
                for t in range(T4):
                    w = turn(bT[0][:, t * P:(t + 1) * P], xn[:, t], idn[:])
                w.then_inc(s_xnp, 1)
                pe.wait_ge(s_xnT, 1 + b + 1)
                xm = xnT[:, KC - 1:KC - 1 + L]
                for g in range(2 * G0):
                    if g >= 4:
                        pe.wait_ge(s_qk, 1 + b * 2 * G0 + g - 3)
                    mul(K4[g % 4][:], Wqk[:, g], xm, start=True, stop=True).then_inc(s_qp, 1)
                for t in range(T4):
                    w = mul(bT[1][:, t * P:(t + 1) * P], xnT[:, KC - 1 + t * P:KC - 1 + (t + 1) * P], Wv[:], start=True, stop=True)
                w.then_inc(s_vp, 1)
                for t in range(T4):
                    w = mul(bO[:, t * E:(t + 1) * E], xnT[:, KC - 1 + t * P:KC - 1 + (t + 1) * P], Wr[:], start=True, stop=True)
                w.then_inc(s_rp, 1)
                pe.wait_ge(s_qk, 1 + (b + 1) * 2 * G0)
                pe.wait_ge(s_ex, 1 + b + 1)
                pe.wait_ge(s_V, 1 + b + 1)

                def scores(t):
                    if t:
                        pe.wait_ge(s_exp, 1 + (b * T4 + t) * H0)
                    for g in range(G0):
                        for h in range(HG):
                            r = slice(32 * h, 32 * h + 32)
                            w = mul(K4[h][:, g * P:(g + 1) * P], qk[r, g, t * P:(t + 1) * P],
                                    qk[r, G0 + g, t * P:(t + 1) * P], start=True, stop=True, tile_position=(32 * h, 0))
                    w.then_inc(s_s, 1)

                def turn_weights(t, g):
                    n = t * G0 + g
                    if g == 0:
                        pe.wait_ge(s_exp, 1 + (b * T4 + t + 1) * H0)
                    if n >= 2:
                        pe.wait_ge(s_pte, 1 + b * NG + n - 1)
                    for h in range(HG):
                        w = turn(bT[n % 2][:, h * P:(h + 1) * P], Pe[:, t % 2, h * G0 + g], idn[:])
                    w.then_inc(s_pt, 1)

                def mix(t, g):
                    n = t * G0 + g
                    pe.wait_ge(s_pte, 1 + b * NG + n + 1)
                    if g == 0 and t:
                        pe.wait_ge(s_O, 1 + b * T4 + t)
                    for h in range(HG):
                        hh = g * HG + h
                        w = mul(bO[:, hh * D0:(hh + 1) * D0], PT[:, n % 2, h], V[:, t, hh * D0:(hh + 1) * D0], start=True, stop=True)
                    w.then_inc(s_pv, 1)

                def turn_out(t):
                    pe.wait_ge(s_O, 1 + b * T4 + t + 1)
                    turn(bA[:, t * P:(t + 1) * P], O[:, t % 2], idn[:]).then_inc(s_op, 1)

                for t in range(T4 + 1):
                    if t < T4:
                        scores(t)
                    if t:
                        for g in range(G0):
                            turn_weights(t - 1, g)
                            if g:
                                mix(t - 1, g - 1)
                            elif t >= 2:
                                turn_out(t - 2)
                        mix(t - 1, G0 - 1)
                pe.wait_ge(s_cw, 1 + b + 1)
                for t in range(T4):
                    w = turn(bT[0][0:E, t * P:(t + 1) * P], cwt[:, t * E:(t + 1) * E], idn[:])
                w.then_inc(s_cwp, 1)
                for m in range(PAIRS):
                    mul(K4[2 * m][:], Wg[:, m * P:(m + 1) * P], xm, start=True, stop=True)
                    mul(K4[2 * m + 1][:], Wu[:, m * P:(m + 1) * P], xm, start=True, stop=True).then_inc(s_gu, 1)
                turn_out(T4 - 1)
                pe.wait_ge(s_cwT, 1 + b + 1)
                for m in range(PAIRS):
                    mul(bT[m][:], sel[:, m], cwT[:], start=True, stop=True).then_inc(s_cb, 1)
                pe.wait_ge(s_OT, 1 + b + 1)
                pe.wait_ge(s_hid, 1 + (b + 1) * PAIRS * 2)
                for t in range(T4):
                    o, q = bA[:, t * P:(t + 1) * P], slice(t * P, (t + 1) * P)
                    for k in range(KC):
                        mul(o, xnT[:, k + t * P:k + (t + 1) * P], diag[:, k], start=k == 0, stop=False)
                    mul(o, ones2[:], row2[:], start=False, stop=False)
                    mul(o, OT[:, q], Wo[:], start=False, stop=False)
                    for m in range(PAIRS):
                        w = mul(o, hid[:, m, q], Wd[:, m], start=False, stop=m == PAIRS - 1)
                w.then_inc(s_acc, 1)
                pe.wait_ge(s_xn1, 1 + b + 1)
                for t in range(T4):
                    w = turn(bO[:, t * P:(t + 1) * P], xn[:, t], idn[:])
                w.then_inc(s_x1p, 1)

        @block.scalar
        def _(act):
            f = nc.scalar.activation
            act.wait_ge(s_c, 1 + CONSTS)
            act.wait_ge(s_ini, 1 + 2)
            with act.Fori(0, B) as b:
                act.wait_ge(s_xnp, 1 + b + 1)
                f(xnT[:, KC - 1:KC - 1 + L], bT[0][:], ACT.Copy).then_inc(s_xnT, 1)
                for g in range(2 * G0):
                    act.wait_ge(s_qp, 1 + b * 2 * G0 + g + 1)
                    f(qk[:, g], K4[g % 4][:], ACT.Identity, bias=Bqk[:, g:g + 1]).then_inc(s_qk, 1)
                act.wait_ge(s_rp, 1 + b + 1)
                f(ex[:], bO[:, 0:T4 * E], ACT.Exp, scale=-1.0).then_inc(s_ex, 1)

                def exps(t):
                    act.wait_ge(s_nm, 1 + b * T4 + t + 1)
                    if t >= 2:
                        act.wait_ge(s_pt, 1 + b * NG + (t - 1) * G0)
                    for i in range(H0):
                        f(Pe[:, t % 2, i], K4[i // G0][:, (i % G0) * P:(i % G0 + 1) * P], ACT.Exp,
                          bias=nm[:, t % 2, i:i + 1], scale=SC0, accum_out=su[:, t % 2, i:i + 1]).then_inc(s_exp, 1)

                for t in range(T4):
                    exps(t)
                for m in range(PAIRS):
                    act.wait_ge(s_gu, 1 + b * PAIRS + m + 1)
                    f(gs[:, m], K4[2 * m][:], ACT.Silu).then_inc(s_gs, 1)
                act.wait_ge(s_op, 1 + (b + 1) * T4)
                f(OT[:], bA[:], ACT.Copy).then_inc(s_OT, 1)
                act.wait_ge(s_x1p, 1 + b + 1)
                act.wait_ge(s_st, 1 + b * 32)
                f(xn1T[:], bO[:], ACT.Copy).then_inc(s_x1T, 1)

        @block.vector
        def _(dve):
            tt, ts, stt = nc.vector.tensor_tensor, nc.vector.tensor_scalar, nc.vector.scalar_tensor_tensor
            red = nc.vector.tensor_reduce
            dve.wait_ge(s_c, 1 + CONSTS)
            dve.wait_ge(s_ini, 1 + 2)
            for k in range(KC):
                ts(diag[:, k], idn[:], cw[:, k:k + 1], None, ALU.mult).then_inc(s_ini, 1)
            with dve.Fori(0, B) as b:
                n = [0]

                def link(ins):
                    n[0] += 1
                    ins.then_inc(s_v, 1)
                    dve.wait_ge(s_v, 1 + b * VCH + n[0])

                def norm(src):
                    for t in range(T4):
                        ins = nc.vector.bn_stats(st6[:, t], src[:, t])
                    link(ins)
                    nc.vector.memset(pad[:], 0.0)
                    for t in range(T4):
                        ins = nc.vector.bn_aggr(mv[:, t], st6[:, t])
                    link(ins)
                    link(ts(va[:], mv[:, :, 1], 1e-5, None, ALU.add))
                    base = b * VCH + n[0]
                    rsqrt(nc, dve, s_v, base, va[:], rstd[:], vt[:])
                    n[0] += RSQRT_STEPS
                    for t in range(T4):
                        ins = ts(xn[:, t], src[:, t], mv[:, t, 0:1], rstd[:, t:t + 1], ALU.subtract, ALU.mult)
                    return ins

                dve.wait_ge(s_x, 1 + (b + 1) * 16)
                dve.wait_ge(s_x1p, 1 + b)
                norm(x).then_inc(s_xn, 1)
                dve.wait_ge(s_vp, 1 + b + 1)
                tt(V[:], bT[1][:].rearrange("p (t c) -> p t c", t=T4), Bv[:].unsqueeze(1).broadcast_to([P, T4, C]), ALU.add)\
                    .then_inc(s_V, 1)
                dve.wait_ge(s_ex, 1 + b + 1)
                ev = [P, T4, E]
                eev = [P, T4, E, E]
                te = lambda a: a.rearrange("p (t e) -> p t e", t=T4)
                tef = lambda a: a.rearrange("p (t e f) -> p t e f", t=T4, e=E)
                link(ts(ex[:], ex[:], 1.0, None, ALU.add))
                link(nc.vector.reciprocal(sg[:], ex[:]))
                link(tt(te(sbi[:]), te(sg[:]), Rb[:].unsqueeze(1).broadcast_to(ev), ALU.add))
                mine = te(sbi[:]).unsqueeze(3).broadcast_to(eev)
                other = te(sbi[:]).unsqueeze(2).broadcast_to(eev)
                tt(tef(c1[:]), other, mine, ALU.is_gt)
                link(tt(tef(c2[:]), other, mine, ALU.is_equal))
                link(tt(c2[:].rearrange("p (t e) -> p t e", t=T4), c2[:].rearrange("p (t e) -> p t e", t=T4),
                        Tri[:].unsqueeze(1).broadcast_to([P, T4, E * E]), ALU.mult))
                link(tt(c1[:], c1[:], c2[:], ALU.add))
                link(red(te(rk[:]), tef(c1[:]), AX, ALU.add))
                link(stt(cwt[:], rk[:], 1.5, sg[:], ALU.is_lt, ALU.mult))
                link(red(ws[:], te(cwt[:]), AX, ALU.add))
                link(ts(ws[:], ws[:], 1e-9, None, ALU.add))
                link(nc.vector.reciprocal(aw[:], ws[:]))
                ins = tt(te(cwt[:]), te(cwt[:]), aw[:].unsqueeze(2).broadcast_to(ev), ALU.mult)
                ins.then_inc(s_cw, 1)
                dve.wait_ge(s_cw, 1 + b + 1)
                link(tt(aw[:], te(cwt[:])[:, :, 4], te(cwt[:])[:, :, 6], ALU.add))
                for t in range(T4):
                    ins = ts(idt[:, t], xn[:, t], 0.0, cwt[:, t * E + 7:t * E + 8], ALU.max, ALU.mult)
                link(ins)
                for t in range(T4):
                    ins = stt(idt[:, t], xn[:, t], aw[:, t:t + 1], idt[:, t], ALU.mult, ALU.add)
                link(ins)
                link(tt(idt[:], idt[:], x[:], ALU.add))

                def maxima(t):
                    dve.wait_ge(s_s, 1 + b * T4 + t + 1)
                    for h in range(HG):
                        ins = red(mx[:, t % 2, h * G0:(h + 1) * G0], K4[h][:].rearrange("p (g j) -> p g j", g=G0), AX, ALU.max)
                    link(ins)
                    if t >= 2:
                        dve.wait_ge(s_exp, 1 + (b * T4 + t - 1) * H0)
                    ts(nm[:, t % 2], mx[:, t % 2], -SC0, None, ALU.mult).then_inc(s_nm, 1)

                def evacuate(t, g):
                    m = t * G0 + g
                    dve.wait_ge(s_pt, 1 + b * NG + m + 1)
                    if m >= 2:
                        dve.wait_ge(s_pv, 1 + b * NG + m - 1)
                    nc.vector.tensor_copy(PT[:, m % 2].rearrange("p h j -> p (h j)"), bT[m % 2][:]).then_inc(s_pte, 1)

                def normalise(t):
                    dve.wait_ge(s_exp, 1 + (b * T4 + t + 1) * H0)
                    link(nc.vector.reciprocal(rc[:, t % 2], su[:, t % 2]))
                    dve.wait_ge(s_pv, 1 + b * NG + (t + 1) * G0)
                    if t >= 2:
                        dve.wait_ge(s_op, 1 + b * T4 + t - 1)
                    tt(O[:, t % 2].rearrange("p (g h d) -> p g h d", g=G0, h=HG),
                       bO[:, 0:C].rearrange("p (g h d) -> p g h d", g=G0, h=HG),
                       rc[:, t % 2].rearrange("p (h g) -> p g h", h=HG).unsqueeze(3).broadcast_to([P, G0, HG, D0]),
                       ALU.mult).then_inc(s_O, 1)

                for t in range(T4 + 1):
                    if t < T4:
                        maxima(t)
                    if t:
                        for g in range(G0):
                            evacuate(t - 1, g)
                        normalise(t - 1)
                dve.wait_ge(s_cwp, 1 + b + 1)
                nc.vector.tensor_copy(cwT[:], bT[0][0:E, :]).then_inc(s_cwT, 1)
                for m in range(PAIRS):
                    dve.wait_ge(s_gs, 1 + b * PAIRS + m + 1)
                    tt(hid[:, m], K4[2 * m + 1][:], gs[:, m], ALU.mult).then_inc(s_hid, 1)
                for m in range(PAIRS):
                    dve.wait_ge(s_cb, 1 + b * PAIRS + m + 1)
                    dve.wait_ge(s_hid, 1 + b * 2 * PAIRS + m + 1)
                    tt(hid[:, m], hid[:, m], bT[m][:], ALU.mult).then_inc(s_hid, 1)
                dve.wait_ge(s_acc, 1 + b + 1)
                dve.wait_ge(s_st, 1 + b * 32)
                tt(x1[:].rearrange("p t c -> p (t c)"), bA[:], idt[:].rearrange("p t c -> p (t c)"), ALU.add).then_inc(s_x1, 1)
                dve.wait_ge(s_x1, 1 + b + 1)
                norm(x1).then_inc(s_xn1, 1)
                assert n[0] == VCH


def pack_layer0(d):
    def heads(w):
        out = np.zeros((w.shape[0], G0, HG, 32), np.float32)
        out[..., 0:D0] = w.reshape(w.shape[0], G0, HG, D0)
        return out.reshape(w.shape[0], G0, P)
    g = lambda n: d["L0_" + n]
    bqk = np.concatenate([heads(g("attn_bq")[None]), heads(g("attn_bk")[None])], 1)
    sel = np.zeros((E, PAIRS, P), np.float32)
    for e in range(EM):
        sel[e, e // 2, (e % 2) * EI:(e % 2 + 1) * EI] = 1.0
    return {"w0_wqk": np.concatenate([heads(g("attn_Wq")), heads(g("attn_Wk"))], 1), "w0_bqk": bqk[0].T,
            "w0_wv": g("attn_Wv"), "w0_bv": np.tile(g("attn_bv"), (P, 1)), "w0_wo": g("attn_Wo"),
            "w0_rows": np.stack([g("attn_bo"), g("ffn_conv_b")]), "w0_wr": g("ffn_Wr"),
            "w0_rb": np.tile(g("ffn_router_bias"), (P, 1)),
            "w0_tri": np.tile(np.tril(np.ones((E, E), np.float32), -1).reshape(1, -1), (P, 1)),
            "w0_wg": g("ffn_Wg").transpose(1, 0, 2).reshape(C, -1), "w0_wu": g("ffn_Wu").transpose(1, 0, 2).reshape(C, -1),
            "w0_wd": g("ffn_Wd").reshape(PAIRS, P, C).transpose(1, 0, 2), "w0_cw": g("ffn_conv_w")[:, 0].T, "w0_sel": sel}


def constants():
    return {"ident": np.eye(P, dtype=np.float32), "tabs": rotary_constants(), "masks": band_masks()}


def build(nc, a, out):
    x1_d = nc.dram_tensor("x1_d", [B, L, C], F32, kind="Internal").ap()
    xn1_d = nc.dram_tensor("xn1_d", [C, B * L], F32, kind="Internal").ap()
    ffn_d = nc.dram_tensor("ffn_d", [C, B * L], F32, kind="Internal").ap()
    xi_d = nc.dram_tensor("xi_d", [B, P, NH * L], F32, kind="Internal").ap()
    sz_d = nc.dram_tensor("sz_d", [B, P, NH * L], F32, kind="Internal").ap()
    build_layer0(nc, a["x"], *(a["w0_" + n] for n in ("wqk", "bqk", "wv", "bv", "wo", "rows", "wr", "rb", "tri", "wg",
                                                      "wu", "wd", "cw", "sel")), a["ident"], x1_d, xn1_d)
    build_local(nc, xn1_d, ffn_d, *(a[n] for n in ("tabs", "masks", "f_wqk", "f_wv", "f_wo", "f_w1", "f_w2", "f_scales",
                                                   "f_small")), a["ident"])
    with nc.sbuf_tensor("ssm_dt", [P, HB, L], F32) as dt, nc.sbuf_tensor("ssm_u", [P, HB, L], F32) as u:
        with nc.sbuf_tensor("ssm_bc", [P, L, B], F32) as bc:
            build_ssm_inputs(nc, xn1_d, a["w_in"], a["w_x"], a["w_dt"], a["vec"], dt, u, bc, xi_d, sz_d)
            build_ssm_scan(nc, a["alog"], a["ident"], dt, u, bc)
        build_ssm_output(nc, u, xi_d, sz_d, a["vec"], a["w_out"], a["ident"], x1_d, ffn_d, out)


def pack(d):
    wqk, wv, scales, small = pack_local(d)
    return {"x": d["L0_attn_x"], **constants(), **pack_layer0(d), **pack_ssm(d), "f_wqk": wqk, "f_wv": wv,
            "f_scales": scales, "f_small": small, "f_wo": d["L1_ffn_Wo"], "f_w1": d["L1_ffn_W1"], "f_w2": d["L1_ffn_W2"]}


def kernel(**inputs):
    import concourse.bacc as bacc
    from concourse.bass_utils import run_bass_kernel_spmd

    arrays = {n: np.ascontiguousarray(v) for n, v in pack({n: np.asarray(v) for n, v in inputs.items()}).items()}
    nc = bacc.Bacc("TRN2", target_bir_lowering=False, num_devices=1)
    a = {n: nc.dram_tensor(n, v.shape, F32, kind="ExternalInput").ap() for n, v in arrays.items()}
    out = nc.dram_tensor("out", [B, L, C], F32, kind="ExternalOutput").ap()
    build(nc, a, out)
    return run_bass_kernel_spmd(nc, [arrays], core_ids=[0]).results[0]["out"]
```
